# Optimizing a Trainium2 kernel written in Bass

```python
import numpy as np
import jax
import jax.numpy as jnp

def _softmax(x, axis=-1):
    return jax.nn.softmax(x, axis=axis)

def _gelu(x):
    return jax.nn.gelu(x, approximate=True)

def _silu(x):
    return jax.nn.silu(x)

def _sigmoid(x):
    return jax.nn.sigmoid(x)

def _layernorm(x, axis=-1, eps=1e-05):
    m = jnp.mean(x, axis=axis, keepdims=True)
    v = jnp.var(x, axis=axis, keepdims=True)
    return (x - m) / jnp.sqrt(v + eps)

def _scatter_add(tgt, idx, src, axis=0):
    return tgt.at[idx].add(src)

def _segment_sum(src, seg, n):
    return jax.ops.segment_sum(src, seg, n)
kernel_name = 'mk_gnn_resnorm_d4_gnn_r32_7d839b'

def setup_inputs(seed: int=0):
    np.random.seed(seed)
    _w = jnp.asarray

    def _rec_inputs():
        import jax
        import jax.numpy as jnp
        _gk = jax.random.key(seed)
        x = -0.0003713 + 1 * jax.random.normal(jax.random.fold_in(_gk, 1), (3125, 128), jnp.float32)
        _s = jax.random.randint(jax.random.fold_in(_gk, 2), (25000,), 0, 3125, jnp.int32)
        _d = jax.random.randint(jax.random.fold_in(_gk, 3), (25000,), 0, 3125, jnp.int32)
        _loop = jnp.arange(3125, dtype=jnp.int32)
        src = jnp.concatenate([_s, _d, _loop])
        dst = jnp.concatenate([_d, _s, _loop])
        _o = jnp.argsort(dst, stable=True)
        src = src[_o]
        dst = dst[_o]
        edge_type_3 = jax.random.randint(jax.random.fold_in(_gk, 13), (53125,), 0, 3, jnp.int32)
        return (x, src, dst, edge_type_3)
    x, src, dst, edge_type_3 = _rec_inputs()

    def _L0_gnn_setup():
        import jax, jax.numpy as jnp
        import numpy as np
        N = 3125
        E = 50000
        IN, H, OUT = (128, 256, 128)

        def _sage_conv(x, src, dst, W_l, b_l, W_r):
            ones = jnp.ones(src.shape[0], x.dtype)
            deg = jax.ops.segment_sum(ones, dst, num_segments=N)
            summed = jax.ops.segment_sum(x[src], dst, num_segments=N)
            agg = summed / jnp.maximum(deg, 1.0)[:, None]
            return agg @ W_l + b_l + x @ W_r

        def _layer_norm(x, g, b, eps=1e-05):
            m = jnp.mean(x, axis=-1, keepdims=True)
            v = jnp.mean(jnp.square(x - m), axis=-1, keepdims=True)
            return (x - m) / jnp.sqrt(v + eps) * g + b
        key = jax.random.key(seed)
        ks = jax.random.split(key, 16)

        def w(k, shape):
            fan_in = shape[0]
            return jax.random.normal(k, shape, jnp.float32) * (1.0 / np.sqrt(fan_in))
        return {'x': jax.random.normal(ks[0], (N, IN), jnp.float32), 'edge_src': jax.random.randint(ks[1], (E,), 0, N, dtype=jnp.int32), 'edge_dst': jax.random.randint(ks[2], (E,), 0, N, dtype=jnp.int32), 'W_l0': w(ks[3], (IN, H)), 'b_l0': jnp.zeros((H,), jnp.float32), 'W_r0': w(ks[4], (IN, H)), 'g0': jnp.ones((H,), jnp.float32), 'be0': jnp.zeros((H,), jnp.float32), 'W_l1': w(ks[5], (H, H)), 'b_l1': jnp.zeros((H,), jnp.float32), 'W_r1': w(ks[6], (H, H)), 'g1': jnp.ones((H,), jnp.float32), 'be1': jnp.zeros((H,), jnp.float32), 'W_l2': w(ks[7], (H, OUT)), 'b_l2': jnp.zeros((OUT,), jnp.float32), 'W_r2': w(ks[8], (H, OUT))}
    _L0_gnn_all = _L0_gnn_setup()
    _L0_gnn_in = {k: v for k, v in _L0_gnn_all.items() if k in ('W_l0', 'b_l0', 'W_r0', 'g0', 'be0', 'W_l1', 'b_l1', 'W_r1', 'g1', 'be1', 'W_l2', 'b_l2', 'W_r2')}
    del _L0_gnn_all

    def _L1_gnn_setup():
        import jax, jax.numpy as jnp
        import numpy as np
        N_NODES = 50000
        N_EDGES = 50000
        IN_DIM = 128
        HEADS = 4
        HEAD_DIM = 32
        N_REL = 3
        NEG_SLOPE = 0.2
        key = jax.random.key(seed)
        ks = jax.random.split(key, 8)
        x = jax.random.normal(ks[0], (N_NODES, IN_DIM), dtype=jnp.float32)
        edge_index = jax.random.randint(ks[1], (2, N_EDGES), 0, N_NODES, dtype=jnp.int64)
        edge_type = jax.random.randint(ks[2], (N_EDGES,), 0, N_REL, dtype=jnp.int64)
        s = 1.0 / np.sqrt(IN_DIM)
        W = jax.random.normal(ks[3], (N_REL, IN_DIM, HEADS * HEAD_DIM), dtype=jnp.float32) * s
        att_src = jax.random.normal(ks[4], (N_REL, HEADS, HEAD_DIM), dtype=jnp.float32) * s
        att_dst = jax.random.normal(ks[5], (N_REL, HEADS, HEAD_DIM), dtype=jnp.float32) * s
        bias = jnp.zeros((N_REL, HEADS * HEAD_DIM), dtype=jnp.float32)
        rel_w = jnp.ones((N_REL,), dtype=jnp.float32)
        return {'x': x, 'W': W, 'att_src': att_src, 'att_dst': att_dst, 'bias': bias, 'rel_w': rel_w, 'edge_index': edge_index, 'edge_type': edge_type}
    _L1_gnn_all = _L1_gnn_setup()
    _L1_gnn_in = {k: v for k, v in _L1_gnn_all.items() if k in ('W', 'att_src', 'att_dst', 'bias', 'rel_w')}
    del _L1_gnn_all

    def _L2_gnn_setup():
        import jax, jax.numpy as jnp
        import numpy as np
        N = 50000
        E = 25000
        H = 128
        key = jax.random.key(seed)
        k1, k2, k3, k4, k5 = jax.random.split(key, 5)
        s = 1.0 / np.sqrt(H).astype(np.float32)
        x = jax.random.normal(k1, (N, H), dtype=jnp.float32)
        edge_index = jax.random.randint(k2, (2, E), 0, N, dtype=jnp.int64)
        a_i = jax.random.normal(k3, (H,), dtype=jnp.float32) * s
        a_j = jax.random.normal(k4, (H,), dtype=jnp.float32) * s
        W = jax.random.normal(k5, (H, H), dtype=jnp.float32) * s
        return {'x': x, 'edge_index': edge_index, 'a_i': a_i, 'a_j': a_j, 'W': W}
    _L2_gnn_all = _L2_gnn_setup()
    _L2_gnn_in = {k: v for k, v in _L2_gnn_all.items() if k in ('a_i', 'a_j', 'W')}
    del _L2_gnn_all

    def _L3_gnn_setup():
        import jax, jax.numpy as jnp
        import numpy as np
        N_NODES = 50000
        N_EDGES = 25000
        D_MODEL = 128
        N_HEADS = 4
        N_LAYERS = 2
        F_HEAD = D_MODEL // N_HEADS

        def _gat_layer(x, src, dst, W_l, a_src_l, a_dst_l, b_l, apply_act):
            N = x.shape[0]
            H, F = a_src_l.shape
            h = (x @ W_l).reshape(N, H, F)
            alpha_s = jnp.einsum('nhf,hf->nh', h, a_src_l)
            alpha_d = jnp.einsum('nhf,hf->nh', h, a_dst_l)
            e = jax.nn.leaky_relu(alpha_s[src] + alpha_d[dst], negative_slope=0.2)
            e_max = jax.ops.segment_max(e, dst, num_segments=N)
            e_exp = jnp.exp(e - e_max[dst])
            denom = jax.ops.segment_sum(e_exp, dst, num_segments=N)
            alpha = e_exp / (denom[dst] + 1e-16)
            msg = h[src] * alpha[:, :, None]
            out = jax.ops.segment_sum(msg, dst, num_segments=N).reshape(N, H * F)
            out = out + x + b_l
            return jax.nn.elu(out) if apply_act else out
        key = jax.random.key(seed)
        ks = jax.random.split(key, 6)
        x = jax.random.normal(ks[0], (N_NODES, D_MODEL), dtype=jnp.float32)
        edge_index = jax.random.randint(ks[1], (2, N_EDGES), 0, N_NODES, dtype=jnp.int64)
        scale = 1.0 / np.sqrt(D_MODEL)
        W = jax.random.normal(ks[2], (N_LAYERS, D_MODEL, D_MODEL), dtype=jnp.float32) * scale
        a_src = jax.random.normal(ks[3], (N_LAYERS, N_HEADS, F_HEAD), dtype=jnp.float32) * scale
        a_dst = jax.random.normal(ks[4], (N_LAYERS, N_HEADS, F_HEAD), dtype=jnp.float32) * scale
        b = jnp.zeros((N_LAYERS, D_MODEL), dtype=jnp.float32)
        return {'x': x, 'edge_index': edge_index, 'W': W, 'a_src': a_src, 'a_dst': a_dst, 'b': b}
    _L3_gnn_all = _L3_gnn_setup()
    _L3_gnn_in = {k: v for k, v in _L3_gnn_all.items() if k in ('W', 'a_src', 'a_dst', 'b')}
    del _L3_gnn_all
    return {'x': x, 'src': src, 'dst': dst, 'edge_type_3': edge_type_3, 'L0_gnn_W_l0': _L0_gnn_in['W_l0'], 'L0_gnn_b_l0': _L0_gnn_in['b_l0'], 'L0_gnn_W_r0': _L0_gnn_in['W_r0'], 'L0_gnn_g0': _L0_gnn_in['g0'], 'L0_gnn_be0': _L0_gnn_in['be0'], 'L0_gnn_W_l1': _L0_gnn_in['W_l1'], 'L0_gnn_b_l1': _L0_gnn_in['b_l1'], 'L0_gnn_W_r1': _L0_gnn_in['W_r1'], 'L0_gnn_g1': _L0_gnn_in['g1'], 'L0_gnn_be1': _L0_gnn_in['be1'], 'L0_gnn_W_l2': _L0_gnn_in['W_l2'], 'L0_gnn_b_l2': _L0_gnn_in['b_l2'], 'L0_gnn_W_r2': _L0_gnn_in['W_r2'], 'L1_gnn_W': _L1_gnn_in['W'], 'L1_gnn_att_src': _L1_gnn_in['att_src'], 'L1_gnn_att_dst': _L1_gnn_in['att_dst'], 'L1_gnn_bias': _L1_gnn_in['bias'], 'L1_gnn_rel_w': _L1_gnn_in['rel_w'], 'L2_gnn_a_i': _L2_gnn_in['a_i'], 'L2_gnn_a_j': _L2_gnn_in['a_j'], 'L2_gnn_W': _L2_gnn_in['W'], 'L3_gnn_W': _L3_gnn_in['W'], 'L3_gnn_a_src': _L3_gnn_in['a_src'], 'L3_gnn_a_dst': _L3_gnn_in['a_dst'], 'L3_gnn_b': _L3_gnn_in['b']}

def reference(x, src, dst, edge_type_3, L0_gnn_W_l0, L0_gnn_b_l0, L0_gnn_W_r0, L0_gnn_g0, L0_gnn_be0, L0_gnn_W_l1, L0_gnn_b_l1, L0_gnn_W_r1, L0_gnn_g1, L0_gnn_be1, L0_gnn_W_l2, L0_gnn_b_l2, L0_gnn_W_r2, L1_gnn_W, L1_gnn_att_src, L1_gnn_att_dst, L1_gnn_bias, L1_gnn_rel_w, L2_gnn_a_i, L2_gnn_a_j, L2_gnn_W, L3_gnn_W, L3_gnn_a_src, L3_gnn_a_dst, L3_gnn_b):
    import jax
    import jax.numpy as jnp

    def _L0_gnn_ref(x, edge_src, edge_dst, W_l0, b_l0, W_r0, g0, be0, W_l1, b_l1, W_r1, g1, be1, W_l2, b_l2, W_r2):
        import jax, jax.numpy as jnp
        import numpy as np
        N = 3125
        E = 50000
        IN, H, OUT = (128, 256, 128)

        def _sage_conv(x, src, dst, W_l, b_l, W_r):
            ones = jnp.ones(src.shape[0], x.dtype)
            deg = jax.ops.segment_sum(ones, dst, num_segments=N)
            summed = jax.ops.segment_sum(x[src], dst, num_segments=N)
            agg = summed / jnp.maximum(deg, 1.0)[:, None]
            return agg @ W_l + b_l + x @ W_r

        def _layer_norm(x, g, b, eps=1e-05):
            m = jnp.mean(x, axis=-1, keepdims=True)
            v = jnp.mean(jnp.square(x - m), axis=-1, keepdims=True)
            return (x - m) / jnp.sqrt(v + eps) * g + b
        h = _sage_conv(x, edge_src, edge_dst, W_l0, b_l0, W_r0)
        h = jax.nn.relu(_layer_norm(h, g0, be0))
        h = _sage_conv(h, edge_src, edge_dst, W_l1, b_l1, W_r1)
        h = jax.nn.relu(_layer_norm(h, g1, be1))
        return _sage_conv(h, edge_src, edge_dst, W_l2, b_l2, W_r2)

    def _L1_gnn_ref(x, W, att_src, att_dst, bias, rel_w, edge_index, edge_type):
        import jax, jax.numpy as jnp
        import numpy as np
        N_NODES = 50000
        N_EDGES = 50000
        IN_DIM = 128
        HEADS = 4
        HEAD_DIM = 32
        N_REL = 3
        NEG_SLOPE = 0.2
        N = x.shape[0]
        NEG = jnp.float32(-1000000000.0)
        self_idx = jnp.arange(N, dtype=edge_index.dtype)
        src = jnp.concatenate([edge_index[0], self_idx])
        dst = jnp.concatenate([edge_index[1], self_idx])
        weights = jax.nn.softmax(rel_w)
        out = jnp.zeros((N, HEADS * HEAD_DIM), dtype=x.dtype)
        for r in range(N_REL):
            h = (x @ W[r]).reshape(N, HEADS, HEAD_DIM)
            a_s = jnp.einsum('nhc,hc->nh', h, att_src[r])
            a_d = jnp.einsum('nhc,hc->nh', h, att_dst[r])
            score = jax.nn.leaky_relu(a_s[src] + a_d[dst], NEG_SLOPE)
            mask = jnp.concatenate([edge_type == r, jnp.ones((N,), dtype=bool)])
            score = jnp.where(mask[:, None], score, NEG)
            smax = jax.ops.segment_max(score, dst, num_segments=N)
            ex = jnp.exp(score - smax[dst])
            denom = jax.ops.segment_sum(ex, dst, num_segments=N)
            alpha = ex / denom[dst]
            msg = alpha[:, :, None] * h[src]
            rel_out = jax.ops.segment_sum(msg, dst, num_segments=N).reshape(N, HEADS * HEAD_DIM)
            out = out + weights[r] * (rel_out + bias[r])
        return out

    def _L2_gnn_ref(x, edge_index, a_i, a_j, W):
        import jax, jax.numpy as jnp
        import numpy as np
        N = 50000
        E = 25000
        H = 128
        n = x.shape[0]
        idx_j = edge_index[0]
        idx_i = edge_index[1]
        si = x @ a_i
        sj = x @ a_j
        e = jax.nn.leaky_relu(si[idx_i] + sj[idx_j], negative_slope=0.01)
        seg_max = jax.ops.segment_max(e, idx_i, num_segments=n)
        e_exp = jnp.exp(e - seg_max[idx_i])
        denom = jax.ops.segment_sum(e_exp, idx_i, num_segments=n)
        alpha = e_exp / denom[idx_i]
        m = x + x @ W
        out = jax.ops.segment_sum(alpha[:, None] * m[idx_i], idx_j, num_segments=n)
        return jax.nn.gelu(out, approximate=False)

    def _L3_gnn_ref(x, edge_index, W, a_src, a_dst, b):
        import jax, jax.numpy as jnp
        import numpy as np
        N_NODES = 50000
        N_EDGES = 25000
        D_MODEL = 128
        N_HEADS = 4
        N_LAYERS = 2
        F_HEAD = D_MODEL // N_HEADS

        def _gat_layer(x, src, dst, W_l, a_src_l, a_dst_l, b_l, apply_act):
            N = x.shape[0]
            H, F = a_src_l.shape
            h = (x @ W_l).reshape(N, H, F)
            alpha_s = jnp.einsum('nhf,hf->nh', h, a_src_l)
            alpha_d = jnp.einsum('nhf,hf->nh', h, a_dst_l)
            e = jax.nn.leaky_relu(alpha_s[src] + alpha_d[dst], negative_slope=0.2)
            e_max = jax.ops.segment_max(e, dst, num_segments=N)
            e_exp = jnp.exp(e - e_max[dst])
            denom = jax.ops.segment_sum(e_exp, dst, num_segments=N)
            alpha = e_exp / (denom[dst] + 1e-16)
            msg = h[src] * alpha[:, :, None]
            out = jax.ops.segment_sum(msg, dst, num_segments=N).reshape(N, H * F)
            out = out + x + b_l
            return jax.nn.elu(out) if apply_act else out
        src, dst = (edge_index[0], edge_index[1])
        L = W.shape[0]
        for l in range(L):
            x = _gat_layer(x, src, dst, W[l], a_src[l], a_dst[l], b[l], apply_act=l < L - 1)
        return x
    edge_index = jnp.stack([src, dst])
    x = _layernorm(x + _L0_gnn_ref(x, src, dst, L0_gnn_W_l0, L0_gnn_b_l0, L0_gnn_W_r0, L0_gnn_g0, L0_gnn_be0, L0_gnn_W_l1, L0_gnn_b_l1, L0_gnn_W_r1, L0_gnn_g1, L0_gnn_be1, L0_gnn_W_l2, L0_gnn_b_l2, L0_gnn_W_r2), axis=-1)
    x = _layernorm(x + _L1_gnn_ref(x, L1_gnn_W, L1_gnn_att_src, L1_gnn_att_dst, L1_gnn_bias, L1_gnn_rel_w, edge_index, edge_type_3), axis=-1)
    x = _layernorm(x + _L2_gnn_ref(x, edge_index, L2_gnn_a_i, L2_gnn_a_j, L2_gnn_W), axis=-1)
    x = _layernorm(x + _L3_gnn_ref(x, edge_index, L3_gnn_W, L3_gnn_a_src, L3_gnn_a_dst, L3_gnn_b), axis=-1)
    return x

_drawn_inputs = setup_inputs


def setup_inputs(seed=0):
    import zlib

    import numpy as np

    out = dict(_drawn_inputs(seed))
    spreads = {'L0_gnn_b_l0': (0.0, 0.1),
     'L0_gnn_g0': (1.0, 0.2),
     'L0_gnn_be0': (0.0, 0.1),
     'L0_gnn_b_l1': (0.0, 0.1),
     'L0_gnn_g1': (1.0, 0.2),
     'L0_gnn_be1': (0.0, 0.1),
     'L0_gnn_b_l2': (0.0, 0.1),
     'L1_gnn_bias': (0.0, 0.1),
     'L1_gnn_rel_w': (1.0, 0.2),
     'L3_gnn_b': (0.0, 0.1)}
    factors = {'L1_gnn_att_dst': 10.053, 'L3_gnn_a_src': 3.331, 'L3_gnn_a_dst': 7.337}
    for name, (base, spread) in spreads.items():
        noise = np.random.default_rng([zlib.crc32(name.encode()), seed]).standard_normal(out[name].shape)
        drawn = base * np.exp(spread * noise) if base else spread * noise
        out[name] = jnp.asarray(drawn.astype(out[name].dtype))
    for name, factor in factors.items():
        out[name] = (out[name] * factor).astype(out[name].dtype)
    return out
```

```python
import concourse.bass as bass
from concourse import mybir
from contextlib import ExitStack

P = 128
N = 3125
E = 53125
F = 128
HID = 256
HEADS, HD = 4, 32
NREL = 3
T = (N + P - 1) // P
NP = T * P
TAIL = N - (T - 1) * P
SB = 8
IB = -(-E // (P * 2 * SB)) * 2 * SB
ROWS_FULL, ROW_TAIL = divmod(E, IB)
RING = 16
GB = 4
NG = RING // GB
NB = -(-(-(-E // P) + T) // RING) * RING
NSLOT = NB * P
TURNS = NB // RING
SP_ = NB // 4
SL = 4 * P
PADKEY = 4095
FAR = 1e6
BIG = 1e30
DT = 5
EPS = 1e-5


def build(nc, A, out):
    f32, bf16, i32 = mybir.dt.float32, mybir.dt.bfloat16, mybir.dt.int32
    ALU, ACT, AX = mybir.AluOpType, mybir.ActivationFunctionType, mybir.AxisListType.X
    ds = bass.ds
    ctx = ExitStack()
    with ctx:
        def sb(name, shape, dt=f32):
            return ctx.enter_context(nc.sbuf_tensor(name, shape, dt))

        def dram(name, shape, dt=f32):
            return nc.dram_tensor(name, shape, dt, kind="Internal").ap()

        lists = {"D": dram("edges_by_dst", (NSLOT + 2, 4), i32), "S": dram("edges_by_src", (NSLOT + 2, 4), i32)}
        x_table = dram("x_table", (NP, F))
        hidden1_table = dram("hidden1_table", (NP, HID))
        proj2_table = dram("proj2_table", (NP, F))
        rel_h_table = dram("rel_h_table", (NREL * NP, F))
        rel_src_table = dram("rel_src_table", (NREL * NP, HEADS))
        rel_dst_table = dram("rel_dst_table", (NREL * NP, 2 * HEADS))
        src_table = [dram(f"src_table{i}", (NP, HEADS)) for i in range(3)]
        dst_table = [dram(f"dst_table{i}", (NP, 2 * HEADS)) for i in range(3)]
        row_table = [dram(f"row_table{i}", (NP, F)) for i in range(3)]

        iota_free = sb("iota_free", [P, P])
        iota_hi = sb("iota_hi", [P, T])
        iota_blk = sb("iota_blk", [1, NB])
        ident = sb("ident", [P, P])
        identb = sb("identb", [P, P], bf16)
        ones = sb("ones", [P, P])
        ones_row = sb("ones_row", [P, IB + 1])
        lower = sb("lower", [P, P])
        X = sb("X", [P, T, F])
        bigf = sb("bigf", [P, (IB + 1) * T])
        hidf = sb("hidf", [P, T * HID])
        ringf = sb("ringf", [P, RING * HID])
        onehot = sb("onehot", [P, GB, P])
        rhs = sb("rhs", [P, GB, 396])
        idx_stage = sb("idx_stage", [P, RING], i32)
        weights = sb("weights", [P, 4 * HID])
        biases = sb("biases", [P, 6 * HID])
        dxt = sb("dxt", [P, 4 * DT * P])
        sm = sb("sm", [P, 640])
        deg = sb("deg", [P, T])
        node_a = sb("node_a", [P, T, 36])
        idx = {k: sb("idx_" + k, [P, NB], i32) for k in ("Dsrc", "Ddst", "DsrcT", "DdstT", "Ssrc", "Sdst")}
        lo = {"D": sb("lo_D", [P, NB]), "S": sb("lo_S", [P, NB])}
        typ = sb("typ", [P, NB])
        tid = {"D": sb("tid_D", [1, NB], i32), "S": sb("tid_S", [1, NB], i32)}
        cont = sb("cont", [SP_, SL])
        isend = sb("isend", [SP_, SL])
        typ_s = sb("typ_s", [SP_, SL])
        ebuf = sb("ebuf", [P, NB, 12])
        em = sb("em", [P, NB, 12])
        posidx = sb("posidx", [P, 2, SB], i32)
        recst = sb("recst", [P, 2, SB, 4], i32)
        ps = ctx.enter_context(nc.psum_tensor("ps", [P, 8, 512], f32))
        psf = ps[:, :, :].rearrange("p a b -> p (a b)")

        hist = bigf[:, :].rearrange("p (b h) -> p b h", h=T)
        hid = hidf[:, :].rearrange("p (t f) -> p t f", t=T)
        H1 = hidf[:, 0:T * F].rearrange("p (t f) -> p t f", t=T)
        XR = hidf[:, T * F:2 * T * F].rearrange("p (t f) -> p t f", t=T)
        ring = ringf[:, :].rearrange("p (r f) -> p r f", r=RING)
        ebuf_i = ebuf[:, :, :].rearrange("p a b -> p (a b)").bitcast(i32)
        edge_raw = ebuf_i[:, 0:3 * IB].rearrange("p (k b) -> p k b", k=3)
        rec_all = ebuf_i[:, 3 * IB:7 * IB].rearrange("p (b k) -> p b k", k=4)
        key_lo = {"D": hidf[:, 0:IB], "S": hidf[:, IB:2 * IB]}
        key_hi = {"D": hidf[:, 2 * IB:3 * IB], "S": hidf[:, 3 * IB:4 * IB]}
        key_far = {"D": hidf[:, 4 * IB:5 * IB], "S": hidf[:, 5 * IB:6 * IB]}
        key_tmp = hidf[:, 6 * IB:7 * IB].bitcast(i32)
        pad_rec = {"D": ringf[:, 0:4 * SL].bitcast(i32), "S": ringf[:, 4 * SL:8 * SL].bitcast(i32)} if RING * HID >= 8 * SL else None
        dxt3 = dxt[:, :].rearrange("p (s f) -> p s f", f=P)

        def big_view(n):
            return bigf[:, 0:T * n].rearrange("p (t f) -> p t f", t=T)

        def w_view(k, n):
            return weights[:, 0:k * n].rearrange("p (k n) -> p k n", k=k)

        def tiles(table):
            return table.rearrange("(t p) f -> p t f", p=P)

        def bc(ap, shape, at):
            return ap.unsqueeze(at).to_broadcast(shape)

        sem_sets = [[ctx.enter_context(nc.semaphore(f"stage{z}_{i}")) for i in range(16)] for z in range(2)]
        used_sems = []
        gathered = [ctx.enter_context(nc.semaphore(f"gathered{j}")) for j in range(NG)]
        scattered = [ctx.enter_context(nc.semaphore(f"scattered{z}")) for z in range(2)]
        before = {"gathered": 0, "scattered": 0}

        def stage(*names):
            k = len(used_sems)
            if k:
                for s in sem_sets[(k - 1) % 2][0:used_sems[-1]]:
                    nc.gpsimd.sem_clear(s)
            used_sems.append(len(names))
            st = ExitStack()
            block = st.enter_context(nc.Block())
            return st, block, sem_sets[k % 2][0:len(names)]

        def hold(eng, s, value, tick):
            eng.wait_ge(s, value)
            eng.sem_inc(tick, 1)

        def constants():
            st, block, (built, cleared, loaded, filled) = stage("built", "cleared", "loaded", "filled")
            with st:
                @block.gpsimd
                def _(pool):
                    pool.memset(ident[:, :], 0.0)
                    pool.memset(ones[:, :], 1.0)
                    pool.memset(ones_row[:, :], 1.0)
                    pool.memset(lower[:, :], 1.0)
                    pool.iota(iota_free[:, :], [[1, P]], base=0, channel_multiplier=0,
                              allow_small_or_imprecise_dtypes=True)
                    pool.iota(iota_hi[:, :], [[1, T]], base=0, channel_multiplier=0,
                              allow_small_or_imprecise_dtypes=True)
                    pool.iota(iota_blk[:, :], [[1, NB]], base=0, channel_multiplier=0,
                              allow_small_or_imprecise_dtypes=True)
                    pool.drain()
                    pool.affine_select(out=ident[:, :], in_=ident[:, :], compare_op=ALU.not_equal, fill=1.0, base=0,
                                       pattern=[[-1, P]], channel_multiplier=1)
                    pool.affine_select(out=lower[:, :], in_=lower[:, :], compare_op=ALU.is_gt, fill=0.0, base=0,
                                       pattern=[[1, P]], channel_multiplier=-1)
                    pool.drain().then_inc(built, 1)

                @block.vector
                def _(dve):
                    dve.memset(X[:, T - 1, :], 0.0)
                    dve.memset(edge_raw, PADKEY)
                    for key, col in (("D", 1), ("S", 0)):
                        dve.memset(pad_rec[key], 0)
                    dve.drain()
                    for key, col in (("D", 1), ("S", 0)):
                        dve.memset(pad_rec[key].rearrange("p (s f) -> p s f", f=4)[:, :, col:col + 1], PADKEY)
                    dve.drain().then_inc(cleared, 1)
                    dve.wait_ge(built, 1)
                    dve.tensor_copy(identb[:, :], ident[:, :])

                @block.sync
                def _(sp):
                    sp.wait_ge(cleared, 1)
                    n = 0
                    for key in ("D", "S"):
                        sp.dma_start(lists[key][0:NSLOT, :].rearrange("(p b) f -> p (b f)", p=SP_),
                                     pad_rec[key][0:SP_, :]).then_inc(filled, 16)
                        sp.dma_start(lists[key][NSLOT:NSLOT + 2, :].rearrange("(p b) f -> p (b f)", p=1),
                                     pad_rec[key][0:1, 0:8]).then_inc(filled, 16)
                    sp.dma_start(X[:, 0:T - 1, :], A["x"][0:(T - 1) * P, :].rearrange("(t p) f -> p t f", p=P)
                                 ).then_inc(loaded, 16)
                    sp.dma_start(X[0:TAIL, T - 1, :], A["x"][(T - 1) * P:N, :]).then_inc(loaded, 16)
                    for i, name in enumerate(("src", "dst", "edge_type_3")):
                        sp.dma_start(edge_raw[0:ROWS_FULL, i, :],
                                     A[name][0:ROWS_FULL * IB].rearrange("(p b) -> p b", b=IB)).then_inc(loaded, 16)
                        sp.dma_start(edge_raw[ROWS_FULL:ROWS_FULL + 1, i, 0:ROW_TAIL],
                                     A[name][ROWS_FULL * IB:E].rearrange("(p b) -> p b", p=1)).then_inc(loaded, 16)
                    sp.wait_ge(loaded, 16 * 8)
                    sp.wait_ge(filled, 16 * 4)

        def store_load(stores, loads):
            st, block, (stored, loaded) = stage("stored", "loaded")
            with st:
                @block.sync
                def _(sp):
                    for dst, src in stores:
                        sp.dma_start(dst, src).then_inc(stored, 16)
                    for dst, src in loads:
                        sp.dma_start(dst, src).then_inc(loaded, 16)
                    if stores:
                        sp.wait_ge(stored, 16 * len(stores))
                    if loads:
                        sp.wait_ge(loaded, 16 * len(loads))

        def rowb(a, n):
            return a.rearrange("(o n) -> o n", o=1).to_broadcast([P, n])

        def split_keys():
            st, block, _ = stage()
            with st:
                @block.vector
                def _(dve):
                    for k in range(3):
                        dve.tensor_copy(rec_all[:, :, k:k + 1], edge_raw[:, k, :].unsqueeze(2))
                    dve.memset(rec_all[:, :, 3:4], 0)
                    for key, i in (("D", 1), ("S", 0)):
                        dve.drain()
                        dve.tensor_scalar(key_tmp, edge_raw[:, i, :], 7, None, ALU.arith_shift_right)
                        dve.drain()
                        dve.tensor_copy(key_hi[key], key_tmp)
                        dve.drain()
                        dve.tensor_scalar(key_tmp, edge_raw[:, i, :], P - 1, None, ALU.bitwise_and)
                        dve.drain()
                        dve.tensor_copy(key_lo[key], key_tmp)
                        dve.tensor_scalar(key_far[key], key_hi[key], float(T), FAR, ALU.is_ge, ALU.mult)

        def histogram(key):
            st, block, (masks, counted, kept, t_dve, t_pe, t_act) = stage(
                "masks", "counted", "kept", "tick_dve", "tick_pe", "tick_act")
            lob = onehot[:, :, :].rearrange("p a b -> p (a b)").bitcast(bf16).rearrange("p (a b) -> p a b", b=P)
            hib = rhs[:, 0:2, :].rearrange("p a b -> p (a b)").bitcast(bf16)
            lo2 = ringf[:, 0:SB * P].bitcast(bf16).rearrange("p (z a b) -> p z a b", z=2, b=P)
            hi2 = ringf[:, SB * P:SB * P + SB * T].bitcast(bf16).rearrange("p (z a b) -> p z a b", z=2, b=T)
            with st:
                @block.vector
                def _(dve):
                    dve.sem_inc(counted, 2)
                    with dve.Fori(0, IB // SB // 2, 1) as i:
                        for z in range(2):
                            hold(dve, counted, 2 * i + z + 1, t_dve)
                            b = i * (2 * SB) + z * SB
                            dve.tensor_tensor(lo2[:, z], bc(iota_free[:, :], [P, SB, P], 1),
                                              bc(key_lo[key][:, ds(b, SB)], [P, SB, P], 2), ALU.is_equal)
                            dve.tensor_tensor(hi2[:, z], bc(iota_hi[:, :], [P, SB, T], 1),
                                              bc(key_hi[key][:, ds(b, SB)], [P, SB, T], 2), ALU.is_equal)
                            dve.drain().then_inc(masks, 1)

                @block.tensor
                def _(pe):
                    pe.sem_inc(kept, 2)
                    with pe.Fori(0, IB // SB // 2, 1) as i:
                        for z in range(2):
                            hold(pe, masks, 2 * i + z + 1, t_pe)
                            hold(pe, kept, 2 * i + z + 1, t_pe)
                            for u in range(SB):
                                mm = pe.matmul(ps[:, z, u * T:u * T + T], lo2[:, z, u, :], hi2[:, z, u, :],
                                               start=True, stop=True)
                            mm.then_inc(counted, 1)

                @block.scalar
                def _(act):
                    with act.Fori(0, IB // SB // 2, 1) as i:
                        for z in range(2):
                            hold(act, counted, 2 * i + z + 3, t_act)
                            b = i * (2 * SB) + z * SB + 1
                            act.activation(hist[:, ds(b, SB), :],
                                           ps[:, z, 0:SB * T].rearrange("p (b h) -> p b h", h=T), ACT.Copy)
                            act.drain().then_inc(kept, 1)

        def bases(key):
            st, block, (counted, summed) = stage("counted", "summed")
            cnt, tot, nblk, bend, bst, pre = (sm[:, i * 32:i * 32 + T] for i in range(6))
            nblk_i = sm[:, 192:192 + T].bitcast(i32)
            tidf = sm[0:1, 192:192 + NB]
            with st:
                @block.vector
                def _(dve):
                    dve.tensor_reduce(cnt, hist[:, 1:, :].rearrange("p b h -> p h b"), AX, ALU.add)
                    dve.drain().then_inc(counted, 1)
                    dve.wait_ge(summed, 1)
                    if key == "D":
                        dve.tensor_copy(deg[:, :], cnt)
                    dve.tensor_copy(pre, ps[:, 1, 0:T])
                    dve.tensor_scalar(tot, ps[:, 0, 0:T], float(P - 1), None, ALU.add)
                    dve.drain()
                    dve.tensor_copy(nblk_i, tot)
                    dve.drain()
                    dve.tensor_scalar(nblk_i, nblk_i, 7, None, ALU.arith_shift_right)
                    dve.drain()
                    dve.tensor_copy(nblk, nblk_i)
                    dve.drain()
                    dve.tensor_tensor_scan(bend, ones[:, 0:T], nblk, 0.0, ALU.mult, ALU.add)
                    dve.drain()
                    dve.tensor_tensor(bst, bend, nblk, ALU.subtract)
                    dve.drain()
                    dve.tensor_scalar(bst, bst, float(P), 1.0, ALU.mult, ALU.add)
                    dve.drain()
                    dve.tensor_tensor(hist[:, 0, :], bst, pre, ALU.add)
                    dve.memset(tidf, 0.0)
                    dve.drain()
                    for h in range(T):
                        dve.tensor_tensor_scan(hist[:, :, h], ones_row[:, :], hist[:, :, h], 0.0, ALU.mult, ALU.add)
                        dve.scalar_tensor_tensor(tidf, iota_blk[0:1, :], bend[0:1, h:h + 1], tidf, ALU.is_ge, ALU.add)
                        dve.drain()
                    dve.tensor_scalar(tidf, tidf, float(T - 1), None, ALU.min)
                    dve.drain()
                    dve.tensor_copy(tid[key][:, :], tidf)

                @block.tensor
                def _(pe):
                    pe.wait_ge(counted, 1)
                    pe.matmul(ps[:, 0, 0:T], ones[:, :], cnt, start=True, stop=True)
                    pe.matmul(ps[:, 1, 0:T], lower[:, :], cnt, start=True, stop=True).then_inc(summed, 1)

        def place(key):
            (st, block, (masks, turned, turned_kept, gram_done, gram_kept, found, placed, written,
                         t_dve, t_pe, t_act, t_pool, t_sp)) = stage(
                "masks", "turned", "turned_kept", "gram_done", "gram_kept", "found", "placed", "written",
                 "tick_dve", "tick_pe", "tick_act", "tick_pool", "tick_sp")
            rows0 = before["scattered"]
            before["scattered"] += 16 * SB * (IB // SB // 2)
            low = ringf[:, 0:SB * P // 2].bitcast(bf16).rearrange("p (a b) -> p a b", b=P)
            gram = ringf[:, SB * P:2 * SB * P].rearrange("p (a b) -> p a b", b=P)
            lowT = ringf[:, 2 * SB * P:3 * SB * P].rearrange("p (a b) -> p a b", b=P)
            high = rhs[:, :, :].rearrange("p a b -> p (a b)")[:, 0:SB * T].rearrange("p (a b) -> p a b", b=T)
            sel = onehot[:, :, :].rearrange("p a b -> p (a b)")[:, 0:SB * T].rearrange("p (a b) -> p a b", b=T)
            posf = sm[:, 0:SB]
            with st:
                @block.vector
                def _(dve):
                    with dve.Fori(0, IB // SB // 2, 1) as i:
                        for z in range(2):
                            b = i * (2 * SB) + z * SB
                            n = 2 * i + z
                            dve.drain()
                            dve.tensor_tensor(low[:, :, :], bc(iota_free[:, :], [P, SB, P], 1),
                                              bc(key_lo[key][:, ds(b, SB)], [P, SB, P], 2), ALU.is_equal)
                            dve.tensor_tensor(high, bc(iota_hi[:, :], [P, SB, T], 1),
                                              bc(key_hi[key][:, ds(b, SB)], [P, SB, T], 2), ALU.is_equal)
                            dve.drain().then_inc(masks, 1)
                            hold(dve, gram_done, n + 1, t_dve)
                            dve.tensor_tensor(gram[:, :, :],
                                              psf[:, 1024:1024 + SB * P].rearrange("p (a b) -> p a b", b=P),
                                              bc(lower[:, :], [P, SB, P], 1), ALU.mult)
                            dve.drain().then_inc(gram_kept, 1)
                            hold(dve, found, n + 1, t_dve)
                            dve.tensor_tensor(sel, ps[:, 4, 0:SB * T].rearrange("p (a b) -> p a b", b=T), high, ALU.mult)
                            dve.drain()
                            dve.tensor_reduce(posf, sel, AX, ALU.add)
                            dve.drain()
                            hold(dve, written, n + 1, t_dve)
                            dve.tensor_tensor(posidx[:, z, :], posf, key_far[key][:, ds(b, SB)], ALU.add)
                            dve.tensor_copy(recst[:, z], rec_all[:, ds(b, SB), :])
                            dve.drain().then_inc(placed, 1)

                @block.tensor
                def _(pe):
                    with pe.Fori(0, IB // SB, 1) as n:
                        hold(pe, masks, n + 1, t_pe)
                        for u in range(SB):
                            mm = pe.matmul(psf[:, u * P:u * P + P], low[:, u, :], identb[:, :], start=True, stop=True)
                        mm.then_inc(turned, 1)
                        hold(pe, turned_kept, n + 1, t_pe)
                        for u in range(SB):
                            mm = pe.matmul(psf[:, 1024 + u * P:1024 + u * P + P], lowT[:, u, :], lowT[:, u, :],
                                           start=True, stop=True)
                        mm.then_inc(gram_done, 1)
                        hold(pe, gram_kept, n + 1, t_pe)
                        for u in range(SB):
                            o = ps[:, 4, u * T:u * T + T]
                            pe.matmul(o, lowT[:, u, :], hist[:, ds(n * SB + u, 1), :], start=True, stop=False)
                            mm = pe.matmul(o, gram[:, u, :], high[:, u, :], start=False, stop=True)
                        mm.then_inc(found, 1)

                @block.scalar
                def _(act):
                    with act.Fori(0, IB // SB, 1) as n:
                        hold(act, turned, n + 1, t_act)
                        act.activation(lowT[:, :, :], psf[:, 0:SB * P].rearrange("p (a b) -> p a b", b=P), ACT.Copy)
                        act.drain().then_inc(turned_kept, 1)

                @block.gpsimd
                def _(pool):
                    with pool.Fori(0, IB // SB // 2, 1) as i:
                        for z in range(2):
                            hold(pool, placed, 2 * i + z + 1, t_pool)
                            for u in range(SB):
                                pool.indirect_dma_start(
                                    lists[key][:, :], bass.IndirectOffsetOnAxis(posidx[:, z, u:u + 1], 0),
                                    recst[:, z, u, :], None, bounds_check=NSLOT + 1, oob_is_err=False
                                ).then_inc(scattered[z], 16)

                @block.sync
                def _(sp):
                    sp.sem_inc(written, 2)
                    with sp.Fori(0, IB // SB // 2, 1) as i:
                        for z in range(2):
                            hold(sp, scattered[z], i * (16 * SB) + (rows0 + 16 * SB), t_sp)
                            sp.sem_inc(written, 1)

        def load_list(key):
            st, block, (loaded, conv, turned, kept) = stage("loaded", "converted", "turned", "kept")
            rec = ringf[0:SP_, 0:4 * SL].bitcast(i32).rearrange("p (s f) -> p s f", f=4)
            prev = ringf[0:SP_, 4 * SL:8 * SL].bitcast(i32).rearrange("p (s f) -> p s f", f=4)
            nxt = hidf[0:SP_, 0:4 * SL].bitcast(i32).rearrange("p (s f) -> p s f", f=4)
            fld = bigf[0:SP_, 0:3 * SL].rearrange("p (k s) -> p k s", k=3)
            tmp = bigf[:, 3 * SL:3 * SL + 6 * NB].rearrange("p (k b) -> p k b", k=6)
            tmp_i = tmp.bitcast(i32)
            own, other = (1, 0) if key == "D" else (0, 1)
            with st:
                @block.sync
                def _(sp):
                    n = 0
                    views = [(rec, 1)] + ([(prev, 0), (nxt, 2)] if key == "D" else [])
                    for dst, first in views:
                        sp.dma_start(dst, lists[key][first:first + NSLOT, :].rearrange("(p s) f -> p s f", p=SP_)
                                     ).then_inc(loaded, 16)
                    sp.wait_ge(loaded, 16 * len(views))

                @block.vector
                def _(dve):
                    dve.wait_ge(loaded, 48 if key == "D" else 16)
                    for k in range(3):
                        dve.tensor_copy(fld[:, k, :].unsqueeze(2), rec[:, :, k:k + 1])
                    dve.drain().then_inc(conv, 1)
                    if key == "D":
                        dve.tensor_copy(typ_s[:, :], fld[:, 2, :])
                        dve.tensor_copy(cont[:, :].unsqueeze(2), prev[:, :, 1:2])
                        dve.tensor_copy(isend[:, :].unsqueeze(2), nxt[:, :, 1:2])
                        dve.drain()
                        dve.tensor_tensor(cont[:, :], cont[:, :], fld[:, 1, :], ALU.not_equal)
                        dve.tensor_tensor(isend[:, :], isend[:, :], fld[:, 1, :], ALU.not_equal)
                        dve.drain()
                        dve.tensor_scalar(cont[:, :], cont[:, :], -BIG, None, ALU.mult)
                    dve.wait_ge(turned, 1)
                    for k in range(3):
                        dve.tensor_copy(tmp[:, k, :].rearrange("p (q c) -> p c q", c=4),
                                        ps[:, k, 0:NB].rearrange("p (c q) -> p c q", c=4))
                    dve.drain()
                    dve.tensor_copy(tmp_i[:, 3, :], tmp[:, own, :])
                    dve.drain()
                    dve.tensor_scalar(tmp_i[:, 3, :], tmp_i[:, 3, :], P - 1, None, ALU.bitwise_and)
                    dve.tensor_scalar(tmp[:, 4, :], tmp[:, own, :], float(NP), 1000.0, ALU.is_ge, ALU.mult)
                    dve.drain()
                    dve.tensor_copy(tmp[:, 5, :], tmp_i[:, 3, :])
                    dve.drain()
                    dve.tensor_tensor(lo[key][:, :], tmp[:, 5, :], tmp[:, 4, :], ALU.add)
                    for k in range(2):
                        dve.tensor_scalar(tmp[:, k, :], tmp[:, k, :], float(NP - 1), None, ALU.min)
                    dve.drain()
                    dve.tensor_copy(idx[key + "src"][:, :], tmp[:, 0, :])
                    dve.tensor_copy(idx[key + "dst"][:, :], tmp[:, 1, :])
                    if key == "D":
                        dve.tensor_copy(typ[:, :], tmp[:, 2, :])
                        dve.scalar_tensor_tensor(idx["DsrcT"][:, :], tmp[:, 2, :], float(NP), tmp[:, 0, :],
                                                 ALU.mult, ALU.add)
                        dve.scalar_tensor_tensor(idx["DdstT"][:, :], tmp[:, 2, :], float(NP), tmp[:, 1, :],
                                                 ALU.mult, ALU.add)

                @block.tensor
                def _(pe):
                    pe.wait_ge(conv, 1)
                    for k in range(3):
                        for c in range(4):
                            mm = pe.transpose(ps[:, k, c * SP_:(c + 1) * SP_], fld[:, k, c * P:(c + 1) * P],
                                              ident[0:SP_, 0:SP_])
                    mm.then_inc(turned, 1)

        def gather_issue(act, pool_idx, used, staged, tick):
            with act.Fori(0, TURNS, 1) as i:
                for j in range(NG):
                    hold(act, used, i * NG + j + 1, tick)
                    act.activation(idx_stage[:, j * GB:(j + 1) * GB], pool_idx[:, ds(i * RING + j * GB, GB)], ACT.Copy)
                    act.drain().then_inc(staged, 1)

        def gather_rows(pool, table, width, staged, gathered, tick):
            with pool.Fori(0, TURNS, 1) as i:
                for j in range(NG):
                    hold(pool, staged, i * NG + j + 1, tick)
                    for u in range(GB):
                        s = j * GB + u
                        pool.indirect_dma_start(ring[:, s, 0:width], None, table,
                                                bass.IndirectOffsetOnAxis(idx_stage[:, s:s + 1], 0)
                                                ).then_inc(gathered[j], 16)

        def fetch(table, index, width, dest):
            st, block, (used, staged, t_act, t_pool, t_dve) = stage(
                "used", "staged", "tick_act", "tick_pool", "tick_dve")
            rows0 = before["gathered"]
            before["gathered"] += 16 * GB * TURNS
            with st:
                @block.scalar
                def _(act):
                    gather_issue(act, index, used, staged, t_act)

                @block.gpsimd
                def _(pool):
                    gather_rows(pool, table, width, staged, gathered, t_pool)

                @block.vector
                def _(dve):
                    dve.sem_inc(used, NG)
                    with dve.Fori(0, TURNS, 1) as i:
                        for j in range(NG):
                            hold(dve, gathered[j], i * (16 * GB) + (rows0 + 16 * GB), t_dve)
                            dve.tensor_copy(dest[:, ds(i * RING + j * GB, GB), :], ring[:, j * GB:(j + 1) * GB, 0:width])
                            dve.drain().then_inc(used, 1)

        def edge_pass(key, n, table=None, index=None, payload=None, heads=0, rels=1):
            st, block, (used, staged, ready, t_act, t_pool, t_dve, t_pe) = stage(
                "summed", "staged", "operands",
                "tick_act", "tick_pool", "tick_dve", "tick_pe")
            rows0 = before["gathered"]
            if table is not None:
                before["gathered"] += 16 * GB * TURNS
            acc = big_view(n)
            width = F if heads or n == F else n
            with st:
                if table is not None:
                    @block.scalar
                    def _(act):
                        gather_issue(act, index, used, staged, t_act)

                    @block.gpsimd
                    def _(pool):
                        gather_rows(pool, table, width, staged, gathered, t_pool)

                @block.vector
                def _(dve):
                    dve.sem_inc(used, NG)
                    dve.memset(acc, 0.0)
                    with dve.Fori(0, TURNS, 1) as i:
                        for j in range(NG):
                            b = i * RING + j * GB
                            dve.drain()
                            dve.tensor_tensor(onehot[:, :, :], bc(iota_free[:, :], [P, GB, P], 1),
                                              bc(lo[key][:, ds(b, GB)], [P, GB, P], 2), ALU.is_equal)
                            if heads:
                                hold(dve, gathered[j], i * (16 * GB) + (rows0 + 16 * GB), t_dve)
                                c = F // heads
                                for r in range(rels):
                                    w4 = payload[:, ds(b, GB), r * heads:(r + 1) * heads]
                                    if heads == 1:
                                        dve.tensor_tensor(rhs[:, :, 0:F], ring[:, j * GB:(j + 1) * GB, 0:F],
                                                          w4.to_broadcast([P, GB, F]), ALU.mult)
                                    else:
                                        dve.tensor_tensor(
                                            rhs[:, :, r * F:(r + 1) * F].rearrange("p b (h c) -> p b h c", c=c),
                                            ring[:, j * GB:(j + 1) * GB, 0:F].rearrange("p b (h c) -> p b h c", c=c),
                                            bc(w4, [P, GB, heads, c], 3), ALU.mult)
                                if n > rels * F:
                                    dve.tensor_copy(rhs[:, :, rels * F:n], payload[:, ds(b, GB), 0:n - rels * F])
                            elif table is None:
                                dve.tensor_copy(rhs[:, :, 0:n], payload[:, ds(b, GB), 0:n])
                            dve.drain().then_inc(ready, 1)
                            hold(dve, used, i * NG + j + NG + 1, t_dve)
                            for u in range(GB):
                                t = dve.value_load(tid[key][0:1, ds(b + u, 1)], min_val=0, max_val=T - 1)
                                at = acc[:, ds(t, 1), :]
                                dve.tensor_tensor(at, at, ps[:, u:u + 1, 0:n], ALU.add)
                                dve.drain()

                @block.tensor
                def _(pe):
                    with pe.Fori(0, TURNS, 1) as i:
                        for j in range(NG):
                            hold(pe, ready, i * NG + j + 1, t_pe)
                            if table is not None and not heads:
                                hold(pe, gathered[j], i * (16 * GB) + (rows0 + 16 * GB), t_pe)
                            for u in range(GB):
                                r = ring[:, j * GB + u, 0:n] if table is not None and not heads else rhs[:, u, 0:n]
                                mm = pe.matmul(ps[:, u, 0:n], onehot[:, u, :], r, start=True, stop=True)
                            mm.then_inc(used, 1)

        def dense(sources, n, dest, bias=None, add=False):
            chunks = sum(k for _, k, _ in sources)
            wv = w_view(chunks, n)
            din = ringf[:, 0:DT * chunks * P].rearrange("p (t f) -> p t f", t=DT)
            first = 2 if n > 256 else 5
            step = 512 if n > 256 else 256
            outs = psf[:, first * 512:first * 512 + (DT - 1) * step + n]
            ov = psf[:, first * 512:min(first * 512 + DT * step, 4096)].rearrange("p (t f) -> p t f", f=step)[:, :, 0:n]
            st, block, (staged, turned, turned_kept, done, taken, t_dve, t_pe, t_act) = stage(
                "staged", "turned", "turned_kept", "done", "taken", "tick_dve", "tick_pe", "tick_act")
            with st:
                @block.vector
                def _(dve):
                    with dve.Fori(0, T // DT, 1) as q:
                        dve.drain()
                        c = 0
                        for view, k, scaled in sources:
                            for m in range(k):
                                o = din[:, :, (c + m) * P:(c + m + 1) * P]
                                i = view[:, ds(q * DT, DT), m * P:(m + 1) * P]
                                if scaled:
                                    dve.tensor_tensor(o, i, bc(deg[:, ds(q * DT, DT)], [P, DT, P], 2), ALU.mult)
                                else:
                                    dve.tensor_copy(o, i)
                            c += k
                        dve.drain().then_inc(staged, 1)
                        hold(dve, done, q + 1, t_dve)
                        d = dest[:, ds(q * DT, DT), :]
                        if bias is not None:
                            dve.tensor_tensor(d, ov, bc(bias, [P, DT, n], 1), ALU.add)
                        elif add:
                            dve.tensor_tensor(d, d, ov, ALU.add)
                        else:
                            dve.tensor_copy(d, ov)

                @block.tensor
                def _(pe):
                    with pe.Fori(0, T // DT, 1) as q:
                        hold(pe, staged, q + 1, t_pe)
                        for c in range(chunks):
                            for k in range(DT):
                                mm = pe.transpose(psf[:, (c * DT + k) * P:(c * DT + k + 1) * P],
                                                  din[:, k, c * P:(c + 1) * P], ident[:, :])
                        mm.then_inc(turned, 1)
                        hold(pe, turned_kept, q + 1, t_pe)
                        for k in range(DT):
                            o = psf[:, first * 512 + k * step:first * 512 + k * step + n]
                            for c in range(chunks):
                                mm = pe.matmul(o, dxt3[:, c * DT + k, :], wv[:, c, :], start=c == 0, stop=c == chunks - 1)
                        mm.then_inc(done, 1)

                @block.scalar
                def _(act):
                    with act.Fori(0, T // DT, 1) as q:
                        hold(act, turned, q + 1, t_act)
                        act.activation(dxt[:, 0:chunks * DT * P], psf[:, 0:chunks * DT * P], ACT.Copy)
                        act.drain().then_inc(turned_kept, 1)

        def norm_dve(dve, Y, n, scratch, var_ready, std_ready, k, gamma=None, beta=None):
            mean, var = sm[:, 0:T], sm[:, 32:32 + T]
            full = [P, T, n]
            dve.drain()
            dve.tensor_reduce(mean, Y, AX, ALU.add)
            dve.drain()
            dve.tensor_scalar(mean, mean, 1.0 / n, None, ALU.mult)
            dve.drain()
            dve.tensor_tensor(Y, Y, bc(mean, full, 2), ALU.subtract)
            dve.drain()
            dve.tensor_tensor(scratch, Y, Y, ALU.mult)
            dve.drain()
            dve.tensor_reduce(var, scratch, AX, ALU.add)
            dve.drain()
            dve.tensor_scalar(var, var, 1.0 / n, EPS, ALU.mult, ALU.add)
            dve.drain().then_inc(var_ready, 1)
            dve.wait_ge(std_ready, k)
            dve.reciprocal(var, var)
            dve.drain()
            dve.tensor_tensor(Y, Y, bc(var, full, 2), ALU.mult)
            dve.drain()
            if gamma is not None:
                dve.tensor_tensor(Y, Y, bc(gamma, full, 1), ALU.mult)
                dve.drain()
                dve.tensor_tensor(Y, Y, bc(beta, full, 1), ALU.add)
                dve.drain()
                dve.tensor_scalar(Y, Y, 0.0, None, ALU.max)

        def norm(Y, n, scratch, gamma=None, beta=None, before=None):
            st, block, (var_ready, std_ready) = stage("var_ready", "std_ready")
            with st:
                @block.vector
                def _(dve):
                    if before:
                        before(dve)
                    norm_dve(dve, Y, n, scratch, var_ready, std_ready, 1, gamma, beta)

                @block.scalar
                def _(act):
                    act.wait_ge(var_ready, 1)
                    act.activation(sm[:, 32:32 + T], sm[:, 32:32 + T], ACT.Sqrt)
                    act.drain().then_inc(std_ready, 1)

        def dve_stage(body):
            st, block, _ = stage()
            with st:
                @block.vector
                def _(dve):
                    body(dve)

        def edge_maxima(K, rels):
            st, block, (turned, tails, tails_up, carry, carry_up, ends, back, taken) = stage(
                "turned", "tails", "tails_turned", "carry", "carry_turned", "ends", "back", "taken")
            hs = min(K, HEADS)
            V = bigf[0:SP_, 0:K * SL].rearrange("p (k s) -> p k s", k=K)
            R = hidf[0:SP_, 0:K * SL].rearrange("p (k s) -> p k s", k=K)
            if K == HEADS or K == 1:
                R = dxt[0:SP_, 0:K * SL].rearrange("p (k s) -> p k s", k=K)
            tail = sm[0:SP_, 0:2 * K].rearrange("p (z k) -> p z k", z=2)
            rows = sm[0:K, 64:64 + 2 * SP_].rearrange("p (z s) -> p z s", z=2)
            crow = sm[0:K, 64 + 2 * SP_:64 + 3 * SP_ + 1]
            init = sm[0:SP_, 32:32 + K]
            mask = onehot[0:SP_, :, :].rearrange("p a b -> p (a b)")
            maskb = rhs[0:SP_, :, :].rearrange("p a b -> p (a b)")[:, 0:SL]
            with st:
                @block.tensor
                def _(pe):
                    for h in range(hs):
                        for c in range(4):
                            mm = pe.transpose(ps[0:SP_, h, c * P:(c + 1) * P],
                                              ebuf[:, :, h].rearrange("p (q c) -> p c q", c=4)[:, c, :], ident[:, :])
                    mm.then_inc(turned, 1)
                    pe.wait_ge(tails, 1)
                    pe.transpose(ps[0:K, 4, 0:SP_], tail[:, 0, :], ident[0:SP_, 0:SP_])
                    pe.transpose(ps[0:K, 4, SP_:2 * SP_], tail[:, 1, :], ident[0:SP_, 0:SP_]).then_inc(tails_up, 1)
                    pe.wait_ge(carry, 1)
                    pe.transpose(ps[0:SP_, 5, 0:K], crow[:, 0:SP_], ident[0:K, 0:K]).then_inc(carry_up, 1)
                    pe.wait_ge(ends, 1)
                    for k in range(K):
                        if k >= 4:
                            pe.wait_ge(taken, k - 3)
                        for c in range(4):
                            mm = pe.transpose(ps[:, k % 4, c * SP_:(c + 1) * SP_], V[:, k, c * P:(c + 1) * P],
                                              ident[0:SP_, 0:SP_])
                        mm.then_inc(back, 1)

                @block.vector
                def _(dve):
                    dve.wait_ge(turned, 1)
                    for r in range(rels):
                        if rels > 1:
                            dve.drain()
                            dve.tensor_scalar(mask, typ_s[:, :], float(r), None, ALU.is_equal)
                            dve.drain()
                            dve.tensor_scalar(maskb, mask, 1.0, BIG, ALU.subtract, ALU.mult)
                            dve.drain()
                        for h in range(hs):
                            v = V[:, r * hs + h, :]
                            if rels > 1:
                                dve.tensor_tensor(v, ps[0:SP_, h, :], mask, ALU.mult)
                                dve.drain()
                                dve.tensor_tensor(v, v, maskb, ALU.add)
                            else:
                                dve.tensor_copy(v, ps[0:SP_, h, :])
                    dve.drain()
                    for k in range(K):
                        dve.tensor_tensor_scan(R[:, k, :], cont[:, :], V[:, k, :], -BIG, ALU.add, ALU.max)
                    dve.tensor_reduce(tail[:, 1, 0:1], cont[:, :], AX, ALU.min)
                    dve.drain()
                    dve.tensor_copy(tail[:, 0, :].unsqueeze(2), R[:, :, SL - 1:SL])
                    if K > 1:
                        dve.tensor_copy(tail[:, 1, 1:K], tail[:, 1, 0:1].to_broadcast([SP_, K - 1]))
                    dve.drain().then_inc(tails, 1)
                    dve.wait_ge(tails_up, 1)
                    dve.tensor_copy(rows, ps[0:K, 4, 0:2 * SP_].rearrange("p (z s) -> p z s", z=2))
                    dve.memset(crow[:, 0:1], -BIG)
                    dve.drain()
                    dve.tensor_tensor_scan(crow[:, 1:SP_ + 1], rows[:, 1, :], rows[:, 0, :], -BIG, ALU.add, ALU.max)
                    dve.drain().then_inc(carry, 1)
                    dve.wait_ge(carry_up, 1)
                    dve.tensor_copy(init, ps[0:SP_, 5, 0:K])
                    dve.drain()
                    for k in range(K):
                        dve.tensor_tensor_scan(R[:, k, :], cont[:, :], V[:, k, :], init[:, k:k + 1], ALU.add, ALU.max)
                    dve.drain()
                    for k in range(K):
                        dve.tensor_tensor(V[:, k, :], R[:, k, :], isend[:, :], ALU.mult)
                    dve.drain().then_inc(ends, 1)
                    for k in range(K):
                        dve.wait_ge(back, k + 1)
                        dve.tensor_copy(em[:, :, k].rearrange("p (q c) -> p c q", c=4),
                                        ps[:, k % 4, 0:NB].rearrange("p (c q) -> p c q", c=4))
                        dve.drain().then_inc(taken, 1)

        def node_maxima(K, slope, own):
            def body(dve):
                M = big_view(K)
                m = node_a[:, :, 24:24 + K] if K == 12 else node_a[:, :, 8:8 + K]
                d = node_a[:, :, 12:12 + K] if K == 12 else node_a[:, :, 4:4 + K]
                if own:
                    lone = sm[:, 64:64 + T]
                    dve.tensor_scalar(lone, sm[:, 128:128 + T], -BIG, None, ALU.mult)
                    dve.drain()
                    dve.tensor_tensor(M, M, bc(lone, [P, T, K], 2), ALU.add)
                    dve.drain()
                    dve.tensor_tensor(M, M, node_a[:, :, 0:K], ALU.max)
                    dve.drain()
                dve.tensor_tensor(M, M, d, ALU.add)
                dve.drain()
                dve.scalar_tensor_tensor(m, M, slope, M, ALU.mult, ALU.max)
            dve_stage(body)

        def edge_weights(slope, rels, heads):
            st, block, (arg, done) = stage("argument", "weights_done")
            with st:
                @block.vector
                def _(dve):
                    a, d, m = ebuf[:, :, 0:heads], ebuf[:, :, 4:4 + heads], ebuf[:, :, 8:8 + heads]
                    dve.tensor_tensor(a, a, d, ALU.add)
                    dve.drain()
                    dve.scalar_tensor_tensor(a, a, slope, a, ALU.mult, ALU.max)
                    dve.drain()
                    dve.tensor_tensor(a, a, m, ALU.subtract)
                    dve.drain().then_inc(arg, 1)
                    dve.wait_ge(done, 1)
                    if rels > 1:
                        mask = ebuf[:, :, 4]
                        for r in range(rels):
                            dve.drain()
                            dve.tensor_scalar(mask, typ[:, :], float(r), None, ALU.is_equal)
                            dve.drain()
                            dve.tensor_tensor(em[:, :, r * heads:(r + 1) * heads], a, bc(mask, [P, NB, heads], 2), ALU.mult)

                @block.scalar
                def _(act):
                    act.wait_ge(arg, 1)
                    o = ebuf[:, :, 0:heads] if rels > 1 else em[:, :, 0:heads]
                    act.activation(o, ebuf[:, :, 0:heads], ACT.Exp)
                    act.drain().then_inc(done, 1)

        def head_terms(src, att, dst, scratch, groups):
            c = src.shape[2] // groups

            def body(dve):
                dve.tensor_tensor(scratch, src, bc(att, list(src.shape), 1), ALU.mult)
                dve.drain()
                dve.tensor_reduce(dst, scratch.rearrange("p t (g c) -> p t g c", c=c), AX, ALU.add)
                dve.drain()
            return body

        constants()
        store_load([(tiles(x_table), X[:, :, :])],
                   [(w_view(2, HID)[:, 0, :], A["L0_gnn_W_l0"]), (w_view(2, HID)[:, 1, :], A["L0_gnn_W_r0"]),
                    (biases[:, 0:HID], rowb(A["L0_gnn_b_l0"], HID)), (biases[:, HID:2 * HID], rowb(A["L0_gnn_g0"], HID)),
                    (biases[:, 2 * HID:3 * HID], rowb(A["L0_gnn_be0"], HID)),
                    (biases[:, 3 * HID:4 * HID], rowb(A["L0_gnn_b_l1"], HID)),
                    (biases[:, 4 * HID:5 * HID], rowb(A["L0_gnn_g1"], HID)),
                    (biases[:, 5 * HID:6 * HID], rowb(A["L0_gnn_be1"], HID))])
        split_keys()
        for key in ("D", "S"):
            histogram(key)
            bases(key)
            place(key)
        load_list("S")
        load_list("D")

        def degrees(dve):
            dve.tensor_scalar(sm[:, 128:128 + T], deg[:, :], 0.0, None, ALU.is_equal)
            dve.tensor_scalar(deg[:, :], deg[:, :], 1.0, None, ALU.max)
            dve.drain()
            dve.reciprocal(deg[:, :], deg[:, :])
        no_edge = sb("no_edge", [P, T])

        def degrees(dve):
            dve.tensor_scalar(no_edge[:, :], deg[:, :], 0.0, None, ALU.is_equal)
            dve.drain()
            dve.tensor_scalar(deg[:, :], deg[:, :], 1.0, None, ALU.max)
            dve.drain()
            dve.reciprocal(deg[:, :], deg[:, :])
        dve_stage(degrees)

        edge_pass("D", F, x_table, idx["Dsrc"][:, :])
        dense([(big_view(F), 1, True), (X[:, :, :], 1, False)], HID, hid, bias=biases[:, 0:HID])
        norm(hid, HID, big_view(HID), biases[:, HID:2 * HID], biases[:, 2 * HID:3 * HID])
        kn = "(k p) n -> p k n"
        store_load([(tiles(hidden1_table), hid)],
                   [(w_view(4, HID)[:, 0:2, :], A["L0_gnn_W_l1"].rearrange(kn, p=P)),
                    (w_view(4, HID)[:, 2:4, :], A["L0_gnn_W_r1"].rearrange(kn, p=P))])
        edge_pass("D", HID, hidden1_table, idx["Dsrc"][:, :])
        dense([(big_view(HID), 2, True), (hid, 2, False)], HID, hid, bias=biases[:, 3 * HID:4 * HID])
        norm(hid, HID, big_view(HID), biases[:, 4 * HID:5 * HID], biases[:, 5 * HID:6 * HID])
        store_load([], [(w_view(2, F), A["L0_gnn_W_l2"].rearrange(kn, p=P))])
        dense([(hid, 2, False)], F, big_view(F))
        store_load([(tiles(proj2_table), big_view(F))],
                   [(w_view(2, F), A["L0_gnn_W_r2"].rearrange(kn, p=P)),
                    (biases[:, 0:F], rowb(A["L0_gnn_b_l2"], F))])
        edge_pass("D", F, proj2_table, idx["Dsrc"][:, :])
        full = [P, T, F]

        def sage2(dve):
            acc = big_view(F)
            dve.tensor_tensor(acc, acc, bc(deg[:, :], full, 2), ALU.mult)
            dve.drain()
            dve.tensor_tensor(acc, acc, bc(biases[:, 0:F], full, 1), ALU.add)
            dve.drain()
            dve.tensor_tensor(X[:, :, :], X[:, :, :], acc, ALU.add)
        dve_stage(sage2)
        dense([(hid, 2, False)], F, X[:, :, :], add=True)
        norm(X[:, :, :], F, big_view(F))

        att_src, att_dst = biases[:, 0:384], biases[:, 384:768]
        rel_bias, rel_w = biases[:, 768:1152], biases[:, 1152:1155]
        rhc = "(o r) h c -> o (r h c)"
        store_load([], [(w_view(1, 384)[:, 0, :].rearrange("p (r n) -> p r n", r=NREL), A["L1_gnn_W"].rearrange("r p n -> p r n")),
                        (att_src, A["L1_gnn_att_src"].rearrange(rhc, o=1).to_broadcast([P, 384])),
                        (att_dst, A["L1_gnn_att_dst"].rearrange(rhc, o=1).to_broadcast([P, 384])),
                        (rel_bias, A["L1_gnn_bias"].rearrange("(o r) c -> o (r c)", o=1).to_broadcast([P, 384])),
                        (rel_w, rowb(A["L1_gnn_rel_w"], NREL))])
        relh = big_view(384)
        dense([(X[:, :, :], 1, False)], 384, relh)

        def rel_terms(dve):
            for r in range(NREL):
                h = relh[:, :, r * F:(r + 1) * F]
                head_terms(h, att_src[:, r * F:(r + 1) * F], node_a[:, :, 4 * r:4 * r + 4], H1, HEADS)(dve)
                head_terms(h, att_dst[:, r * F:(r + 1) * F], node_a[:, :, 12 + 4 * r:16 + 4 * r], H1, HEADS)(dve)
        dve_stage(rel_terms)
        rows = [slice(r * NP, (r + 1) * NP) for r in range(NREL)]
        store_load([(tiles(rel_h_table[rows[r], :]), relh[:, :, r * F:(r + 1) * F]) for r in range(NREL)]
                   + [(tiles(rel_src_table[rows[r], :]), node_a[:, :, 4 * r:4 * r + 4]) for r in range(NREL)], [])
        fetch(rel_src_table, idx["DsrcT"][:, :], 4, ebuf[:, :, 0:4])
        edge_maxima(12, NREL)
        edge_pass("D", 12, payload=em)

        def rel_maxima(dve):
            M = big_view(12)
            lone = sm[:, 64:64 + T]
            dve.tensor_scalar(lone, no_edge[:, :], -BIG, None, ALU.mult)
            dve.drain()
            dve.tensor_tensor(M, M, bc(lone, [P, T, 12], 2), ALU.add)
            dve.drain()
            dve.tensor_tensor(M, M, node_a[:, :, 0:12], ALU.max)
            dve.drain()
            dve.tensor_tensor(M, M, node_a[:, :, 12:24], ALU.add)
            dve.drain()
            dve.scalar_tensor_tensor(node_a[:, :, 24:36], M, 0.2, M, ALU.mult, ALU.max)
        dve_stage(rel_maxima)
        store_load([(tiles(rel_dst_table[rows[r], 4 * z:4 * z + 4]), node_a[:, :, 12 + 12 * z + 4 * r:16 + 12 * z + 4 * r])
                    for r in range(NREL) for z in range(2)], [])
        fetch(rel_dst_table, idx["DdstT"][:, :], 8, ebuf[:, :, 4:12])
        edge_weights(0.2, NREL, HEADS)
        edge_pass("D", 396, rel_h_table, idx["DsrcT"][:, :], payload=em, heads=HEADS, rels=NREL)

        own_w = node_a[:, :, 0:12]

        def own_args(dve):
            dve.tensor_tensor(own_w, own_w, node_a[:, :, 12:24], ALU.add)
            dve.drain()
            dve.scalar_tensor_tensor(own_w, own_w, 0.2, own_w, ALU.mult, ALU.max)
            dve.drain()
            dve.tensor_tensor(own_w, own_w, node_a[:, :, 24:36], ALU.subtract)
            dve.tensor_reduce(sm[:, 0:1], rel_w, AX, ALU.max)
            dve.drain()
            dve.tensor_scalar(rel_w, rel_w, sm[:, 0:1], None, ALU.subtract)

        def exp_stage(before, pairs):
            st, block, (arg,) = stage("argument")
            with st:
                @block.vector
                def _(dve):
                    before(dve)
                    dve.drain().then_inc(arg, 1)

                @block.scalar
                def _(act):
                    act.wait_ge(arg, 1)
                    for o, i, f in pairs:
                        act.activation(o, i, f)
        exp_stage(own_args, [(own_w, own_w, ACT.Exp), (rel_w, rel_w, ACT.Exp)])
        acc3 = big_view(396)

        def rel_norms(dve):
            dve.tensor_reduce(sm[:, 0:1], rel_w, AX, ALU.add)
            dve.tensor_tensor(acc3[:, :, 384:396], acc3[:, :, 384:396], own_w, ALU.add)
            dve.drain()
            dve.reciprocal(sm[:, 0:1], sm[:, 0:1])
            dve.reciprocal(acc3[:, :, 384:396], acc3[:, :, 384:396])
            dve.drain()
            dve.tensor_scalar(rel_w, rel_w, sm[:, 0:1], None, ALU.mult)
        dve_stage(rel_norms)
        for r in range(NREL):
            store_load([], [(H1, tiles(rel_h_table[rows[r], :]))])

            def rel_sum(dve):
                for t in range(0, T, DT):
                    def v(a):
                        return a[:, t:t + DT, :].rearrange("p t (h c) -> p t h c", c=HD)

                    def w(a):
                        return bc(a[:, t:t + DT, :], [P, DT, HEADS, HD], 3)
                    h, s = v(H1), v(acc3[:, :, r * F:(r + 1) * F])
                    dve.tensor_tensor(h, h, w(own_w[:, :, 4 * r:4 * r + 4]), ALU.mult)
                    dve.drain()
                    dve.tensor_tensor(h, h, s, ALU.add)
                    dve.drain()
                    dve.tensor_tensor(h, h, w(acc3[:, :, 384 + 4 * r:388 + 4 * r]), ALU.mult)
                dve.drain()
                dve.tensor_tensor(H1, H1, bc(rel_bias[:, r * F:(r + 1) * F], full, 1), ALU.add)
                dve.drain()
                dve.scalar_tensor_tensor(X[:, :, :], H1, rel_w[:, r:r + 1], X[:, :, :], ALU.mult, ALU.add)
            dve_stage(rel_sum)
        norm(X[:, :, :], F, big_view(F))

        store_load([], [(w_view(1, F)[:, 0, :], A["L2_gnn_W"]), (biases[:, 0:F], rowb(A["L2_gnn_a_i"], F)),
                        (biases[:, F:2 * F], rowb(A["L2_gnn_a_j"], F))])
        dense([(X[:, :, :], 1, False)], F, H1)

        def l2_terms(dve):
            dve.tensor_tensor(H1, H1, X[:, :, :], ALU.add)
            dve.memset(node_a[:, :, :], 0.0)
            dve.drain()
            head_terms(X[:, :, :], biases[:, F:2 * F], node_a[:, :, 0:1], big_view(F), 1)(dve)
            head_terms(X[:, :, :], biases[:, 0:F], node_a[:, :, 4:5], big_view(F), 1)(dve)
        dve_stage(l2_terms)
        store_load([(tiles(src_table[0]), node_a[:, :, 0:4])], [])
        fetch(src_table[0], idx["Dsrc"][:, :], 4, ebuf[:, :, 0:4])
        edge_maxima(1, 1)
        edge_pass("D", 1, payload=em)
        node_maxima(1, 0.01, False)
        store_load([(tiles(dst_table[0]), node_a[:, :, 4:12])], [])
        fetch(dst_table[0], idx["Ddst"][:, :], 8, ebuf[:, :, 4:12])
        edge_weights(0.01, 1, 1)
        edge_pass("D", 1, payload=em)

        def l2_messages(dve):
            den = sm[:, 0:T]
            dve.tensor_tensor(den, big_view(1)[:, :, 0], no_edge[:, :], ALU.add)
            dve.drain()
            dve.reciprocal(den, den)
            dve.drain()
            dve.tensor_tensor(H1, H1, bc(den, full, 2), ALU.mult)
        dve_stage(l2_messages)
        store_load([(tiles(row_table[0]), H1)], [])
        fetch(src_table[0], idx["Ssrc"][:, :], 4, ebuf[:, :, 0:4])
        fetch(dst_table[0], idx["Sdst"][:, :], 8, ebuf[:, :, 4:12])
        edge_weights(0.01, 1, 1)
        edge_pass("S", F, row_table[0], idx["Sdst"][:, :], payload=em, heads=1)
        exp_stage(lambda dve: None, [(big_view(F), big_view(F), ACT.Gelu)])

        def add_acc(dve):
            dve.tensor_tensor(X[:, :, :], X[:, :, :], big_view(F), ALU.add)
        norm(X[:, :, :], F, big_view(F), before=add_acc)

        def keep_x(dve):
            dve.tensor_copy(XR, X[:, :, :])
        dve_stage(keep_x)
        for l in range(2):
            store_load([], [(w_view(1, F)[:, 0, :], A["L3_gnn_W"][l]),
                            (biases[:, 0:F], A["L3_gnn_a_src"][l:l + 1].rearrange("o h c -> o (h c)").to_broadcast([P, F])),
                            (biases[:, F:2 * F], A["L3_gnn_a_dst"][l:l + 1].rearrange("o h c -> o (h c)").to_broadcast([P, F])),
                            (biases[:, 2 * F:3 * F], A["L3_gnn_b"][l:l + 1, :].to_broadcast([P, F]))])
            dense([(X[:, :, :], 1, False)], F, H1)

            def gat_terms(dve):
                head_terms(H1, biases[:, 0:F], node_a[:, :, 0:4], big_view(F), HEADS)(dve)
                head_terms(H1, biases[:, F:2 * F], node_a[:, :, 4:8], big_view(F), HEADS)(dve)
            dve_stage(gat_terms)
            store_load([(tiles(src_table[1 + l]), node_a[:, :, 0:4]), (tiles(row_table[1 + l]), H1)], [])
            fetch(src_table[1 + l], idx["Dsrc"][:, :], 4, ebuf[:, :, 0:4])
            edge_maxima(4, 1)
            edge_pass("D", 4, payload=em)
            node_maxima(4, 0.2, False)
            store_load([(tiles(dst_table[1 + l]), node_a[:, :, 4:12])], [])
            fetch(dst_table[1 + l], idx["Ddst"][:, :], 8, ebuf[:, :, 4:12])
            edge_weights(0.2, 1, HEADS)
            edge_pass("D", F + 4, row_table[1 + l], idx["Dsrc"][:, :], payload=em, heads=HEADS)
            acc = big_view(F + 4)

            def gat_node(dve):
                dve.tensor_scalar(acc[:, :, F:F + 4], acc[:, :, F:F + 4], 1e-16, None, ALU.add)
                dve.tensor_tensor(X[:, :, :], X[:, :, :], bc(biases[:, 2 * F:3 * F], full, 1), ALU.add)
                dve.drain()
                dve.reciprocal(acc[:, :, F:F + 4], acc[:, :, F:F + 4])
                dve.drain()
                for t in range(0, T, DT):
                    a = acc[:, t:t + DT, 0:F].rearrange("p t (h c) -> p t h c", c=HD)
                    dve.tensor_tensor(a, a, bc(acc[:, t:t + DT, F:F + 4], [P, DT, HEADS, HD], 3), ALU.mult)
                dve.drain()
                dve.tensor_tensor(X[:, :, :], X[:, :, :], acc[:, :, 0:F], ALU.add)
                if l == 0:
                    dve.drain()
                    dve.tensor_scalar(H1, X[:, :, :], 0.0, None, ALU.min)

            def elu_sum(dve):
                dve.tensor_scalar(X[:, :, :], X[:, :, :], 0.0, -1.0, ALU.max, ALU.add)
                dve.drain()
                dve.tensor_tensor(X[:, :, :], X[:, :, :], H1, ALU.add)
            if l == 0:
                exp_stage(gat_node, [(H1, H1, ACT.Exp)])
                dve_stage(elu_sum)
            else:
                dve_stage(gat_node)

        def add_back(dve):
            dve.tensor_tensor(X[:, :, :], X[:, :, :], XR, ALU.add)
        norm(X[:, :, :], F, big_view(F), before=add_back)
        store_load([(out[0:(T - 1) * P, :].rearrange("(t p) f -> p t f", p=P), X[:, 0:T - 1, :]),
                    (out[(T - 1) * P:N, :], X[0:TAIL, T - 1, :])], [])


_IN = ["x", "src", "dst", "edge_type_3", "L0_gnn_W_l0", "L0_gnn_b_l0", "L0_gnn_W_r0", "L0_gnn_g0", "L0_gnn_be0",
       "L0_gnn_W_l1", "L0_gnn_b_l1", "L0_gnn_W_r1", "L0_gnn_g1", "L0_gnn_be1", "L0_gnn_W_l2", "L0_gnn_b_l2",
       "L0_gnn_W_r2", "L1_gnn_W", "L1_gnn_att_src", "L1_gnn_att_dst", "L1_gnn_bias", "L1_gnn_rel_w", "L2_gnn_a_i",
       "L2_gnn_a_j", "L2_gnn_W", "L3_gnn_W", "L3_gnn_a_src", "L3_gnn_a_dst", "L3_gnn_b"]


def kernel(**inputs):
    import numpy as np
    import concourse.bacc as bacc
    from concourse.bass_utils import run_bass_kernel_spmd as run
    nc = bacc.Bacc("TRN2", target_bir_lowering=False, num_devices=1)
    arrays, aps = {}, {}
    for name in _IN:
        a = np.ascontiguousarray(inputs[name])
        arrays["in_" + name] = a
        aps[name] = nc.dram_tensor("in_" + name, a.shape, mybir.dt.from_np(a.dtype), kind="ExternalInput").ap()
    o = nc.dram_tensor("out", (N, F), mybir.dt.float32, kind="ExternalOutput").ap()
    build(nc, aps, o)
    r = run(nc, [arrays], core_ids=[0])
    return r.results[0]["out"]
```

```python
import concourse.bass as bass
from concourse import mybir
from contextlib import ExitStack

P = 128
N = 3125
E = 53125
F = 128
HID = 256
HEADS, HD = 4, 32
NREL = 3
T = (N + P - 1) // P
NP = T * P
TAIL = N - (T - 1) * P
SB = 8
IB = -(-E // (P * 2 * SB)) * 2 * SB
ROWS_FULL, ROW_TAIL = divmod(E, IB)
RING = 16
GB = 4
NG = RING // GB
NB = -(-(-(-E // P) + T) // RING) * RING
NSLOT = NB * P
TURNS = NB // RING
SP_ = NB // 4
SL = 4 * P
PADKEY = 4095
FAR = 1e6
BIG = 1e30
DT = 5
EPS = 1e-5
SIDE = 2 * NREL * HEADS
SIDE_FIT = 512 // SIDE
SIDE_BACK = 7 * 512 + SIDE_FIT * SIDE - T * F


def build(nc, A, out):
    f32, bf16, i32 = mybir.dt.float32, mybir.dt.bfloat16, mybir.dt.int32
    ALU, ACT, AX = mybir.AluOpType, mybir.ActivationFunctionType, mybir.AxisListType.X
    ds = bass.ds
    ctx = ExitStack()
    with ctx:
        def sb(name, shape, dt=f32):
            return ctx.enter_context(nc.sbuf_tensor(name, shape, dt))

        def dram(name, shape, dt=f32):
            return nc.dram_tensor(name, shape, dt, kind="Internal").ap()

        lists = {"D": dram("edges_by_dst", (NSLOT + 2, 4), i32), "S": dram("edges_by_src", (NSLOT + 2, 4), i32)}
        x_table = dram("x_table", (NP, F))
        hidden1_table = dram("hidden1_table", (NP, HID))
        proj2_table = dram("proj2_table", (NP, F))
        rel_h_table = dram("rel_h_table", (NREL * NP, F))
        rel_src_table = dram("rel_src_table", (NREL * NP, HEADS))
        row_table = [dram(f"row_table{i}", (NP, F)) for i in range(3)]

        iota_free = sb("iota_free", [P, P])
        iota_part = sb("iota_part", [P, 1])
        iota_hi = sb("iota_hi", [P, T])
        iota_blk = sb("iota_blk", [1, NB])
        ident = sb("ident", [P, P])
        identb = sb("identb", [P, P], bf16)
        ones = sb("ones", [P, P])
        lower = sb("lower", [P, P])
        X = sb("X", [P, T, F])
        bigf = sb("bigf", [P, (IB + 1) * T])
        hidf = sb("hidf", [P, T * HID])
        ringf = sb("ringf", [P, RING * HID])
        onehot2 = sb("onehot2", [P, 2, GB, P])
        onehot = onehot2[:, 0]
        zeros = sb("zeros", [P, 512], bf16)
        rhsf = sb("rhsf", [P, GB * 396])
        rhs = rhsf[:, :].rearrange("p (b f) -> p b f", b=GB)
        rhs2 = rhsf[:, 0:2 * GB * 160].rearrange("p (z b f) -> p z b f", z=2, b=GB)
        idx_stage = sb("idx_stage", [P, RING], i32)
        weights = sb("weights", [P, 4 * HID])
        biases = sb("biases", [P, 6 * HID])
        dxt = sb("dxt", [P, 4 * DT * P])
        sm = sb("sm", [P, 640])
        deg = sb("deg", [P, T])
        node_a = sb("node_a", [P, T, 36])
        idx = {k: sb("idx_" + k, [P, NB], i32) for k in ("Dsrc", "DsrcT", "Sdst")}
        lo = {"D": sb("lo_D", [P, NB]), "S": sb("lo_S", [P, NB])}
        typ = sb("typ", [P, NB])
        hi_other = {"D": sb("hi_other_D", [P, NB]), "S": sb("hi_other_S", [P, NB])}
        rows_own = {k: sb("rows_own_" + k, [SP_, SL], bf16) for k in ("D", "S")}
        rows_other = {k: sb("rows_other_" + k, [SP_, SL], bf16) for k in ("D", "S")}
        minus_part = sb("minus_part", [P, 1])
        no_edge = sb("no_edge", [P, T])
        tid_side = sb("tid_side", [1, NB], i32)
        tid = {"D": sb("tid_D", [1, NB], i32), "S": sb("tid_S", [1, NB], i32)}
        cont = sb("cont", [SP_, SL])
        isend = sb("isend", [SP_, SL])
        typ_s = sb("typ_s", [SP_, SL])
        ebuf = sb("ebuf", [P, NB, 12])
        em = sb("em", [P, NB, 12])
        posidx = sb("posidx", [P, 2, SB], i32)
        recst = sb("recst", [P, 2, SB, 4], i32)
        ps = ctx.enter_context(nc.psum_tensor("ps", [P, 8, 512], f32))
        psf = ps[:, :, :].rearrange("p a b -> p (a b)")

        hist = bigf[:, :].rearrange("p (b h) -> p b h", h=T)
        hid = hidf[:, :].rearrange("p (t f) -> p t f", t=T)
        H1 = hidf[:, 0:T * F].rearrange("p (t f) -> p t f", t=T)
        XR = hidf[:, T * F:2 * T * F].rearrange("p (t f) -> p t f", t=T)
        ring = ringf[:, :].rearrange("p (r f) -> p r f", r=RING)
        ebuf_i = ebuf[:, :, :].rearrange("p a b -> p (a b)").bitcast(i32)
        edge_raw = ebuf_i[:, 0:3 * IB].rearrange("p (k b) -> p k b", k=3)
        rec_all = ebuf_i[:, 3 * IB:7 * IB].rearrange("p (b k) -> p b k", k=4)
        KW = IB + SB
        key_lo_all = {"D": hidf[:, 0:KW], "S": hidf[:, KW:2 * KW]}
        key_hi_all = {"D": hidf[:, 2 * KW:3 * KW], "S": hidf[:, 3 * KW:4 * KW]}
        key_lo = {k: v[:, 0:IB] for k, v in key_lo_all.items()}
        key_hi = {k: v[:, 0:IB] for k, v in key_hi_all.items()}
        key_far = {"D": hidf[:, 4 * KW:4 * KW + IB], "S": hidf[:, 5 * KW:5 * KW + IB]}
        key_tmp = hidf[:, 6 * KW:6 * KW + IB].bitcast(i32)
        pad_rec = {"D": ringf[:, 0:4 * SL].bitcast(i32), "S": ringf[:, 4 * SL:8 * SL].bitcast(i32)} if RING * HID >= 8 * SL else None
        dxt3 = dxt[:, :].rearrange("p (s f) -> p s f", f=P)

        def big_view(n):
            return bigf[:, 0:T * n].rearrange("p (t f) -> p t f", t=T)

        def w_view(k, n):
            return weights[:, 0:k * n].rearrange("p (k n) -> p k n", k=k)

        def tiles(table):
            return table.rearrange("(t p) f -> p t f", p=P)

        def bc(ap, shape, at):
            return ap.unsqueeze(at).to_broadcast(shape)

        sem_sets = [[ctx.enter_context(nc.semaphore(f"stage{z}_{i}")) for i in range(16)] for z in range(2)]
        used_sems = []
        gathered = [ctx.enter_context(nc.semaphore(f"gathered{j}")) for j in range(NG)]
        scattered = [ctx.enter_context(nc.semaphore(f"scattered{z}")) for z in range(2)]
        before = {"gathered": 0, "scattered": 0}

        def stage(*names):
            k = len(used_sems)
            if k:
                for s in sem_sets[(k - 1) % 2][0:used_sems[-1]]:
                    nc.gpsimd.sem_clear(s)
            used_sems.append(len(names))
            st = ExitStack()
            block = st.enter_context(nc.Block())
            return st, block, sem_sets[k % 2][0:len(names)]


        def constants():
            st, block, (built, cleared, loaded, filled) = stage("built", "cleared", "loaded", "filled")
            with st:
                @block.gpsimd
                def _(pool):
                    pool.memset(ident[:, :], 0.0)
                    pool.memset(ones[:, :], 1.0)
                    pool.memset(lower[:, :], 1.0)
                    pool.memset(zeros[:, :], 0.0)
                    pool.iota(iota_free[:, :], [[1, P]], base=0, channel_multiplier=0,
                              allow_small_or_imprecise_dtypes=True)
                    pool.iota(iota_hi[:, :], [[1, T]], base=0, channel_multiplier=0,
                              allow_small_or_imprecise_dtypes=True)
                    pool.iota(iota_blk[:, :], [[1, NB]], base=0, channel_multiplier=0,
                              allow_small_or_imprecise_dtypes=True)
                    pool.iota(iota_part[:, :], [[0, 1]], base=0, channel_multiplier=1,
                              allow_small_or_imprecise_dtypes=True)
                    pool.iota(minus_part[:, :], [[0, 1]], base=0, channel_multiplier=-1,
                              allow_small_or_imprecise_dtypes=True)
                    pool.drain()
                    pool.affine_select(out=ident[:, :], in_=ident[:, :], compare_op=ALU.not_equal, fill=1.0, base=0,
                                       pattern=[[-1, P]], channel_multiplier=1)
                    pool.affine_select(out=lower[:, :], in_=lower[:, :], compare_op=ALU.is_gt, fill=0.0, base=0,
                                       pattern=[[1, P]], channel_multiplier=-1)
                    pool.drain().then_inc(built, 1)

                @block.vector
                def _(dve):
                    dve.memset(X[:, T - 1, :], 0.0)
                    dve.memset(hidf[:, 0:4 * KW], 0.0)
                    dve.memset(edge_raw, PADKEY)
                    for key, col in (("D", 1), ("S", 0)):
                        dve.memset(pad_rec[key], 0)
                    dve.drain()
                    for key, col in (("D", 1), ("S", 0)):
                        dve.memset(pad_rec[key].rearrange("p (s f) -> p s f", f=4)[:, :, col:col + 1], PADKEY)
                    dve.drain().then_inc(cleared, 1)
                    dve.wait_ge(built, 1)
                    dve.tensor_copy(identb[:, :], ident[:, :])

                @block.sync
                def _(sp):
                    sp.wait_ge(cleared, 1)
                    n = 0
                    for key in ("D", "S"):
                        sp.dma_start(lists[key][0:NSLOT, :].rearrange("(p b) f -> p (b f)", p=SP_),
                                     pad_rec[key][0:SP_, :]).then_inc(filled, 16)
                        sp.dma_start(lists[key][NSLOT:NSLOT + 2, :].rearrange("(p b) f -> p (b f)", p=1),
                                     pad_rec[key][0:1, 0:8]).then_inc(filled, 16)
                    sp.dma_start(X[:, 0:T - 1, :], A["x"][0:(T - 1) * P, :].rearrange("(t p) f -> p t f", p=P)
                                 ).then_inc(loaded, 16)
                    sp.dma_start(X[0:TAIL, T - 1, :], A["x"][(T - 1) * P:N, :]).then_inc(loaded, 16)
                    for i, name in enumerate(("src", "dst", "edge_type_3")):
                        sp.dma_start(edge_raw[0:ROWS_FULL, i, :],
                                     A[name][0:ROWS_FULL * IB].rearrange("(p b) -> p b", b=IB)).then_inc(loaded, 16)
                        sp.dma_start(edge_raw[ROWS_FULL:ROWS_FULL + 1, i, 0:ROW_TAIL],
                                     A[name][ROWS_FULL * IB:E].rearrange("(p b) -> p b", p=1)).then_inc(loaded, 16)
                    sp.wait_ge(loaded, 16 * 8)
                    sp.wait_ge(filled, 16 * 4)

        def store_load(stores, loads):
            st, block, (stored, loaded) = stage("stored", "loaded")
            with st:
                @block.sync
                def _(sp):
                    for dst, src in stores:
                        sp.dma_start(dst, src).then_inc(stored, 16)
                    for dst, src in loads:
                        sp.dma_start(dst, src).then_inc(loaded, 16)
                    if stores:
                        sp.wait_ge(stored, 16 * len(stores))
                    if loads:
                        sp.wait_ge(loaded, 16 * len(loads))

        def rowb(a, n):
            return a.rearrange("(o n) -> o n", o=1).to_broadcast([P, n])

        def split_keys():
            st, block, _ = stage()
            with st:
                @block.vector
                def _(dve):
                    for k in range(3):
                        dve.tensor_copy(rec_all[:, :, k:k + 1], edge_raw[:, k, :].unsqueeze(2))
                    dve.memset(rec_all[:, :, 3:4], 0)
                    for key, i in (("D", 1), ("S", 0)):
                        dve.drain()
                        dve.tensor_scalar(key_tmp, edge_raw[:, i, :], 7, None, ALU.arith_shift_right)
                        dve.drain()
                        dve.tensor_copy(key_hi[key], key_tmp)
                        dve.drain()
                        dve.tensor_scalar(key_tmp, edge_raw[:, i, :], P - 1, None, ALU.bitwise_and)
                        dve.drain()
                        dve.tensor_copy(key_lo[key], key_tmp)
                        dve.tensor_scalar(key_far[key], key_hi[key], float(T), FAR, ALU.is_ge, ALU.mult)

        def histogram(key):
            st, block, (masks, counted, kept, t_dve, t_pe, t_act) = stage(
                "masks", "counted", "kept", "tick_dve", "tick_pe", "tick_act")
            lob = onehot[:, :, :].rearrange("p a b -> p (a b)").bitcast(bf16).rearrange("p (a b) -> p a b", b=P)
            hib = rhs[:, 0:2, :].rearrange("p a b -> p (a b)").bitcast(bf16)
            lo2 = ringf[:, 0:SB * P].bitcast(bf16).rearrange("p (z a b) -> p z a b", z=2, b=P)
            hi2 = ringf[:, SB * P:SB * P + SB * T].bitcast(bf16).rearrange("p (z a b) -> p z a b", z=2, b=T)
            with st:
                @block.vector
                def _(dve):
                    dve.sem_inc(counted, 2)
                    with dve.Fori(0, IB // SB // 2, 1) as i:
                        for z in range(2):
                            dve.wait_ge(counted, 2 * i + z + 1)
                            dve.sem_inc(t_dve, 1)
                            b = i * (2 * SB) + z * SB
                            dve.tensor_tensor(lo2[:, z], bc(iota_free[:, :], [P, SB, P], 1),
                                              bc(key_lo[key][:, ds(b, SB)], [P, SB, P], 2), ALU.is_equal)
                            dve.tensor_tensor(hi2[:, z], bc(iota_hi[:, :], [P, SB, T], 1),
                                              bc(key_hi[key][:, ds(b, SB)], [P, SB, T], 2), ALU.is_equal)
                            dve.drain().then_inc(masks, 1)

                @block.tensor
                def _(pe):
                    pe.sem_inc(kept, 2)
                    with pe.Fori(0, IB // SB // 2, 1) as i:
                        for z in range(2):
                            pe.wait_ge(masks, 2 * i + z + 1)
                            pe.sem_inc(t_pe, 1)
                            pe.wait_ge(kept, 2 * i + z + 1)
                            pe.sem_inc(t_pe, 1)
                            for u in range(SB):
                                mm = pe.matmul(ps[:, z, u * T:u * T + T], lo2[:, z, u, :], hi2[:, z, u, :],
                                               start=True, stop=True)
                            mm.then_inc(counted, 1)

                @block.scalar
                def _(act):
                    with act.Fori(0, IB // SB // 2, 1) as i:
                        for z in range(2):
                            act.wait_ge(counted, 2 * i + z + 3)
                            act.sem_inc(t_act, 1)
                            b = i * (2 * SB) + z * SB + 1
                            act.activation(hist[:, ds(b, SB), :],
                                           ps[:, z, 0:SB * T].rearrange("p (b h) -> p b h", h=T), ACT.Copy)
                            act.drain().then_inc(kept, 1)

        def bases(key):
            st, block, (counted, summed) = stage("counted", "summed")
            cnt, tot, nblk, bend, bst, pre = (sm[:, i * 32:i * 32 + T] for i in range(6))
            nblk_i = sm[:, 192:192 + T].bitcast(i32)
            tidf = sm[0:1, 192:192 + NB]
            ones_row = dxt[:, 0:IB + 1]
            with st:
                @block.vector
                def _(dve):
                    dve.memset(ones_row, 1.0)
                    dve.tensor_reduce(cnt, hist[:, 1:, :].rearrange("p b h -> p h b"), AX, ALU.add)
                    dve.drain().then_inc(counted, 1)
                    dve.wait_ge(summed, 1)
                    if key == "D":
                        dve.tensor_copy(deg[:, :], cnt)
                    dve.tensor_copy(pre, ps[:, 1, 0:T])
                    dve.tensor_scalar(tot, ps[:, 0, 0:T], float(P - 1), None, ALU.add)
                    dve.drain()
                    dve.tensor_copy(nblk_i, tot)
                    dve.drain()
                    dve.tensor_scalar(nblk_i, nblk_i, 7, None, ALU.arith_shift_right)
                    dve.drain()
                    dve.tensor_copy(nblk, nblk_i)
                    dve.drain()
                    dve.tensor_tensor_scan(bend, ones[:, 0:T], nblk, 0.0, ALU.mult, ALU.add)
                    dve.drain()
                    dve.tensor_tensor(bst, bend, nblk, ALU.subtract)
                    dve.drain()
                    dve.tensor_scalar(bst, bst, float(P), 1.0, ALU.mult, ALU.add)
                    dve.drain()
                    dve.tensor_tensor(hist[:, 0, :], bst, pre, ALU.add)
                    dve.memset(tidf, 0.0)
                    dve.drain()
                    for h in range(T):
                        dve.tensor_tensor_scan(hist[:, :, h], ones_row, hist[:, :, h], 0.0, ALU.mult, ALU.add)
                        dve.scalar_tensor_tensor(tidf, iota_blk[0:1, :], bend[0:1, h:h + 1], tidf, ALU.is_ge, ALU.add)
                        dve.drain()
                    dve.tensor_scalar(tidf, tidf, float(T - 1), None, ALU.min)
                    dve.drain()
                    dve.tensor_copy(tid[key][:, :], tidf)
                    if key == "D":
                        over, offs = rhsf[0:1, 0:NB], rhsf[0:1, NB:2 * NB]
                        dve.tensor_scalar(over, tidf, float(SIDE_FIT), float(SIDE_BACK), ALU.is_ge, ALU.mult)
                        dve.tensor_scalar(offs, tidf, float(SIDE), float(7 * 512), ALU.mult, ALU.add)
                        dve.drain()
                        dve.tensor_tensor(offs, offs, over, ALU.subtract)
                        dve.drain()
                        dve.tensor_copy(tid_side[:, :], offs)

                @block.tensor
                def _(pe):
                    pe.wait_ge(counted, 1)
                    pe.matmul(ps[:, 0, 0:T], ones[:, :], cnt, start=True, stop=True)
                    pe.matmul(ps[:, 1, 0:T], lower[:, :], cnt, start=True, stop=True).then_inc(summed, 1)

        def place(key):
            (st, block, (masks, turned, turned_kept, gram_done, gram_kept, found, placed, written,
                         t_dve, t_pe, t_act, t_pool, t_sp)) = stage(
                "masks", "turned", "turned_kept", "gram_done", "gram_kept", "found", "placed", "written",
                 "tick_dve", "tick_pe", "tick_act", "tick_pool", "tick_sp")
            rows0 = before["scattered"]
            before["scattered"] += 16 * SB * (IB // SB // 2)
            low = ringf[:, 0:SB * P].bitcast(bf16).rearrange("p (z a b) -> p z a b", z=2, b=P)
            lowT = dxt[:, 0:SB * P].bitcast(bf16).rearrange("p (z a b) -> p z a b", z=2, b=P)
            gram = ringf[:, SB * P:SB * P + SB * P // 2].bitcast(bf16).rearrange("p (a b) -> p a b", b=P)
            high = rhsf[:, 0:SB * T].bitcast(bf16).rearrange("p (z a b) -> p z a b", z=2, b=T)
            sel = rhsf[:, SB * T:2 * SB * T].rearrange("p (a b) -> p a b", b=T)
            base = rhsf[:, 2 * SB * T:4 * SB * T].bitcast(bf16).rearrange("p (z k a b) -> p z k a b", z=2, k=2, b=T)
            posf = sm[:, 0:SB]
            steps = IB // SB

            def make_masks(dve, b, z):
                dve.tensor_tensor(low[:, z], bc(iota_free[:, :], [P, SB, P], 1),
                                  bc(key_lo_all[key][:, ds(b, SB)], [P, SB, P], 2), ALU.is_equal)
                dve.tensor_tensor(high[:, z], bc(iota_hi[:, :], [P, SB, T], 1),
                                  bc(key_hi_all[key][:, ds(b, SB)], [P, SB, T], 2), ALU.is_equal)
                dve.drain().then_inc(masks, 1)

            def split_bases(dve, b, z):
                dve.tensor_copy(base[:, z, 0], hist[:, ds(b, SB), :])
                dve.drain()
                dve.tensor_tensor(base[:, z, 1], hist[:, ds(b, SB), :], base[:, z, 0], ALU.subtract)

            def turn(pe, z):
                for u in range(SB):
                    mm = pe.matmul(psf[:, u * P:u * P + P], low[:, z, u, :], identb[:, :], start=True, stop=True)
                mm.then_inc(turned, 1)

            def agree(pe, z):
                for u in range(SB):
                    mm = pe.matmul(psf[:, 1024 + u * P:1024 + u * P + P], lowT[:, z, u, :], lowT[:, z, u, :],
                                   start=True, stop=True)
                mm.then_inc(gram_done, 1)

            with st:
                @block.vector
                def _(dve):
                    make_masks(dve, 0, 0)
                    with dve.Fori(0, steps // 2, 1) as i:
                        for z in range(2):
                            b = i * (2 * SB) + z * SB
                            n = 2 * i + z
                            make_masks(dve, b + SB, 1 - z)
                            split_bases(dve, b, z)
                            dve.wait_ge(gram_done, n + 1)
                            dve.sem_inc(t_dve, 1)
                            dve.tensor_tensor(gram[:, :, :],
                                              psf[:, 1024:1024 + SB * P].rearrange("p (a b) -> p a b", b=P),
                                              bc(lower[:, :], [P, SB, P], 1), ALU.mult)
                            dve.drain().then_inc(gram_kept, 1)
                            dve.wait_ge(found, n + 1)
                            dve.sem_inc(t_dve, 1)
                            dve.tensor_tensor(sel, ps[:, 4, 0:SB * T].rearrange("p (a b) -> p a b", b=T), high[:, z],
                                              ALU.mult)
                            dve.drain()
                            dve.tensor_reduce(posf, sel, AX, ALU.add)
                            dve.drain()
                            dve.wait_ge(written, n + 1)
                            dve.sem_inc(t_dve, 1)
                            dve.tensor_tensor(posidx[:, z, :], posf, key_far[key][:, ds(b, SB)], ALU.add)
                            dve.tensor_copy(recst[:, z], rec_all[:, ds(b, SB), :])
                            dve.drain().then_inc(placed, 1)

                @block.tensor
                def _(pe):
                    pe.wait_ge(masks, 1)
                    turn(pe, 0)
                    pe.wait_ge(turned_kept, 1)
                    agree(pe, 0)
                    with pe.Fori(0, steps // 2, 1) as i:
                        for z in range(2):
                            n = 2 * i + z
                            pe.wait_ge(masks, n + 2)
                            pe.sem_inc(t_pe, 1)
                            turn(pe, 1 - z)
                            pe.wait_ge(gram_kept, n + 1)
                            pe.sem_inc(t_pe, 1)
                            for u in range(SB):
                                o = ps[:, 4, u * T:u * T + T]
                                pe.matmul(o, lowT[:, z, u, :], base[:, z, 0, u, :], start=True, stop=False)
                                pe.matmul(o, lowT[:, z, u, :], base[:, z, 1, u, :], start=False, stop=False)
                                mm = pe.matmul(o, gram[:, u, :], high[:, z, u, :], start=False, stop=True)
                            mm.then_inc(found, 1)
                            pe.wait_ge(turned_kept, n + 2)
                            pe.sem_inc(t_pe, 1)
                            agree(pe, 1 - z)

                @block.scalar
                def _(act):
                    def keep(z):
                        act.activation(lowT[:, z], psf[:, 0:SB * P].rearrange("p (a b) -> p a b", b=P), ACT.Copy)
                        act.drain().then_inc(turned_kept, 1)
                    act.wait_ge(turned, 1)
                    keep(0)
                    with act.Fori(0, steps // 2, 1) as i:
                        for z in range(2):
                            act.wait_ge(turned, 2 * i + z + 2)
                            act.sem_inc(t_act, 1)
                            keep(1 - z)

                @block.gpsimd
                def _(pool):
                    with pool.Fori(0, IB // SB // 2, 1) as i:
                        for z in range(2):
                            pool.wait_ge(placed, 2 * i + z + 1)
                            pool.sem_inc(t_pool, 1)
                            for u in range(SB):
                                pool.indirect_dma_start(
                                    lists[key][:, :], bass.IndirectOffsetOnAxis(posidx[:, z, u:u + 1], 0),
                                    recst[:, z, u, :], None, bounds_check=NSLOT + 1, oob_is_err=False
                                ).then_inc(scattered[z], 16)

                @block.sync
                def _(sp):
                    sp.sem_inc(written, 2)
                    with sp.Fori(0, IB // SB // 2, 1) as i:
                        for z in range(2):
                            sp.wait_ge(scattered[z], i * (16 * SB) + (rows0 + 16 * SB))
                            sp.sem_inc(t_sp, 1)
                            sp.sem_inc(written, 1)

        def load_list(key):
            st, block, (loaded, conv, turned, kept) = stage("loaded", "converted", "turned", "kept")
            rec = ringf[0:SP_, 0:4 * SL].bitcast(i32).rearrange("p (s f) -> p s f", f=4)
            prev = ringf[0:SP_, 4 * SL:8 * SL].bitcast(i32).rearrange("p (s f) -> p s f", f=4)
            nxt = hidf[0:SP_, 0:4 * SL].bitcast(i32).rearrange("p (s f) -> p s f", f=4)
            fld = bigf[0:SP_, 0:3 * SL].rearrange("p (k s) -> p k s", k=3)
            tmp = bigf[:, 3 * SL:3 * SL + 6 * NB].rearrange("p (k b) -> p k b", k=6)
            tmp_i = tmp.bitcast(i32)
            own, other = (1, 0) if key == "D" else (0, 1)
            with st:
                @block.sync
                def _(sp):
                    n = 0
                    views = [(rec, 1)] + ([(prev, 0), (nxt, 2)] if key == "D" else [])
                    for dst, first in views:
                        sp.dma_start(dst, lists[key][first:first + NSLOT, :].rearrange("(p s) f -> p s f", p=SP_)
                                     ).then_inc(loaded, 16)
                    sp.wait_ge(loaded, 16 * len(views))

                @block.vector
                def _(dve):
                    dve.wait_ge(loaded, 48 if key == "D" else 16)
                    for k in range(3):
                        dve.tensor_copy(fld[:, k, :].unsqueeze(2), rec[:, :, k:k + 1])
                    dve.drain().then_inc(conv, 1)
                    if key == "D":
                        dve.tensor_copy(typ_s[:, :], fld[:, 2, :])
                        dve.tensor_copy(cont[:, :].unsqueeze(2), prev[:, :, 1:2])
                        dve.tensor_copy(isend[:, :].unsqueeze(2), nxt[:, :, 1:2])
                        dve.drain()
                        dve.tensor_tensor(cont[:, :], cont[:, :], fld[:, 1, :], ALU.not_equal)
                        dve.tensor_tensor(isend[:, :], isend[:, :], fld[:, 1, :], ALU.not_equal)
                        dve.drain()
                        dve.tensor_scalar(cont[:, :], cont[:, :], -BIG, None, ALU.mult)
                    dve.wait_ge(turned, 1)
                    for k in range(3):
                        dve.tensor_copy(tmp[:, k, :].rearrange("p (q c) -> p c q", c=4),
                                        ps[:, k, 0:NB].rearrange("p (c q) -> p c q", c=4))
                    dve.drain()
                    for side in (own, other):
                        dve.tensor_copy(tmp_i[:, 3, :], tmp[:, side, :])
                        dve.drain()
                        dve.tensor_scalar(tmp_i[:, 4, :], tmp_i[:, 3, :], 7, None, ALU.arith_shift_right)
                        dve.tensor_scalar(tmp_i[:, 5, :], tmp_i[:, 3, :], P - 1, None, ALU.bitwise_and)
                        dve.drain()
                        if side == other:
                            dve.tensor_copy(hi_other[key][:, :], tmp_i[:, 4, :])
                        else:
                            dve.tensor_copy(lo[key][:, :], tmp_i[:, 5, :])
                            dve.drain()
                            dve.tensor_scalar(tmp[:, 5, :], tmp[:, own, :], float(NP), 1000.0, ALU.is_ge, ALU.mult)
                            dve.drain()
                            dve.tensor_tensor(lo[key][:, :], lo[key][:, :], tmp[:, 5, :], ALU.add)
                        dve.drain()
                    for side, rows in ((own, rows_own[key]), (other, rows_other[key])):
                        sc, sc_i = dxt[0:SP_, 0:SL], dxt[0:SP_, SL:2 * SL].bitcast(i32)
                        dve.tensor_copy(sc_i, fld[:, side, :])
                        dve.tensor_scalar(sc, fld[:, side, :], float(NP), 1000.0, ALU.is_ge, ALU.mult)
                        dve.drain()
                        dve.tensor_scalar(sc_i, sc_i, P - 1, None, ALU.bitwise_and)
                        dve.drain()
                        dve.tensor_tensor(rows[:, :], sc, sc_i, ALU.add)
                        dve.drain()
                    if key == "D":
                        dve.tensor_copy(idx["Dsrc"][:, :], tmp[:, 0, :])
                        dve.tensor_copy(typ[:, :], tmp[:, 2, :])
                        dve.scalar_tensor_tensor(idx["DsrcT"][:, :], tmp[:, 2, :], float(NP), tmp[:, 0, :],
                                                 ALU.mult, ALU.add)
                    else:
                        dve.tensor_scalar(tmp[:, 1, :], tmp[:, 1, :], float(NP - 1), None, ALU.min)
                        dve.drain()
                        dve.tensor_copy(idx["Sdst"][:, :], tmp[:, 1, :])

                @block.tensor
                def _(pe):
                    pe.wait_ge(conv, 1)
                    for k in range(3):
                        for c in range(4):
                            mm = pe.transpose(ps[:, k, c * SP_:(c + 1) * SP_], fld[:, k, c * P:(c + 1) * P],
                                              ident[0:SP_, 0:SP_])
                    mm.then_inc(turned, 1)

        def gather_issue(act, pool_idx, used, staged, tick):
            with act.Fori(0, TURNS, 1) as i:
                for j in range(NG):
                    act.wait_ge(used, i * NG + j + 1)
                    act.sem_inc(tick, 1)
                    act.activation(idx_stage[:, j * GB:(j + 1) * GB], pool_idx[:, ds(i * RING + j * GB, GB)], ACT.Copy)
                    act.drain().then_inc(staged, 1)

        def gather_rows(pool, table, width, staged, gathered, tick):
            with pool.Fori(0, TURNS, 1) as i:
                for j in range(NG):
                    pool.wait_ge(staged, i * NG + j + 1)
                    pool.sem_inc(tick, 1)
                    for u in range(GB):
                        s = j * GB + u
                        pool.indirect_dma_start(ring[:, s, 0:width], None, table,
                                                bass.IndirectOffsetOnAxis(idx_stage[:, s:s + 1], 0)
                                                ).then_inc(gathered[j], 16)

        def block_tiles(pe, key, i):
            _, t = nc.values_load_multi_w_load_instructions(
                tid[key][0:1, ds(i * RING, RING)], engines=(mybir.EngineType.PE,), min_val=0, max_val=T - 1,
                skip_runtime_bounds_check_because="bases() clamps the tiles to 0..T-1")
            return t

        def parts_view(at, rows, n):
            return bigf[:, at:at + (3 * rows * n + 1) // 2].bitcast(bf16)[:, 0:3 * rows * n].rearrange(
                "p (k t n) -> p k t n", k=3, t=rows)

        def split_rows(dve, src, parts, rest):
            n = src.shape[2]
            rest = rest[:, :, 0:n]
            dve.drain()
            dve.tensor_copy(parts[:, 0], src)
            dve.drain()
            dve.tensor_tensor(rest, src, parts[:, 0], ALU.subtract)
            dve.drain()
            dve.tensor_copy(parts[:, 1], rest)
            dve.drain()
            dve.tensor_tensor(parts[:, 2], rest, parts[:, 1], ALU.subtract)
            dve.drain()

        def node_fetch(key, own, own_dest, other=None, other_dest=None, table=None, index=None):
            (st, block, (own_row, own_mask, own_res, other_row, other_mask, other_res, used, staged, other_taken,
                         parts_ready, t_pe, t_dve, t_act, t_pool)) = stage(
                "own_row", "own_mask", "own_result", "other_row", "other_mask", "other_result", "used", "staged",
                "other_taken", "parts_ready", "tick_pe", "tick_dve", "tick_act", "tick_pool")
            no, nx = own.shape[2], (other.shape[2] if other is not None else 0)
            om = dxt[:, 0:SL].bitcast(bf16).rearrange("p (z b f) -> p z b f", z=2, b=GB)
            xm = dxt[:, SL:2 * SL].bitcast(bf16).rearrange("p (z b f) -> p z b f", z=2, b=GB)
            own3 = parts_view(0, T, no)
            other3 = parts_view(T * no * 3 // 2 + 8, T, nx) if nx else None
            rest = bigf[:, 4096:4096 + T * max(no, nx)].rearrange("p (t k) -> p t k", t=T)
            sq = dxt[:, 4 * SL:5 * SL]
            pick = rhsf[:, 0:GB * T].rearrange("p (b h) -> p b h", b=GB)
            prod = rhsf[:, GB * T:GB * T + GB * T * HEADS]
            rows0 = before["gathered"]
            if table is not None:
                before["gathered"] += 16 * GB * TURNS

            with st:
                @block.tensor
                def _(pe):
                    def spread(q, z):
                        pick_q = identb[0:SP_, ds(q, 1)].to_broadcast([SP_, P])
                        pe.matmul(ps[:, z, :], pick_q, rows_own[key][:, :], start=True, stop=True).then_inc(own_row, 1)
                        if other is not None:
                            pe.matmul(ps[:, 2 + z, :], pick_q, rows_other[key][:, :], start=True, stop=True
                                      ).then_inc(other_row, 1)
                    spread(0, 0)
                    pe.wait_ge(parts_ready, 1)
                    with pe.Fori(0, TURNS, 1) as i:
                        t = block_tiles(pe, key, i)
                        for j in range(NG):
                            z, n = j % 2, i * NG + j
                            spread(n + 1, 1 - z)
                            if other is not None:
                                pe.wait_ge(other_mask, n + 1)
                                pe.sem_inc(t_pe, 1)
                                for u in range(GB):
                                    for k in range(3):
                                        mm = pe.matmul(ps[:, 4 + z, u * T * nx:(u + 1) * T * nx], xm[:, z, u, :],
                                                       other3[:, k], start=k == 0, stop=k == 2)
                                mm.then_inc(other_res, 1)
                            pe.wait_ge(own_mask, n + 1)
                            pe.sem_inc(t_pe, 1)
                            if table is not None:
                                pe.wait_ge(other_taken, n + 1)
                                pe.sem_inc(t_pe, 1)
                            for u in range(GB):
                                for k in range(3):
                                    mm = pe.matmul(ps[:, 6 + z, u * no:(u + 1) * no], om[:, z, u, :],
                                                   own3[:, k, ds(t[j * GB + u], 1), :], start=k == 0, stop=k == 2)
                            mm.then_inc(own_res, 1)

                @block.scalar
                def _(act):
                    def mask(z, k):
                        act.wait_ge(own_row, k)
                        act.sem_inc(t_act, 1)
                        act.activation(sq, ps[:, z, :], ACT.Square, bias=minus_part[:, 0:1])
                        act.drain()
                        act.activation(om[:, z].rearrange("p b f -> p (b f)"), sq, ACT.Relu, bias=ones[:, 0:1], scale=-1.0)
                        act.drain().then_inc(own_mask, 1)
                    mask(0, 1)
                    with act.Fori(0, TURNS, 1) as i:
                        for j in range(NG):
                            z, n = j % 2, i * NG + j
                            if table is not None:
                                act.wait_ge(used, n + 1)
                                act.sem_inc(t_act, 1)
                                act.activation(idx_stage[:, j * GB:(j + 1) * GB], index[:, ds(i * RING + j * GB, GB)],
                                               ACT.Copy)
                                act.drain().then_inc(staged, 1)
                            mask(1 - z, n + 2)
                            if table is None:
                                act.wait_ge(own_res, n + 1)
                                act.sem_inc(t_act, 1)
                                act.activation(own_dest[:, ds(i * RING + j * GB, GB), :],
                                               ps[:, 6 + z, 0:GB * no].rearrange("p (b k) -> p b k", b=GB), ACT.Copy)
                                act.drain()

                if table is not None:
                    @block.gpsimd
                    def _(pool):
                        gather_rows(pool, table, HEADS, staged, gathered, t_pool)

                @block.vector
                def _(dve):
                    def mask(z, k):
                        dve.wait_ge(other_row, k)
                        dve.sem_inc(t_dve, 1)
                        dve.tensor_scalar(xm[:, z].rearrange("p b f -> p (b f)"), ps[:, 2 + z, :], iota_part[:, 0:1],
                                          None, ALU.is_equal)
                        dve.drain().then_inc(other_mask, 1)

                    split_rows(dve, own, own3, rest)
                    if other is not None:
                        split_rows(dve, other, other3, rest)
                    dve.drain().then_inc(parts_ready, 1)
                    if other is not None:
                        mask(0, 1)
                    else:
                        dve.sem_inc(used, NG)
                        dve.sem_inc(other_taken, 2)
                    with dve.Fori(0, TURNS, 1) as i:
                        for j in range(NG):
                            z, n, b = j % 2, i * NG + j, i * RING + j * GB
                            if other is not None:
                                mask(1 - z, n + 2)
                                dve.tensor_tensor(pick, bc(iota_hi[:, :], [P, GB, T], 1),
                                                  bc(hi_other[key][:, ds(b, GB)], [P, GB, T], 2), ALU.is_equal)
                                dve.drain()
                                dve.wait_ge(other_res, n + 1)
                                dve.sem_inc(t_dve, 1)
                                pr = prod[:, 0:GB * T * nx].rearrange("p (b h k) -> p b h k", b=GB, k=nx)
                                dve.tensor_tensor(pr, ps[:, 4 + z, 0:GB * T * nx].rearrange("p (b h k) -> p b h k", b=GB, k=nx),
                                                  bc(pick, [P, GB, T, nx], 3), ALU.mult)
                                dve.drain()
                                dve.tensor_reduce(other_dest[:, ds(b, GB), :], pr.rearrange("p b h k -> p b k h"), AX, ALU.add)
                            else:
                                dve.wait_ge(gathered[j], i * (16 * GB) + (rows0 + 16 * GB))
                                dve.sem_inc(t_dve, 1)
                                dve.tensor_copy(other_dest[:, ds(b, GB), :], ring[:, j * GB:(j + 1) * GB, 0:HEADS])
                                dve.drain().then_inc(used, 1)
                                rel = rhsf[:, 0:GB * NREL].rearrange("p (b r) -> p b r", b=GB)
                                dve.tensor_tensor(rel, bc(iota_hi[:, 0:NREL], [P, GB, NREL], 1),
                                                  bc(typ[:, ds(b, GB)], [P, GB, NREL], 2), ALU.is_equal)
                                dve.drain()
                                dve.wait_ge(own_res, n + 1)
                                dve.sem_inc(t_dve, 1)
                                m = no // NREL
                                pr = prod[:, 0:GB * no].rearrange("p (b k r) -> p b k r", b=GB, r=NREL)
                                dve.tensor_tensor(pr, ps[:, 6 + z, 0:GB * no].rearrange("p (b k r) -> p b k r", b=GB, r=NREL),
                                                  bc(rel, [P, GB, m, NREL], 2), ALU.mult)
                                dve.drain()
                                dve.tensor_reduce(own_dest[:, ds(b, GB), :], pr, AX, ALU.add)
                                dve.drain().then_inc(other_taken, 1)

        def weighted(dve, o, rows, w, heads):
            c = F // heads
            if heads == 1:
                dve.tensor_tensor(o, rows, w.to_broadcast([P, GB, F]), ALU.mult)
            else:
                dve.tensor_tensor(o.rearrange("p b (h c) -> p b h c", c=c), rows.rearrange("p b (h c) -> p b h c", c=c),
                                  bc(w, [P, GB, heads, c], 3), ALU.mult)

        def edge_pass(key, table=None, index=None, payload=None, heads=0, sides=()):
            st, block, (used, staged, ready, t_act, t_pool, t_dve, t_pe) = stage(
                "summed", "staged", "operands", "tick_act", "tick_pool", "tick_dve", "tick_pe")
            nf = F if table is not None else 0
            ns = sum(v.shape[2] for v in sides)
            n = nf + ns
            rows0 = before["gathered"]
            if table is not None:
                before["gathered"] += 16 * GB * TURNS
            acc = big_view(n)
            row_sums = psf[:, 0:T * F].rearrange("p (t f) -> p t f", f=F)
            spilled = T * ns > 512
            if ns:
                side_sums = ps[:, 7, 0:min(T, 512 // ns) * ns].rearrange("p (t f) -> p t f", f=ns)
            banks = (list(range(7)) if nf else []) + ([7] if ns else [])
            with st:
                if table is not None:
                    @block.scalar
                    def _(act):
                        gather_issue(act, index, used, staged, t_act)

                    @block.gpsimd
                    def _(pool):
                        gather_rows(pool, table, F, staged, gathered, t_pool)

                @block.vector
                def _(dve):
                    dve.sem_inc(used, NG)
                    with dve.Fori(0, TURNS, 1) as i:
                        for j in range(NG):
                            b, z = i * RING + j * GB, j % 2
                            dve.wait_ge(used, i * NG + j + NG - 1)
                            dve.sem_inc(t_dve, 1)
                            dve.tensor_tensor(onehot2[:, z], bc(iota_free[:, :], [P, GB, P], 1),
                                              bc(lo[key][:, ds(b, GB)], [P, GB, P], 2), ALU.is_equal)
                            at = nf
                            for more in sides:
                                k = more.shape[2]
                                dve.tensor_copy(rhs2[:, z, :, at:at + k], more[:, ds(b, GB), :])
                                at += k
                            if heads:
                                dve.wait_ge(gathered[j], i * (16 * GB) + (rows0 + 16 * GB))
                                dve.sem_inc(t_dve, 1)
                                weighted(dve, rhs2[:, z, :, 0:F], ring[:, j * GB:(j + 1) * GB, 0:F],
                                         payload[:, ds(b, GB), 0:heads], heads)
                            dve.drain().then_inc(ready, 1)
                    dve.wait_ge(used, NG * TURNS + NG + 1)
                    if nf:
                        dve.tensor_copy(acc[:, :, 0:F], row_sums)
                    if ns:
                        k = side_sums.shape[1]
                        dve.tensor_copy(acc[:, 0:k, nf:n], side_sums)
                        if spilled:
                            dve.tensor_copy(acc[:, k:T, nf:n],
                                            psf[:, T * F:T * F + (T - k) * ns].rearrange("p (t f) -> p t f", f=ns))

                @block.tensor
                def _(pe):
                    for k in banks:
                        pe.matmul(ps[:, k, :], zeros[:, 0:P], zeros[:, :], start=True, stop=False)
                    with pe.Fori(0, TURNS, 1) as i:
                        t = block_tiles(pe, key, i)
                        if spilled:
                            _, side = nc.values_load_multi_w_load_instructions(
                                tid_side[0:1, ds(i * RING, RING)], engines=(mybir.EngineType.PE,), min_val=T * F,
                                max_val=8 * 512 - SIDE, skip_runtime_bounds_check_because="bases() makes them from tiles 0..T-1")
                        for j in range(NG):
                            pe.wait_ge(ready, i * NG + j + 1)
                            pe.sem_inc(t_pe, 1)
                            if table is not None and not heads:
                                pe.wait_ge(gathered[j], i * (16 * GB) + (rows0 + 16 * GB))
                                pe.sem_inc(t_pe, 1)
                            for u in range(GB):
                                m, at = onehot2[:, j % 2, u, :], t[j * GB + u]
                                if nf:
                                    r = rhs2[:, j % 2, u, 0:F] if heads else ring[:, j * GB + u, 0:F]
                                    mm = pe.matmul(row_sums[:, ds(at, 1), :], m, r, start=False, stop=False,
                                                   skip_group_check=True)
                                if ns:
                                    o = psf[:, ds(side[j * GB + u], SIDE)] if spilled else side_sums[:, ds(at, 1), :]
                                    mm = pe.matmul(o, m, rhs2[:, j % 2, u, nf:n],
                                                   start=False, stop=False, skip_group_check=True)
                            mm.then_inc(used, 1)
                    for k in banks:
                        mm = pe.matmul(ps[:, k, :], zeros[:, 0:P], zeros[:, :], start=False, stop=True)
                    mm.then_inc(used, 1)

        def side_pass(key, values):
            st, block, (used, ready, parts_ready, t_dve, t_pe) = stage(
                "summed", "operands", "parts_ready", "tick_dve", "tick_pe")
            n = values.shape[2]
            acc = big_view(n)
            at, size = T * n, (3 * NB * n + 1) // 2
            parts = bigf[:, at:at + size].bitcast(bf16)[:, 0:3 * NB * n].rearrange("p (b k n) -> p b k n", k=3, n=n)
            rest = bigf[:, at + size:at + size + NB * n].rearrange("p (b n) -> p b n", n=n)
            onehots = onehot2[:, :, :, :].rearrange("p z a b -> p (z a b)").bitcast(bf16).rearrange(
                "p (z a b) -> p z a b", z=4, b=P)
            sums = ps[:, 7, 0:T * 3 * n].rearrange("p (t k n) -> p t k n", k=3, n=n)
            with st:
                @block.vector
                def _(dve):
                    dve.sem_inc(used, NG)
                    split_rows(dve, values, parts.rearrange("p b k n -> p k b n"), rest)
                    dve.drain().then_inc(parts_ready, 1)
                    with dve.Fori(0, TURNS, 1) as i:
                        for j in range(NG):
                            dve.wait_ge(used, i * NG + j + 1)
                            dve.sem_inc(t_dve, 1)
                            dve.tensor_tensor(onehots[:, j], bc(iota_free[:, :], [P, GB, P], 1),
                                              bc(lo[key][:, ds(i * RING + j * GB, GB)], [P, GB, P], 2), ALU.is_equal)
                            dve.drain().then_inc(ready, 1)
                    dve.wait_ge(used, NG * TURNS + NG + 1)
                    dve.tensor_copy(acc, sums[:, :, 0])
                    for k in (1, 2):
                        dve.drain()
                        dve.tensor_tensor(acc, acc, sums[:, :, k], ALU.add)

                @block.tensor
                def _(pe):
                    pe.matmul(ps[:, 7, :], zeros[:, 0:P], zeros[:, :], start=True, stop=False)
                    pe.wait_ge(parts_ready, 1)
                    with pe.Fori(0, TURNS, 1) as i:
                        t = block_tiles(pe, key, i)
                        for j in range(NG):
                            pe.wait_ge(ready, i * NG + j + 1)
                            pe.sem_inc(t_pe, 1)
                            for u in range(GB):
                                mm = pe.matmul(sums[:, ds(t[j * GB + u], 1)], onehots[:, j, u, :],
                                               parts[:, ds(i * RING + j * GB + u, 1)],
                                               start=False, stop=False, skip_group_check=True)
                            mm.then_inc(used, 1)
                    pe.matmul(ps[:, 7, :], zeros[:, 0:P], zeros[:, :], start=False, stop=True).then_inc(used, 1)

        def wide_pass(key, n, table, index):
            st, block, (used, staged, ready, added, t_act, t_pool, t_dve, t_pe) = stage(
                "summed", "staged", "operands", "added", "tick_act", "tick_pool", "tick_dve", "tick_pe")
            rows0 = before["gathered"]
            before["gathered"] += 16 * GB * TURNS
            acc = big_view(n)
            with st:
                @block.scalar
                def _(act):
                    gather_issue(act, index, used, staged, t_act)

                @block.gpsimd
                def _(pool):
                    gather_rows(pool, table, n, staged, gathered, t_pool)

                @block.vector
                def _(dve):
                    dve.sem_inc(used, NG)
                    dve.memset(acc, 0.0)
                    with dve.Fori(0, TURNS, 1) as i:
                        _, t = nc.values_load_multi_w_load_instructions(
                            tid[key][0:1, ds(i * RING, RING)], engines=(mybir.EngineType.DVE,), min_val=0,
                            max_val=T - 1, skip_runtime_bounds_check_because="bases() clamps the tiles to 0..T-1")
                        for j in range(-2, NG):
                            if j >= 0:
                                dve.wait_ge(used, i * NG + j + NG + 1)
                                dve.sem_inc(t_dve, 1)
                                for u in range(GB):
                                    at = acc[:, ds(t[j * GB + u], 1), :]
                                    dve.tensor_tensor(at, at, ps[:, j % 2 * 4 + u:j % 2 * 4 + u + 1, 0:n], ALU.add)
                                    dve.drain()
                            if j + 2 < NG:
                                dve.tensor_tensor(onehot2[:, j % 2], bc(iota_free[:, :], [P, GB, P], 1),
                                                  bc(lo[key][:, ds(i * RING + (j + 2) * GB, GB)], [P, GB, P], 2),
                                                  ALU.is_equal)
                                dve.drain().then_inc(ready, 1)

                @block.tensor
                def _(pe):
                    with pe.Fori(0, TURNS, 1) as i:
                        for j in range(NG):
                            pe.wait_ge(ready, i * NG + j + 1)
                            pe.sem_inc(t_pe, 1)
                            pe.wait_ge(gathered[j], i * (16 * GB) + (rows0 + 16 * GB))
                            pe.sem_inc(t_pe, 1)
                            for u in range(GB):
                                mm = pe.matmul(ps[:, j % 2 * 4 + u, 0:n], onehot2[:, j % 2, u, :], ring[:, j * GB + u, 0:n],
                                               start=True, stop=True)
                            mm.then_inc(used, 1)

        def dense(sources, n, dest, bias=None, add=False):
            chunks = sum(k for _, k, _ in sources)
            wv = w_view(chunks, n)
            din = ringf[:, 0:DT * chunks * P].rearrange("p (t f) -> p t f", t=DT)
            first = 2 if n > 256 else 5
            step = 512 if n > 256 else 256
            outs = psf[:, first * 512:first * 512 + (DT - 1) * step + n]
            ov = psf[:, first * 512:min(first * 512 + DT * step, 4096)].rearrange("p (t f) -> p t f", f=step)[:, :, 0:n]
            st, block, (staged, turned, turned_kept, done, taken, t_dve, t_pe, t_act) = stage(
                "staged", "turned", "turned_kept", "done", "taken", "tick_dve", "tick_pe", "tick_act")
            with st:
                @block.vector
                def _(dve):
                    with dve.Fori(0, T // DT, 1) as q:
                        dve.drain()
                        c = 0
                        for view, k, scaled in sources:
                            for m in range(k):
                                o = din[:, :, (c + m) * P:(c + m + 1) * P]
                                i = view[:, ds(q * DT, DT), m * P:(m + 1) * P]
                                if scaled:
                                    dve.tensor_tensor(o, i, bc(deg[:, ds(q * DT, DT)], [P, DT, P], 2), ALU.mult)
                                else:
                                    dve.tensor_copy(o, i)
                            c += k
                        dve.drain().then_inc(staged, 1)
                        dve.wait_ge(done, q + 1)
                        dve.sem_inc(t_dve, 1)
                        d = dest[:, ds(q * DT, DT), :]
                        if bias is not None:
                            dve.tensor_tensor(d, ov, bc(bias, [P, DT, n], 1), ALU.add)
                        elif add:
                            dve.tensor_tensor(d, d, ov, ALU.add)
                        else:
                            dve.tensor_copy(d, ov)

                @block.tensor
                def _(pe):
                    with pe.Fori(0, T // DT, 1) as q:
                        pe.wait_ge(staged, q + 1)
                        pe.sem_inc(t_pe, 1)
                        for c in range(chunks):
                            for k in range(DT):
                                mm = pe.transpose(psf[:, (c * DT + k) * P:(c * DT + k + 1) * P],
                                                  din[:, k, c * P:(c + 1) * P], ident[:, :])
                        mm.then_inc(turned, 1)
                        pe.wait_ge(turned_kept, q + 1)
                        pe.sem_inc(t_pe, 1)
                        for k in range(DT):
                            o = psf[:, first * 512 + k * step:first * 512 + k * step + n]
                            for c in range(chunks):
                                mm = pe.matmul(o, dxt3[:, c * DT + k, :], wv[:, c, :], start=c == 0, stop=c == chunks - 1)
                        mm.then_inc(done, 1)

                @block.scalar
                def _(act):
                    with act.Fori(0, T // DT, 1) as q:
                        act.wait_ge(turned, q + 1)
                        act.sem_inc(t_act, 1)
                        act.activation(dxt[:, 0:chunks * DT * P], psf[:, 0:chunks * DT * P], ACT.Copy)
                        act.drain().then_inc(turned_kept, 1)

        def norm_dve(dve, Y, n, scratch, var_ready, std_ready, k, gamma=None, beta=None):
            mean, var = sm[:, 0:T], sm[:, 32:32 + T]
            full = [P, T, n]
            dve.drain()
            dve.tensor_reduce(mean, Y, AX, ALU.add)
            dve.drain()
            dve.tensor_scalar(mean, mean, 1.0 / n, None, ALU.mult)
            dve.drain()
            dve.tensor_tensor(Y, Y, bc(mean, full, 2), ALU.subtract)
            dve.drain()
            dve.tensor_tensor(scratch, Y, Y, ALU.mult)
            dve.drain()
            dve.tensor_reduce(var, scratch, AX, ALU.add)
            dve.drain()
            dve.tensor_scalar(var, var, 1.0 / n, EPS, ALU.mult, ALU.add)
            dve.drain().then_inc(var_ready, 1)
            dve.wait_ge(std_ready, k)
            dve.reciprocal(var, var)
            dve.drain()
            dve.tensor_tensor(Y, Y, bc(var, full, 2), ALU.mult)
            dve.drain()
            if gamma is not None:
                dve.tensor_tensor(Y, Y, bc(gamma, full, 1), ALU.mult)
                dve.drain()
                dve.tensor_tensor(Y, Y, bc(beta, full, 1), ALU.add)
                dve.drain()
                dve.tensor_scalar(Y, Y, 0.0, None, ALU.max)

        def norm(Y, n, scratch, gamma=None, beta=None, before=None):
            st, block, (var_ready, std_ready) = stage("var_ready", "std_ready")
            with st:
                @block.vector
                def _(dve):
                    if before:
                        before(dve)
                    norm_dve(dve, Y, n, scratch, var_ready, std_ready, 1, gamma, beta)

                @block.scalar
                def _(act):
                    act.wait_ge(var_ready, 1)
                    act.activation(sm[:, 32:32 + T], sm[:, 32:32 + T], ACT.Sqrt)
                    act.drain().then_inc(std_ready, 1)

        def dve_stage(body):
            st, block, _ = stage()
            with st:
                @block.vector
                def _(dve):
                    body(dve)

        def segment_totals(op, K, rels, values, total=None, ends=None):
            st, block, (turned, tails, tails_up, carry, carry_up, done, back, taken) = stage(
                "turned", "tails", "tails_turned", "carry", "carry_turned", "results", "back", "taken")
            big3 = bigf[0:SP_, 0:5 * K * SL].rearrange("p (a k s) -> p a k s", a=5, k=K)
            V, RF, RB, TS, U = (big3[:, a] for a in range(5))
            mask = rhsf[0:SP_, 0:SL]
            maskb = rhsf[0:SP_, SL:2 * SL]
            oh = onehot2[0:SP_, :, :, :].rearrange("p z a b -> p (z a b)")
            near = [oh[:, 0:SL], oh[:, SL:2 * SL]]
            gates = ringf[0:SP_, 0:2 * SL].rearrange("p (z s) -> p z s", z=2)
            tail = sm[0:SP_, 8:8 + 4 * K].rearrange("p (z k) -> p z k", z=4)
            rows = sm[0:K, 32:32 + 4 * SP_].rearrange("p (z s) -> p z s", z=4)
            crow = ringf[0:K, 2 * SL:2 * SL + 2 * (SP_ + 1)].rearrange("p (z s) -> p z s", z=2)
            init = sm[0:SP_, 500:500 + 2 * K].rearrange("p (z k) -> p z k", z=2)
            isum = op == ALU.add
            o0, o1, start = (ALU.mult, ALU.add, 0.0) if isum else (ALU.add, ALU.max, -BIG)
            whole = [SP_, K, SL]
            with st:
                @block.tensor
                def _(pe):
                    for h in range(K):
                        for c in range(4):
                            mm = pe.transpose(ps[0:SP_, h, c * P:(c + 1) * P],
                                              values[:, :, h].rearrange("p (q c) -> p c q", c=4)[:, c, :], ident[:, :])
                    mm.then_inc(turned, 1)
                    outs = 0

                    def give_back(src):
                        for k in range(K):
                            for c in range(4):
                                mm = pe.transpose(ps[:, 6 + k % 2, c * SP_:(c + 1) * SP_], src[:, k, c * P:(c + 1) * P],
                                                  ident[0:SP_, 0:SP_])
                            mm.then_inc(back, 1)
                            yield

                    for r in range(rels):
                        pe.wait_ge(tails, r + 1)
                        for z in range(4):
                            mm = pe.transpose(ps[0:K, 4, z * SP_:(z + 1) * SP_], tail[:, z, :], ident[0:SP_, 0:SP_])
                        mm.then_inc(tails_up, 1)
                        pe.wait_ge(carry, r + 1)
                        pe.transpose(ps[0:SP_, 5, 0:K], crow[:, 0, 0:SP_], ident[0:K, 0:K])
                        pe.transpose(ps[0:SP_, 5, K:2 * K], crow[:, 1, 1:SP_ + 1], ident[0:K, 0:K]).then_inc(carry_up, 1)
                        if ends is not None:
                            pe.wait_ge(done, r + 1)
                            for _ in give_back(U):
                                outs += 1
                                pe.wait_ge(taken, outs)
                    if total is not None:
                        pe.wait_ge(done, rels + 1)
                        for _ in give_back(TS):
                            outs += 1
                            pe.wait_ge(taken, outs)

                @block.vector
                def _(dve):
                    outs = 0

                    def take_back(dest):
                        nonlocal outs
                        for k in range(K):
                            outs += 1
                            dve.wait_ge(back, outs)
                            dve.tensor_copy(dest[:, :, k].rearrange("p (q c) -> p c q", c=4),
                                            ps[:, 6 + k % 2, 0:NB].rearrange("p (c q) -> p c q", c=4))
                            dve.drain().then_inc(taken, 1)

                    if isum:
                        dve.tensor_scalar(gates[:, 0, :], cont[:, :], 0.0, None, ALU.is_equal)
                        dve.tensor_scalar(gates[:, 1, :], isend[:, :], 0.0, None, ALU.is_equal)
                    else:
                        dve.tensor_copy(gates[:, 0, :], cont[:, :])
                        dve.tensor_scalar(gates[:, 1, :], isend[:, :], -BIG, None, ALU.mult)
                    dve.drain()
                    dve.tensor_tensor_scan(near[0], gates[:, 0, :], gates[:, 0, :], BIG, ALU.min, ALU.min)
                    dve.tensor_tensor_scan(near[1][:, ::-1], gates[:, 1, ::-1], gates[:, 1, ::-1], BIG, ALU.min, ALU.min)
                    dve.drain()
                    for z, g in ((1, near[0][:, SL - 1:SL]), (3, near[1][:, 0:1])):
                        dve.tensor_copy(tail[:, z, :], g.to_broadcast([SP_, K]) if K > 1 else g)
                    dve.wait_ge(turned, 1)
                    if rels > 1 and total is not None:
                        dve.memset(TS, 0.0)
                    for r in range(rels):
                        if rels > 1:
                            dve.drain()
                            dve.tensor_scalar(mask, typ_s[:, :], float(r), None, ALU.is_equal)
                            dve.drain()
                            dve.tensor_tensor(V, ps[0:SP_, 0:K, :], bc(mask, whole, 1), ALU.mult)
                            if not isum:
                                dve.tensor_scalar(maskb, mask, 1.0, BIG, ALU.subtract, ALU.mult)
                                dve.drain()
                                dve.tensor_tensor(V, V, bc(maskb, whole, 1), ALU.add)
                        else:
                            dve.tensor_copy(V, ps[0:SP_, 0:K, :])
                        dve.drain()
                        for k in range(K):
                            dve.tensor_tensor_scan(RF[:, k, :], gates[:, 0, :], V[:, k, :], start, o0, o1)
                            dve.tensor_tensor_scan(RB[:, k, ::-1], gates[:, 1, ::-1], V[:, k, ::-1], start, o0, o1)
                        dve.drain()
                        dve.tensor_copy(tail[:, 0, :].unsqueeze(2), RF[:, :, SL - 1:SL])
                        dve.tensor_copy(tail[:, 2, :].unsqueeze(2), RB[:, :, 0:1])
                        dve.drain().then_inc(tails, 1)
                        dve.tensor_tensor(RF, RF, RB, o1)
                        dve.drain()
                        if isum:
                            dve.tensor_tensor(RF, RF, V, ALU.subtract)
                        dve.wait_ge(tails_up, r + 1)
                        dve.tensor_copy(rows, ps[0:K, 4, 0:4 * SP_].rearrange("p (z s) -> p z s", z=4))
                        dve.memset(crow[:, 0, 0:1], start)
                        dve.memset(crow[:, 1, SP_:SP_ + 1], start)
                        dve.drain()
                        dve.tensor_tensor_scan(crow[:, 0, 1:SP_ + 1], rows[:, 1, :], rows[:, 0, :], start, o0, o1)
                        dve.tensor_tensor_scan(crow[:, 1, 0:SP_][:, ::-1], rows[:, 3, ::-1], rows[:, 2, ::-1], start, o0, o1)
                        dve.drain().then_inc(carry, 1)
                        dve.wait_ge(carry_up, r + 1)
                        dve.tensor_copy(init, ps[0:SP_, 5, 0:2 * K].rearrange("p (z k) -> p z k", z=2))
                        for z in range(2):
                            dve.drain()
                            for k in range(K):
                                dve.scalar_tensor_tensor(RF[:, k, :], near[z], init[:, z, k:k + 1], RF[:, k, :], o0, o1)
                        dve.drain()
                        if total is not None:
                            if rels > 1:
                                dve.tensor_tensor(U, RF, bc(mask, whole, 1), ALU.mult)
                                dve.drain()
                                dve.tensor_tensor(TS, TS, U, ALU.add)
                                dve.drain()
                            else:
                                dve.tensor_copy(TS, RF)
                        if ends is not None:
                            dve.tensor_tensor(U, RF, bc(isend[:, :], whole, 1), ALU.mult)
                            dve.drain().then_inc(done, 1)
                            take_back(ends[:, :, r * K:(r + 1) * K])
                    if total is not None:
                        k = rels + 1 - (rels if ends is not None else 0)
                        dve.drain().then_inc(done, k)
                        take_back(total)

        def head_terms(src, att, dst, scratch, groups):
            c = src.shape[2] // groups

            def body(dve):
                dve.tensor_tensor(scratch, src, bc(att, list(src.shape), 1), ALU.mult)
                dve.drain()
                dve.tensor_reduce(dst, scratch.rearrange("p t (g c) -> p t g c", c=c), AX, ALU.add)
                dve.drain()
            return body

        constants()
        store_load([(tiles(x_table), X[:, :, :])],
                   [(w_view(2, HID)[:, 0, :], A["L0_gnn_W_l0"]), (w_view(2, HID)[:, 1, :], A["L0_gnn_W_r0"]),
                    (biases[:, 0:HID], rowb(A["L0_gnn_b_l0"], HID)), (biases[:, HID:2 * HID], rowb(A["L0_gnn_g0"], HID)),
                    (biases[:, 2 * HID:3 * HID], rowb(A["L0_gnn_be0"], HID)),
                    (biases[:, 3 * HID:4 * HID], rowb(A["L0_gnn_b_l1"], HID)),
                    (biases[:, 4 * HID:5 * HID], rowb(A["L0_gnn_g1"], HID)),
                    (biases[:, 5 * HID:6 * HID], rowb(A["L0_gnn_be1"], HID))])
        split_keys()
        for key in ("D", "S"):
            histogram(key)
            bases(key)
            place(key)
        load_list("S")
        load_list("D")

        def degrees(dve):
            dve.tensor_scalar(no_edge[:, :], deg[:, :], 0.0, None, ALU.is_equal)
            dve.drain()
            dve.tensor_scalar(deg[:, :], deg[:, :], 1.0, None, ALU.max)
            dve.drain()
            dve.reciprocal(deg[:, :], deg[:, :])
        dve_stage(degrees)

        edge_pass("D", x_table, idx["Dsrc"][:, :])
        dense([(big_view(F), 1, True), (X[:, :, :], 1, False)], HID, hid, bias=biases[:, 0:HID])
        norm(hid, HID, big_view(HID), biases[:, HID:2 * HID], biases[:, 2 * HID:3 * HID])
        kn = "(k p) n -> p k n"
        store_load([(tiles(hidden1_table), hid)],
                   [(w_view(4, HID)[:, 0:2, :], A["L0_gnn_W_l1"].rearrange(kn, p=P)),
                    (w_view(4, HID)[:, 2:4, :], A["L0_gnn_W_r1"].rearrange(kn, p=P))])
        wide_pass("D", HID, hidden1_table, idx["Dsrc"][:, :])
        dense([(big_view(HID), 2, True), (hid, 2, False)], HID, hid, bias=biases[:, 3 * HID:4 * HID])
        norm(hid, HID, big_view(HID), biases[:, 4 * HID:5 * HID], biases[:, 5 * HID:6 * HID])
        store_load([], [(w_view(2, F), A["L0_gnn_W_l2"].rearrange(kn, p=P))])
        dense([(hid, 2, False)], F, big_view(F))
        store_load([(tiles(proj2_table), big_view(F))],
                   [(w_view(2, F), A["L0_gnn_W_r2"].rearrange(kn, p=P)),
                    (biases[:, 0:F], rowb(A["L0_gnn_b_l2"], F))])
        edge_pass("D", proj2_table, idx["Dsrc"][:, :])
        full = [P, T, F]

        def sage2(dve):
            acc = big_view(F)
            dve.tensor_tensor(acc, acc, bc(deg[:, :], full, 2), ALU.mult)
            dve.drain()
            dve.tensor_tensor(acc, acc, bc(biases[:, 0:F], full, 1), ALU.add)
            dve.drain()
            dve.tensor_tensor(X[:, :, :], X[:, :, :], acc, ALU.add)
        dve_stage(sage2)
        dense([(hid, 2, False)], F, X[:, :, :], add=True)
        norm(X[:, :, :], F, big_view(F))

        att_src, att_dst = biases[:, 0:384], biases[:, 384:768]
        rel_bias, rel_w = biases[:, 768:1152], biases[:, 1152:1155]
        rhc = "(o r) h c -> o (r h c)"
        store_load([], [(w_view(1, 384)[:, 0, :].rearrange("p (r n) -> p r n", r=NREL), A["L1_gnn_W"].rearrange("r p n -> p r n")),
                        (att_src, A["L1_gnn_att_src"].rearrange(rhc, o=1).to_broadcast([P, 384])),
                        (att_dst, A["L1_gnn_att_dst"].rearrange(rhc, o=1).to_broadcast([P, 384])),
                        (rel_bias, A["L1_gnn_bias"].rearrange("(o r) c -> o (r c)", o=1).to_broadcast([P, 384])),
                        (rel_w, rowb(A["L1_gnn_rel_w"], NREL))])
        relh = big_view(384)
        dense([(X[:, :, :], 1, False)], 384, relh)
        own24 = weights[:, 384:384 + T * SIDE].rearrange("p (t k) -> p t k", t=T)

        def rel_terms(dve):
            for r in range(NREL):
                h = relh[:, :, r * F:(r + 1) * F]
                head_terms(h, att_src[:, r * F:(r + 1) * F], node_a[:, :, 4 * r:4 * r + 4], H1, HEADS)(dve)
                head_terms(h, att_dst[:, r * F:(r + 1) * F], node_a[:, :, 12 + 4 * r:16 + 4 * r], H1, HEADS)(dve)
            for r in range(NREL):
                dve.tensor_copy(own24[:, :, r:12:NREL], node_a[:, :, 12 + 4 * r:16 + 4 * r])
                dve.tensor_copy(own24[:, :, 12 + r:24:NREL], node_a[:, :, 4 * r:4 * r + 4])
            dve.tensor_reduce(sm[:, 0:1], rel_w, AX, ALU.max)
            dve.drain()
            dve.tensor_scalar(rel_w, rel_w, sm[:, 0:1], None, ALU.subtract)

        def exp_stage(before, pairs):
            st, block, (arg,) = stage("argument")
            with st:
                @block.vector
                def _(dve):
                    before(dve)
                    dve.drain().then_inc(arg, 1)

                @block.scalar
                def _(act):
                    act.wait_ge(arg, 1)
                    for o, i, f in pairs:
                        act.activation(o, i, f)
        exp_stage(rel_terms, [(rel_w, rel_w, ACT.Exp)])
        rows = [slice(r * NP, (r + 1) * NP) for r in range(NREL)]
        store_load([(tiles(rel_h_table[rows[r], :]), relh[:, :, r * F:(r + 1) * F]) for r in range(NREL)]
                   + [(tiles(rel_src_table[rows[r], :]), node_a[:, :, 4 * r:4 * r + 4]) for r in range(NREL)], [])
        ends_sum = hidf[:, 0:NB * 12].rearrange("p (b k) -> p b k", k=12)
        e_src, e_dst, e_own, e_max = ebuf[:, :, 0:4], ebuf[:, :, 4:8], ebuf[:, :, 8:12], ends_sum[:, :, 0:4]
        node_fetch("D", own24, ebuf[:, :, 4:12], other_dest=e_src, table=rel_src_table, index=idx["DsrcT"][:, :])
        segment_totals(ALU.max, HEADS, NREL, e_src, total=e_max, ends=em)

        def leaky(dve, a, slope):
            dve.scalar_tensor_tensor(a, a, slope, a, ALU.mult, ALU.max)

        def rel_args(dve):
            dve.tensor_tensor(e_max, e_max, e_own, ALU.max)
            dve.tensor_tensor(e_src, e_src, e_dst, ALU.add)
            dve.drain()
            dve.tensor_tensor(e_max, e_max, e_dst, ALU.add)
            dve.tensor_tensor(e_own, e_own, e_dst, ALU.add)
            dve.drain()
            for a in (e_src, e_own, e_max):
                leaky(dve, a, 0.2)
            dve.drain()
            dve.tensor_tensor(e_src, e_src, e_max, ALU.subtract)
            dve.tensor_tensor(e_own, e_own, e_max, ALU.subtract)
            dve.tensor_reduce(sm[:, 0:1], rel_w, AX, ALU.add)
            dve.drain()
            dve.reciprocal(sm[:, 0:1], sm[:, 0:1])
            dve.drain()
            dve.tensor_scalar(rel_w, rel_w, sm[:, 0:1], None, ALU.mult)
        exp_stage(rel_args, [(e_src, e_src, ACT.Exp), (e_own, e_own, ACT.Exp)])
        segment_totals(ALU.add, HEADS, NREL, e_src, total=e_dst, ends=ends_sum)

        def rel_alphas(dve):
            share, one = bigf[:, 0:NB], bigf[:, NB:2 * NB]
            dve.tensor_tensor(e_dst, e_dst, e_own, ALU.add)
            dve.memset(share, 0.0)
            dve.drain()
            dve.reciprocal(e_dst, e_dst)
            for r in range(NREL):
                dve.drain()
                dve.tensor_scalar(one, typ[:, :], float(r), None, ALU.is_equal)
                dve.drain()
                dve.scalar_tensor_tensor(share, one, rel_w[:, r:r + 1], share, ALU.mult, ALU.add)
            dve.tensor_tensor(e_src, e_src, e_dst, ALU.mult)
            dve.drain()
            dve.tensor_tensor(e_src, e_src, bc(share, [P, NB, HEADS], 2), ALU.mult)
        dve_stage(rel_alphas)
        edge_pass("D", rel_h_table, idx["DsrcT"][:, :], payload=e_src, heads=HEADS, sides=(em, ends_sum))

        acc = big_view(F + SIDE)
        own_w, own_m = node_a[:, :, 0:12], node_a[:, :, 24:36]
        node_max, node_sum = acc[:, :, F:F + 12], acc[:, :, F + 12:F + 24]

        def own_args(dve):
            lone = sm[:, 64:64 + T]
            dve.tensor_scalar(lone, no_edge[:, :], -BIG, None, ALU.mult)
            dve.drain()
            dve.tensor_tensor(own_m, node_max, bc(lone, [P, T, 12], 2), ALU.add)
            dve.drain()
            dve.tensor_tensor(own_m, own_m, own_w, ALU.max)
            dve.drain()
            dve.tensor_tensor(own_m, own_m, node_a[:, :, 12:24], ALU.add)
            dve.tensor_tensor(own_w, own_w, node_a[:, :, 12:24], ALU.add)
            dve.drain()
            leaky(dve, own_m, 0.2)
            leaky(dve, own_w, 0.2)
            dve.drain()
            dve.tensor_tensor(own_w, own_w, own_m, ALU.subtract)
        exp_stage(own_args, [(own_w, own_w, ACT.Exp)])

        def own_alphas(dve):
            dve.tensor_tensor(node_sum, node_sum, own_w, ALU.add)
            dve.drain()
            dve.reciprocal(node_sum, node_sum)
            dve.tensor_tensor(X[:, :, :], X[:, :, :], acc[:, :, 0:F], ALU.add)
            dve.drain()
            dve.tensor_tensor(own_w, own_w, node_sum, ALU.mult)
            for r in range(NREL):
                dve.drain()
                dve.tensor_scalar(own_w[:, :, 4 * r:4 * r + 4], own_w[:, :, 4 * r:4 * r + 4], rel_w[:, r:r + 1], None, ALU.mult)
                dve.tensor_scalar(rel_bias[:, r * F:(r + 1) * F], rel_bias[:, r * F:(r + 1) * F], rel_w[:, r:r + 1], None,
                                  ALU.mult)
        dve_stage(own_alphas)
        full = [P, T, F]
        own_rows = [hidf[:, 0:T * F].rearrange("p (t f) -> p t f", t=T), hidf[:, T * F:2 * T * F].rearrange("p (t f) -> p t f", t=T),
                    bigf[:, 0:T * F].rearrange("p (t f) -> p t f", t=T)]
        store_load([], [(own_rows[r], tiles(rel_h_table[rows[r], :])) for r in range(NREL)])

        def own_sums(dve):
            for r in range(NREL):
                for t in range(0, T, DT):
                    h = own_rows[r][:, t:t + DT, :].rearrange("p t (h c) -> p t h c", c=HD)
                    dve.tensor_tensor(h, h, bc(own_w[:, t:t + DT, 4 * r:4 * r + 4], [P, DT, HEADS, HD], 3), ALU.mult)
                dve.tensor_tensor(X[:, :, :], X[:, :, :], bc(rel_bias[:, r * F:(r + 1) * F], full, 1), ALU.add)
                dve.drain()
                dve.tensor_tensor(X[:, :, :], X[:, :, :], own_rows[r], ALU.add)
                dve.drain()
        dve_stage(own_sums)
        norm(X[:, :, :], F, big_view(F))

        store_load([], [(w_view(1, F)[:, 0, :], A["L2_gnn_W"]), (biases[:, 0:F], rowb(A["L2_gnn_a_i"], F)),
                        (biases[:, F:2 * F], rowb(A["L2_gnn_a_j"], F))])
        dense([(X[:, :, :], 1, False)], F, H1)
        sj, si, sm_ = node_a[:, :, 0:1], node_a[:, :, 1:2], node_a[:, :, 2:3]

        def l2_terms(dve):
            dve.tensor_tensor(H1, H1, X[:, :, :], ALU.add)
            head_terms(X[:, :, :], biases[:, F:2 * F], sj, big_view(F), 1)(dve)
            head_terms(X[:, :, :], biases[:, 0:F], si, big_view(F), 1)(dve)
        dve_stage(l2_terms)
        c0, c4, c8 = ebuf[:, :, 0:1], ebuf[:, :, 4:5], ebuf[:, :, 8:9]
        node_fetch("D", si, c4, other=sj, other_dest=c0)
        segment_totals(ALU.max, 1, 1, c0, total=c8, ends=em[:, :, 0:1])

        def weight_args(a, d, m, slope):
            def body(dve):
                dve.tensor_tensor(a, a, d, ALU.add)
                dve.tensor_tensor(m, m, d, ALU.add)
                dve.drain()
                leaky(dve, a, slope)
                leaky(dve, m, slope)
                dve.drain()
                dve.tensor_tensor(a, a, m, ALU.subtract)
            return body
        exp_stage(weight_args(c0, c4, c8, 0.01), [(c0, c0, ACT.Exp)])
        segment_totals(ALU.add, 1, 1, c0, ends=em[:, :, 1:2])
        side_pass("D", em[:, :, 0:2])

        def l2_messages(dve):
            sums, den = big_view(2), sm[:, 0:T]
            dve.tensor_tensor(sm_, sums[:, :, 0:1], si, ALU.add)
            dve.tensor_tensor(den, sums[:, :, 1], no_edge[:, :], ALU.add)
            dve.drain()
            leaky(dve, sm_, 0.01)
            dve.reciprocal(den, den)
            dve.drain()
            dve.tensor_tensor(H1, H1, bc(den, full, 2), ALU.mult)
        dve_stage(l2_messages)
        store_load([(tiles(row_table[0]), H1)], [])
        node_fetch("S", sj, c0, other=node_a[:, :, 1:3], other_dest=ebuf[:, :, 4:6])

        def l2_args(dve):
            dve.tensor_tensor(c0, c0, c4, ALU.add)
            dve.drain()
            leaky(dve, c0, 0.01)
            dve.drain()
            dve.tensor_tensor(c0, c0, ebuf[:, :, 5:6], ALU.subtract)
        exp_stage(l2_args, [(c0, c0, ACT.Exp)])
        edge_pass("S", row_table[0], idx["Sdst"][:, :], payload=c0, heads=1)
        exp_stage(lambda dve: None, [(big_view(F), big_view(F), ACT.Gelu)])

        def add_acc(dve):
            dve.tensor_tensor(X[:, :, :], X[:, :, :], big_view(F), ALU.add)
        norm(X[:, :, :], F, big_view(F), before=add_acc)

        def keep_x(dve):
            dve.tensor_copy(XR, X[:, :, :])
        dve_stage(keep_x)
        for l in range(2):
            store_load([], [(w_view(1, F)[:, 0, :], A["L3_gnn_W"][l]),
                            (biases[:, 0:F], A["L3_gnn_a_src"][l:l + 1].rearrange("o h c -> o (h c)").to_broadcast([P, F])),
                            (biases[:, F:2 * F], A["L3_gnn_a_dst"][l:l + 1].rearrange("o h c -> o (h c)").to_broadcast([P, F])),
                            (biases[:, 2 * F:3 * F], A["L3_gnn_b"][l:l + 1, :].to_broadcast([P, F]))])
            dense([(X[:, :, :], 1, False)], F, H1)

            def gat_terms(dve):
                head_terms(H1, biases[:, 0:F], node_a[:, :, 0:4], big_view(F), HEADS)(dve)
                head_terms(H1, biases[:, F:2 * F], node_a[:, :, 4:8], big_view(F), HEADS)(dve)
            dve_stage(gat_terms)
            store_load([(tiles(row_table[1 + l]), H1)], [])
            node_fetch("D", node_a[:, :, 4:8], ebuf[:, :, 4:8], other=node_a[:, :, 0:4], other_dest=ebuf[:, :, 0:4])
            segment_totals(ALU.max, HEADS, 1, ebuf[:, :, 0:4], total=ebuf[:, :, 8:12])
            exp_stage(weight_args(ebuf[:, :, 0:4], ebuf[:, :, 4:8], ebuf[:, :, 8:12], 0.2),
                      [(ebuf[:, :, 0:4], ebuf[:, :, 0:4], ACT.Exp)])
            edge_pass("D", row_table[1 + l], idx["Dsrc"][:, :], payload=ebuf[:, :, 0:4], heads=HEADS,
                      sides=(ebuf[:, :, 0:4],))
            acc = big_view(F + 4)

            def gat_node(dve):
                dve.tensor_scalar(acc[:, :, F:F + 4], acc[:, :, F:F + 4], 1e-16, None, ALU.add)
                dve.tensor_tensor(X[:, :, :], X[:, :, :], bc(biases[:, 2 * F:3 * F], full, 1), ALU.add)
                dve.drain()
                dve.reciprocal(acc[:, :, F:F + 4], acc[:, :, F:F + 4])
                dve.drain()
                for t in range(0, T, DT):
                    a = acc[:, t:t + DT, 0:F].rearrange("p t (h c) -> p t h c", c=HD)
                    dve.tensor_tensor(a, a, bc(acc[:, t:t + DT, F:F + 4], [P, DT, HEADS, HD], 3), ALU.mult)
                dve.drain()
                dve.tensor_tensor(X[:, :, :], X[:, :, :], acc[:, :, 0:F], ALU.add)
                if l == 0:
                    dve.drain()
                    dve.tensor_scalar(H1, X[:, :, :], 0.0, None, ALU.min)

            def elu_sum(dve):
                dve.tensor_scalar(X[:, :, :], X[:, :, :], 0.0, -1.0, ALU.max, ALU.add)
                dve.drain()
                dve.tensor_tensor(X[:, :, :], X[:, :, :], H1, ALU.add)
            if l == 0:
                exp_stage(gat_node, [(H1, H1, ACT.Exp)])
                dve_stage(elu_sum)
            else:
                dve_stage(gat_node)

        def add_back(dve):
            dve.tensor_tensor(X[:, :, :], X[:, :, :], XR, ALU.add)
        norm(X[:, :, :], F, big_view(F), before=add_back)
        store_load([(out[0:(T - 1) * P, :].rearrange("(t p) f -> p t f", p=P), X[:, 0:T - 1, :]),
                    (out[(T - 1) * P:N, :], X[0:TAIL, T - 1, :])], [])


_IN = ["x", "src", "dst", "edge_type_3", "L0_gnn_W_l0", "L0_gnn_b_l0", "L0_gnn_W_r0", "L0_gnn_g0", "L0_gnn_be0",
       "L0_gnn_W_l1", "L0_gnn_b_l1", "L0_gnn_W_r1", "L0_gnn_g1", "L0_gnn_be1", "L0_gnn_W_l2", "L0_gnn_b_l2",
       "L0_gnn_W_r2", "L1_gnn_W", "L1_gnn_att_src", "L1_gnn_att_dst", "L1_gnn_bias", "L1_gnn_rel_w", "L2_gnn_a_i",
       "L2_gnn_a_j", "L2_gnn_W", "L3_gnn_W", "L3_gnn_a_src", "L3_gnn_a_dst", "L3_gnn_b"]


def kernel(**inputs):
    import numpy as np
    import concourse.bacc as bacc
    from concourse.bass_utils import run_bass_kernel_spmd as run
    nc = bacc.Bacc("TRN2", target_bir_lowering=False, num_devices=1)
    arrays, aps = {}, {}
    for name in _IN:
        a = np.ascontiguousarray(inputs[name])
        arrays["in_" + name] = a
        aps[name] = nc.dram_tensor("in_" + name, a.shape, mybir.dt.from_np(a.dtype), kind="ExternalInput").ap()
    o = nc.dram_tensor("out", (N, F), mybir.dt.float32, kind="ExternalOutput").ap()
    build(nc, aps, o)
    r = run(nc, [arrays], core_ids=[0])
    return r.results[0]["out"]
```

```python
import concourse.bass as bass
from concourse import mybir
from contextlib import ExitStack

P = 128
N = 3125
E = 53125
F = 128
HID = 256
HEADS, HD = 4, 32
NREL = 3
T = (N + P - 1) // P
NP = T * P
TAIL = N - (T - 1) * P
SB = 8
IB = -(-E // (P * 2 * SB)) * 2 * SB
ROWS_FULL, ROW_TAIL = divmod(E, IB)
RING = 16
GB = 4
NG = RING // GB
NB = -(-(-(-E // P) + T) // RING) * RING
NSLOT = NB * P
TURNS = NB // RING
SP_ = NB // 4
SL = 4 * P
LATE = 10
PADKEY = 4095
FAR = 1e6
BIG = 1e30
DT = 5
EPS = 1e-5
SIDE = 2 * NREL * HEADS
SIDE_FIT = 512 // SIDE
SIDE_BACK = 7 * 512 + SIDE_FIT * SIDE - T * F


def build(nc, A, out):
    f32, bf16, i32 = mybir.dt.float32, mybir.dt.bfloat16, mybir.dt.int32
    ALU, ACT, AX = mybir.AluOpType, mybir.ActivationFunctionType, mybir.AxisListType.X
    ds = bass.ds
    ctx = ExitStack()
    with ctx:
        def sb(name, shape, dt=f32):
            return ctx.enter_context(nc.sbuf_tensor(name, shape, dt))

        def dram(name, shape, dt=f32):
            return nc.dram_tensor(name, shape, dt, kind="Internal").ap()

        lists = {"D": dram("edges_by_dst", (NSLOT + 2, 4), i32), "S": dram("edges_by_src", (NSLOT + 2, 4), i32)}
        hidden1_table = dram("hidden1_table", (NP, HID))
        proj2_table = dram("proj2_table", (NP, F))
        rel_h_table = dram("rel_h_table", (NREL * NP, F))
        rel_src_table = dram("rel_src_table", (NREL * NP, HEADS))
        row_table = [dram(f"row_table{i}", (NP, F)) for i in range(3)]

        iota_free = sb("iota_free", [P, P])
        iota_part = sb("iota_part", [P, 1])
        iota_hi = sb("iota_hi", [P, T])
        iota_blk = sb("iota_blk", [1, NB])
        ident = sb("ident", [P, P])
        identb = sb("identb", [P, P], bf16)
        ones = sb("ones", [P, P])
        lower = sb("lower", [P, P])
        X = sb("X", [P, T, F])
        bigf = sb("bigf", [P, (IB + 1) * T])
        hidf = sb("hidf", [P, T * HID])
        ringf = sb("ringf", [P, RING * HID])
        not_lower = sb("not_lower", [P, P], bf16)
        onehot2 = sb("onehot2", [P, 2, GB, P])
        zeros = sb("zeros", [P, 512], bf16)
        rhsf = sb("rhsf", [P, GB * 396])
        rhs2 = rhsf[:, 0:2 * GB * 160].rearrange("p (z b f) -> p z b f", z=2, b=GB)
        idx_stage = sb("idx_stage", [P, RING], i32)
        weights = sb("weights", [P, 4 * HID])
        biases = sb("biases", [P, 6 * HID])
        dxt = sb("dxt", [P, 4 * DT * P])
        sm = sb("sm", [P, 640])
        deg = sb("deg", [P, T])
        node_a = sb("node_a", [P, T, 36])
        idx = {k: sb("idx_" + k, [P, NB], i32) for k in ("Dsrc", "DsrcT", "Sdst")}
        lo = {"D": sb("lo_D", [P, NB]), "S": sb("lo_S", [P, NB])}
        typ = sb("typ", [P, NB])
        hi_other = {"D": sb("hi_other_D", [P, NB]), "S": sb("hi_other_S", [P, NB])}
        rows_own = {k: sb("rows_own_" + k, [SP_, SL], bf16) for k in ("D", "S")}
        rows_other = {k: sb("rows_other_" + k, [SP_, SL], bf16) for k in ("D", "S")}
        minus_part = sb("minus_part", [P, 1])
        no_edge = sb("no_edge", [P, T])
        tid_side = sb("tid_side", [1, NB], i32)
        tid = {"D": sb("tid_D", [1, NB], i32), "S": sb("tid_S", [1, NB], i32)}
        cont = sb("cont", [SP_, SL])
        isend = sb("isend", [SP_, SL])
        typ_s = sb("typ_s", [SP_, SL])
        ebuf = sb("ebuf", [P, NB, 12])
        em = sb("em", [P, NB, 12])
        posidx = sb("posidx", [P, 2, SB], i32)
        recst = sb("recst", [P, 2, SB, 4], i32)
        ps = ctx.enter_context(nc.psum_tensor("ps", [P, 8, 512], f32))
        psf = ps[:, :, :].rearrange("p a b -> p (a b)")

        def block_view(buf, at):
            return buf.bitcast(bf16)[:, at:at + (IB + 1) * T].rearrange("p (b h) -> p b h", h=T)
        emf = em[:, :, :].rearrange("p a b -> p (a b)")
        hist = {"D": [block_view(bigf[:, :], 0), block_view(bigf[:, :], (IB + 1) * T)],
                "S": [block_view(emf, 0), block_view(hidf[:, :], 0)]}
        hid = hidf[:, :].rearrange("p (t f) -> p t f", t=T)
        H1 = hidf[:, 0:T * F].rearrange("p (t f) -> p t f", t=T)
        XR = hidf[:, T * F:2 * T * F].rearrange("p (t f) -> p t f", t=T)
        ring = ringf[:, :].rearrange("p (r f) -> p r f", r=RING)
        ebuf_i = ebuf[:, :, :].rearrange("p a b -> p (a b)").bitcast(i32)
        edge_raw = ebuf_i[:, 0:3 * IB].rearrange("p (k b) -> p k b", k=3)
        rec_all = ebuf_i[:, 3 * IB:7 * IB].rearrange("p (b k) -> p b k", k=4)
        pos_src = ebuf_i[:, 7 * IB:8 * IB]
        late_at = NB * 12
        late_pos = hidf[:, late_at:late_at + 2 * SB * LATE].bitcast(i32)
        late_rec = hidf[:, late_at + 2 * SB * LATE:late_at + 10 * SB * LATE].bitcast(i32).rearrange("p (b k) -> p b k", k=4)
        KW = IB + 2 * SB
        keys = X[:, :, :].rearrange("p a b -> p (a b)")
        key_lo = {"D": keys[:, 0:KW], "S": keys[:, KW:2 * KW]}
        key_hi = {"D": keys[:, 2 * KW:3 * KW], "S": keys[:, 3 * KW:4 * KW]}
        key_far = {"D": keys[:, 4 * KW:4 * KW + IB], "S": keys[:, 4 * KW + IB:4 * KW + 2 * IB]}
        key_tmp = keys[:, 4 * KW + 2 * IB:4 * KW + 3 * IB].bitcast(i32)
        pad_rec = {"D": ringf[:, 0:4 * SL].bitcast(i32), "S": ringf[:, 4 * SL:8 * SL].bitcast(i32)}
        dxt3 = dxt[:, :].rearrange("p (s f) -> p s f", f=P)

        def big_view(n):
            return bigf[:, 0:T * n].rearrange("p (t f) -> p t f", t=T)

        def w_view(k, n):
            return weights[:, 0:k * n].rearrange("p (k n) -> p k n", k=k)

        def tiles(table):
            return table.rearrange("(t p) f -> p t f", p=P)

        def bc(ap, shape, at):
            return ap.unsqueeze(at).to_broadcast(shape)

        sem_sets = [[ctx.enter_context(nc.semaphore(f"stage{z}_{i}")) for i in range(16)] for z in range(2)]
        used_sems = []
        gathered = [ctx.enter_context(nc.semaphore(f"gathered{j}")) for j in range(NG)]
        scattered = [ctx.enter_context(nc.semaphore(f"scattered{z}")) for z in range(2)]
        scattered_src = [ctx.enter_context(nc.semaphore(f"scattered_src{z}")) for z in range(2)]
        before = {"gathered": 0, "scattered_src": 0}

        def stage(*names):
            k = len(used_sems)
            if k:
                for s in sem_sets[(k - 1) % 2][0:used_sems[-1]]:
                    nc.gpsimd.sem_clear(s)
            used_sems.append(len(names))
            st = ExitStack()
            block = st.enter_context(nc.Block())
            return st, block, sem_sets[k % 2][0:len(names)]


        def constants():
            st, block, (built, cleared, loaded, filled) = stage("built", "cleared", "loaded", "filled")
            with st:
                @block.gpsimd
                def _(pool):
                    pool.memset(ident[:, :], 0.0)
                    pool.memset(ones[:, :], 1.0)
                    pool.memset(lower[:, :], 1.0)
                    pool.memset(zeros[:, :], 0.0)
                    pool.iota(iota_free[:, :], [[1, P]], base=0, channel_multiplier=0,
                              allow_small_or_imprecise_dtypes=True)
                    pool.iota(iota_hi[:, :], [[1, T]], base=0, channel_multiplier=0,
                              allow_small_or_imprecise_dtypes=True)
                    pool.iota(iota_blk[:, :], [[1, NB]], base=0, channel_multiplier=0,
                              allow_small_or_imprecise_dtypes=True)
                    pool.iota(iota_part[:, :], [[0, 1]], base=0, channel_multiplier=1,
                              allow_small_or_imprecise_dtypes=True)
                    pool.iota(minus_part[:, :], [[0, 1]], base=0, channel_multiplier=-1,
                              allow_small_or_imprecise_dtypes=True)
                    pool.drain()
                    pool.affine_select(out=ident[:, :], in_=ident[:, :], compare_op=ALU.not_equal, fill=1.0, base=0,
                                       pattern=[[-1, P]], channel_multiplier=1)
                    pool.affine_select(out=lower[:, :], in_=lower[:, :], compare_op=ALU.is_gt, fill=0.0, base=0,
                                       pattern=[[1, P]], channel_multiplier=-1)
                    pool.drain().then_inc(built, 1)

                @block.vector
                def _(dve):
                    dve.memset(keys[:, 0:4 * KW], 0.0)
                    dve.memset(edge_raw, PADKEY)
                    for key, col in (("D", 1), ("S", 0)):
                        dve.memset(pad_rec[key], 0)
                    dve.drain()
                    for key, col in (("D", 1), ("S", 0)):
                        dve.memset(pad_rec[key].rearrange("p (s f) -> p s f", f=4)[:, :, col:col + 1], PADKEY)
                    dve.drain().then_inc(cleared, 1)
                    dve.wait_ge(built, 1)
                    dve.tensor_copy(identb[:, :], ident[:, :])
                    dve.tensor_scalar(not_lower[:, :], lower[:, :], 1.0, 2.0, ALU.subtract, ALU.mult)

                @block.sync
                def _(sp):
                    sp.wait_ge(cleared, 1)
                    for key in ("D", "S"):
                        sp.dma_start(lists[key][0:NSLOT, :].rearrange("(p b) f -> p (b f)", p=SP_),
                                     pad_rec[key][0:SP_, :]).then_inc(filled, 16)
                        sp.dma_start(lists[key][NSLOT:NSLOT + 2, :].rearrange("(p b) f -> p (b f)", p=1),
                                     pad_rec[key][0:1, 0:8]).then_inc(filled, 16)
                    for i, name in enumerate(("src", "dst", "edge_type_3")):
                        sp.dma_start(edge_raw[0:ROWS_FULL, i, :],
                                     A[name][0:ROWS_FULL * IB].rearrange("(p b) -> p b", b=IB)).then_inc(loaded, 16)
                        sp.dma_start(edge_raw[ROWS_FULL:ROWS_FULL + 1, i, 0:ROW_TAIL],
                                     A[name][ROWS_FULL * IB:E].rearrange("(p b) -> p b", p=1)).then_inc(loaded, 16)
                    sp.wait_ge(loaded, 16 * 6)
                    sp.wait_ge(filled, 16 * 4)

        def store_load(stores, loads):
            st, block, (stored, loaded) = stage("stored", "loaded")
            with st:
                @block.sync
                def _(sp):
                    for dst, src in stores:
                        sp.dma_start(dst, src).then_inc(stored, 16)
                    for dst, src in loads:
                        sp.dma_start(dst, src).then_inc(loaded, 16)
                    if stores:
                        sp.wait_ge(stored, 16 * len(stores))
                    if loads:
                        sp.wait_ge(loaded, 16 * len(loads))

        def rowb(a, n):
            return a.rearrange("(o n) -> o n", o=1).to_broadcast([P, n])

        def split_keys():
            st, block, _ = stage()
            with st:
                @block.vector
                def _(dve):
                    for k in range(3):
                        dve.tensor_copy(rec_all[:, :, k:k + 1], edge_raw[:, k, :].unsqueeze(2))
                    dve.memset(rec_all[:, :, 3:4], 0)
                    for key, i in (("D", 1), ("S", 0)):
                        dve.drain()
                        dve.tensor_scalar(key_tmp, edge_raw[:, i, :], 7, None, ALU.arith_shift_right)
                        dve.drain()
                        dve.tensor_copy(key_hi[key][:, 0:IB], key_tmp)
                        dve.drain()
                        dve.tensor_scalar(key_tmp, edge_raw[:, i, :], P - 1, None, ALU.bitwise_and)
                        dve.drain()
                        dve.tensor_copy(key_lo[key][:, 0:IB], key_tmp)
                        dve.tensor_scalar(key_far[key], key_hi[key][:, 0:IB], float(T), FAR, ALU.is_ge, ALU.mult)

        def histograms():
            st, block, (masks, counted, kept, t_dve, t_pe, t_act) = stage(
                "masks", "counted", "kept", "tick_dve", "tick_pe", "tick_act")
            low = ringf[:, 0:2 * SB * P].bitcast(bf16).rearrange("p (z a b) -> p z a b", z=4, b=P)
            high = rhsf[:, 0:2 * SB * T].bitcast(bf16).rearrange("p (z a b) -> p z a b", z=4, b=T)
            steps = [(m, ("D", "S")[m % 2], m // 2 * SB) for m in range(4)]
            with st:
                @block.vector
                def _(dve):
                    dve.sem_inc(counted, 4)
                    with dve.Fori(0, IB // SB // 2, 1) as i:
                        for m, key, b in steps:
                            if m % 2 == 0:
                                dve.wait_ge(counted, 4 * i + m + 2)
                                dve.sem_inc(t_dve, 1)
                            dve.tensor_tensor(low[:, m], bc(iota_free[:, :], [P, SB, P], 1),
                                              bc(key_lo[key][:, ds(i * (2 * SB) + b, SB)], [P, SB, P], 2), ALU.is_equal)
                            dve.tensor_tensor(high[:, m], bc(iota_hi[:, :], [P, SB, T], 1),
                                              bc(key_hi[key][:, ds(i * (2 * SB) + b, SB)], [P, SB, T], 2), ALU.is_equal)
                            if m % 2:
                                dve.drain().then_inc(masks, 2)

                @block.tensor
                def _(pe):
                    pe.sem_inc(kept, 4)
                    with pe.Fori(0, IB // SB // 2, 1) as i:
                        for m, key, b in steps:
                            pe.wait_ge(masks, 4 * i + m + 1)
                            pe.sem_inc(t_pe, 1)
                            pe.wait_ge(kept, 4 * i + m + 1)
                            pe.sem_inc(t_pe, 1)
                            for u in range(SB):
                                mm = pe.matmul(ps[:, m, u * T:u * T + T], low[:, m, u, :], high[:, m, u, :],
                                               start=True, stop=True)
                            mm.then_inc(counted, 1)

                @block.scalar
                def _(act):
                    with act.Fori(0, IB // SB // 2, 1) as i:
                        for m, key, b in steps:
                            act.wait_ge(counted, 4 * i + m + 5)
                            act.sem_inc(t_act, 1)
                            act.activation(hist[key][0][:, ds(i * (2 * SB) + b + 1, SB), :],
                                           ps[:, m, 0:SB * T].rearrange("p (b h) -> p b h", h=T), ACT.Copy)
                            act.drain().then_inc(kept, 1)

        def bases(key):
            st, block, (counted, summed, scanned, rounded) = stage("counted", "summed", "scanned", "rounded")
            cnt, tot, nblk, bend, bst, pre = (sm[:, i * 32:i * 32 + T] for i in range(6))
            nblk_i = sm[:, 192:192 + T].bitcast(i32)
            tidf = sm[0:1, 192:192 + NB]
            ones_row = rhsf[:, 1024:1024 + IB + 1]
            scan = [buf[:, 0:DT * (IB + 1)].rearrange("p (h b) -> p h b", h=DT) for buf in (ringf, dxt)]
            first, second = (part.rearrange("p b h -> p h b") for part in hist[key])
            with st:
                @block.vector
                def _(dve):
                    dve.memset(ones_row, 1.0)
                    dve.memset(hist[key][0][:, 0, :], 0.0)
                    dve.tensor_reduce(cnt, first[:, :, 1:], AX, ALU.add)
                    dve.drain().then_inc(counted, 1)
                    dve.wait_ge(summed, 1)
                    if key == "D":
                        dve.tensor_copy(deg[:, :], cnt)
                    dve.tensor_copy(pre, ps[:, 1, 0:T])
                    dve.tensor_scalar(tot, ps[:, 0, 0:T], float(P - 1), None, ALU.add)
                    dve.drain()
                    dve.tensor_copy(nblk_i, tot)
                    dve.drain()
                    dve.tensor_scalar(nblk_i, nblk_i, 7, None, ALU.arith_shift_right)
                    dve.drain()
                    dve.tensor_copy(nblk, nblk_i)
                    dve.drain()
                    dve.tensor_tensor_scan(bend, ones[:, 0:T], nblk, 0.0, ALU.mult, ALU.add)
                    dve.drain()
                    dve.tensor_tensor(bst, bend, nblk, ALU.subtract)
                    dve.drain()
                    dve.tensor_scalar(bst, bst, float(P), 1.0, ALU.mult, ALU.add)
                    dve.drain()
                    dve.tensor_tensor(bst, bst, pre, ALU.add)
                    dve.memset(tidf, 0.0)
                    dve.drain()

                    def second_part(q):
                        dve.wait_ge(rounded, q + 1)
                        dve.tensor_tensor(second[:, q * DT:(q + 1) * DT, :], scan[q % 2],
                                          first[:, q * DT:(q + 1) * DT, :], ALU.subtract)
                        dve.drain()
                    for q in range(T // DT):
                        for k in range(DT):
                            h = q * DT + k
                            dve.tensor_tensor_scan(scan[q % 2][:, k, :], ones_row, first[:, h, :], bst[:, h:h + 1],
                                                   ALU.mult, ALU.add)
                            dve.scalar_tensor_tensor(tidf, iota_blk[0:1, :], bend[0:1, h:h + 1], tidf, ALU.is_ge, ALU.add)
                            dve.drain()
                        dve.drain().then_inc(scanned, 1)
                        if q:
                            second_part(q - 1)
                    second_part(T // DT - 1)
                    dve.tensor_scalar(tidf, tidf, float(T - 1), None, ALU.min)
                    dve.drain()
                    dve.tensor_copy(tid[key][:, :], tidf)
                    if key == "D":
                        over, offs = rhsf[0:1, 0:NB], rhsf[0:1, NB:2 * NB]
                        dve.tensor_scalar(over, tidf, float(SIDE_FIT), float(SIDE_BACK), ALU.is_ge, ALU.mult)
                        dve.tensor_scalar(offs, tidf, float(SIDE), float(7 * 512), ALU.mult, ALU.add)
                        dve.drain()
                        dve.tensor_tensor(offs, offs, over, ALU.subtract)
                        dve.drain()
                        dve.tensor_copy(tid_side[:, :], offs)

                @block.scalar
                def _(act):
                    for q in range(T // DT):
                        act.wait_ge(scanned, q + 1)
                        act.activation(first[:, q * DT:(q + 1) * DT, :], scan[q % 2], ACT.Copy)
                        act.drain().then_inc(rounded, 1)

                @block.tensor
                def _(pe):
                    pe.wait_ge(counted, 1)
                    pe.matmul(ps[:, 0, 0:T], ones[:, :], cnt, start=True, stop=True)
                    pe.matmul(ps[:, 1, 0:T], lower[:, :], cnt, start=True, stop=True).then_inc(summed, 1)

        def place():
            (st, block, (masks, turned, turned_kept, gram_done, gram_kept, found, placed, written,
                         t_dve, t_pe, t_act, t_pool, t_sp)) = stage(
                "masks", "turned", "turned_kept", "gram_done", "gram_kept", "found", "placed", "written",
                 "tick_dve", "tick_pe", "tick_act", "tick_pool", "tick_sp")
            low = ringf[:, 0:2 * SB * P].bitcast(bf16).rearrange("p (z a b) -> p z a b", z=4, b=P)
            gram = ringf[:, 2 * SB * P:3 * SB * P].bitcast(bf16).rearrange("p (z a b) -> p z a b", z=2, b=P)
            lowT = dxt[:, 0:2 * SB * P].bitcast(bf16).rearrange("p (z a b) -> p z a b", z=4, b=P)
            high = rhsf[:, 0:2 * SB * T].bitcast(bf16).rearrange("p (z a b) -> p z a b", z=4, b=T)
            sel = rhsf[:, 2 * SB * T:3 * SB * T].rearrange("p (a b) -> p a b", b=T)
            posf = sm[:, 0:SB]
            LISTS = ("D", "S", "D", "S")

            def make_masks(dve, m, b):
                key = LISTS[m]
                dve.tensor_tensor(low[:, m], bc(iota_free[:, :], [P, SB, P], 1),
                                  bc(key_lo[key][:, ds(b, SB)], [P, SB, P], 2), ALU.is_equal)
                dve.tensor_tensor(high[:, m], bc(iota_hi[:, :], [P, SB, T], 1),
                                  bc(key_hi[key][:, ds(b, SB)], [P, SB, T], 2), ALU.is_equal)
                dve.drain().then_inc(masks, 1)

            def earlier(act, m):
                act.activation(gram[:, m % 2], psf[:, 1024:1024 + SB * P].rearrange("p (a b) -> p a b", b=P), ACT.Relu)
                act.drain().then_inc(gram_kept, 1)

            def turn(pe, m):
                for u in range(SB):
                    mm = pe.matmul(psf[:, u * P:u * P + P], low[:, m, u, :], identb[:, :], start=True, stop=True)
                mm.then_inc(turned, 1)

            def agree(pe, m):
                for u in range(SB):
                    o = psf[:, 1024 + u * P:1024 + u * P + P]
                    pe.matmul(o, lowT[:, m, u, :], lowT[:, m, u, :], start=True, stop=False)
                    mm = pe.matmul(o, identb[:, :], not_lower[:, :], start=False, stop=True)
                mm.then_inc(gram_done, 1)

            with st:
                @block.vector
                def _(dve):
                    make_masks(dve, 0, 0)
                    make_masks(dve, 1, 0)
                    make_masks(dve, 2, SB)
                    with dve.Fori(0, IB // SB // 2, 1) as i:
                        for m in range(4):
                            b = i * (2 * SB) + m // 2 * SB
                            make_masks(dve, (m + 3) % 4, i * (2 * SB) + (m + 3) // 2 * SB)
                            dve.wait_ge(found, i * 4 + m + 1)
                            dve.sem_inc(t_dve, 1)
                            dve.tensor_tensor(sel, ps[:, 4 + m % 2, 0:SB * T].rearrange("p (a b) -> p a b", b=T),
                                              high[:, m], ALU.mult)
                            dve.drain()
                            dve.tensor_reduce(posf, sel, AX, ALU.add)
                            dve.drain()
                            if LISTS[m] == "D":
                                dve.wait_ge(written, i * 2 + m // 2 + 1)
                                dve.sem_inc(t_dve, 1)
                                dve.tensor_tensor(posidx[:, m // 2, :], posf, key_far["D"][:, ds(b, SB)], ALU.add)
                                dve.tensor_copy(recst[:, m // 2], rec_all[:, ds(b, SB), :])
                                dve.drain().then_inc(placed, 1)
                            else:
                                dve.tensor_tensor(pos_src[:, ds(b, SB)], posf, key_far["S"][:, ds(b, SB)], ALU.add)
                                dve.drain()

                @block.tensor
                def _(pe):
                    pe.wait_ge(masks, 1)
                    turn(pe, 0)
                    pe.wait_ge(turned_kept, 1)
                    pe.wait_ge(masks, 2)
                    turn(pe, 1)
                    agree(pe, 0)
                    with pe.Fori(0, IB // SB // 2, 1) as i:
                        for m in range(4):
                            pe.wait_ge(turned_kept, i * 4 + m + 2)
                            pe.sem_inc(t_pe, 1)
                            pe.wait_ge(gram_kept, i * 4 + m + 1)
                            pe.sem_inc(t_pe, 1)
                            agree(pe, (m + 1) % 4)
                            pe.wait_ge(masks, i * 4 + m + 3)
                            pe.sem_inc(t_pe, 1)
                            turn(pe, (m + 2) % 4)
                            for u in range(SB):
                                o = ps[:, 4 + m % 2, u * T:u * T + T]
                                for k, part in enumerate(hist[LISTS[m]]):
                                    pe.matmul(o, lowT[:, m, u, :], part[:, ds(i * (2 * SB) + m // 2 * SB + u, 1), :],
                                              start=k == 0, stop=False)
                                mm = pe.matmul(o, gram[:, m % 2, u, :], high[:, m, u, :], start=False, stop=True)
                            mm.then_inc(found, 1)

                @block.scalar
                def _(act):
                    def keep(m):
                        act.activation(lowT[:, m], psf[:, 0:SB * P].rearrange("p (a b) -> p a b", b=P), ACT.Copy)
                        act.drain().then_inc(turned_kept, 1)
                    for m in range(2):
                        act.wait_ge(turned, m + 1)
                        keep(m)
                    act.wait_ge(gram_done, 1)
                    earlier(act, 0)
                    with act.Fori(0, IB // SB // 2, 1) as i:
                        for m in range(4):
                            act.wait_ge(gram_done, i * 4 + m + 2)
                            act.sem_inc(t_act, 1)
                            earlier(act, (m + 1) % 4)
                            act.wait_ge(turned, i * 4 + m + 3)
                            act.sem_inc(t_act, 1)
                            keep((m + 2) % 4)

                @block.gpsimd
                def _(pool):
                    with pool.Fori(0, IB // SB // 2, 1) as i:
                        for z in range(2):
                            pool.wait_ge(placed, 2 * i + z + 1)
                            pool.sem_inc(t_pool, 1)
                            for u in range(SB):
                                pool.indirect_dma_start(
                                    lists["D"][:, :], bass.IndirectOffsetOnAxis(posidx[:, z, u:u + 1], 0),
                                    recst[:, z, u, :], None, bounds_check=NSLOT + 1, oob_is_err=False
                                ).then_inc(scattered[z], 16)

                @block.sync
                def _(sp):
                    sp.sem_inc(written, 2)
                    with sp.Fori(0, IB // SB // 2, 1) as i:
                        for z in range(2):
                            sp.wait_ge(scattered[z], i * (16 * SB) + 16 * SB)
                            sp.sem_inc(t_sp, 1)
                            sp.sem_inc(written, 1)

        def scatter_by_source(block, tick, turns):
            done = before["scattered_src"]
            late = done >= IB // (2 * SB) - LATE
            pos, rec, first = (late_pos, late_rec, IB - 2 * SB * LATE) if late else (pos_src, rec_all, 0)
            before["scattered_src"] += turns

            @block.gpsimd
            def _(pool):
                def write(b, z):
                    pool.tensor_copy(posidx[:, z, :], pos[:, ds(b, SB)])
                    pool.tensor_copy(recst[:, z], rec[:, ds(b, SB), :])
                    pool.drain()
                    for u in range(SB):
                        pool.indirect_dma_start(
                            lists["S"][:, :], bass.IndirectOffsetOnAxis(posidx[:, z, u:u + 1], 0),
                            recst[:, z, u, :], None, bounds_check=NSLOT + 1, oob_is_err=False
                        ).then_inc(scattered_src[z], 16)
                if done == 0:
                    for z in range(2):
                        write(z * SB, z)
                with pool.Fori(1 if done == 0 else 0, turns, 1) as i:
                    for z in range(2):
                        pool.wait_ge(scattered_src[z], i * (16 * SB) + done * 16 * SB)
                        pool.sem_inc(tick, 1)
                        write(i * (2 * SB) + (done * 2 * SB + z * SB - first), z)

        def load_list(key):
            st, block, (loaded, conv, turned, x_cleared, x_loaded) = stage(
                "loaded", "converted", "turned", "x_cleared", "x_loaded")
            rec = ringf[0:SP_, 0:4 * SL].bitcast(i32).rearrange("p (s f) -> p s f", f=4)
            prev = ringf[0:SP_, 4 * SL:8 * SL].bitcast(i32).rearrange("p (s f) -> p s f", f=4)
            nxt = hidf[0:SP_, 0:4 * SL].bitcast(i32).rearrange("p (s f) -> p s f", f=4)
            fld = bigf[0:SP_, 0:3 * SL].rearrange("p (k s) -> p k s", k=3)
            tmp = bigf[:, 3 * SL:3 * SL + 6 * NB].rearrange("p (k b) -> p k b", k=6)
            tmp_i = tmp.bitcast(i32)
            own, other = (1, 0) if key == "D" else (0, 1)
            with st:
                @block.sync
                def _(sp):
                    if key == "S":
                        for z in range(2):
                            sp.wait_ge(scattered_src[z], IB // SB // 2 * 16 * SB)
                    views = [(rec, 1)] + ([(prev, 0), (nxt, 2)] if key == "D" else [])
                    for dst, first in views:
                        sp.dma_start(dst, lists[key][first:first + NSLOT, :].rearrange("(p s) f -> p s f", p=SP_)
                                     ).then_inc(loaded, 16)
                    if key == "D":
                        sp.wait_ge(x_cleared, 1)
                        sp.dma_start(X[:, 0:T - 1, :], A["x"][0:(T - 1) * P, :].rearrange("(t p) f -> p t f", p=P)
                                     ).then_inc(x_loaded, 16)
                        sp.dma_start(X[0:TAIL, T - 1, :], A["x"][(T - 1) * P:N, :]).then_inc(x_loaded, 16)
                        sp.wait_ge(x_loaded, 32)
                    sp.wait_ge(loaded, 16 * len(views))

                @block.vector
                def _(dve):
                    if key == "D":
                        dve.memset(X[:, T - 1, :], 0.0)
                        dve.drain().then_inc(x_cleared, 1)
                    dve.wait_ge(loaded, 48 if key == "D" else 16)
                    for k in range(3):
                        dve.tensor_copy(fld[:, k, :].unsqueeze(2), rec[:, :, k:k + 1])
                    dve.drain().then_inc(conv, 1)
                    if key == "D":
                        dve.tensor_copy(typ_s[:, :], fld[:, 2, :])
                        dve.tensor_copy(cont[:, :].unsqueeze(2), prev[:, :, 1:2])
                        dve.tensor_copy(isend[:, :].unsqueeze(2), nxt[:, :, 1:2])
                        dve.drain()
                        dve.tensor_tensor(cont[:, :], cont[:, :], fld[:, 1, :], ALU.not_equal)
                        dve.tensor_tensor(isend[:, :], isend[:, :], fld[:, 1, :], ALU.not_equal)
                        dve.drain()
                        dve.tensor_scalar(cont[:, :], cont[:, :], -BIG, None, ALU.mult)
                    dve.wait_ge(turned, 1)
                    for k in range(3):
                        dve.tensor_copy(tmp[:, k, :].rearrange("p (q c) -> p c q", c=4),
                                        ps[:, k, 0:NB].rearrange("p (c q) -> p c q", c=4))
                    dve.drain()
                    for side in (own, other):
                        dve.tensor_copy(tmp_i[:, 3, :], tmp[:, side, :])
                        dve.drain()
                        dve.tensor_scalar(tmp_i[:, 4, :], tmp_i[:, 3, :], 7, None, ALU.arith_shift_right)
                        dve.tensor_scalar(tmp_i[:, 5, :], tmp_i[:, 3, :], P - 1, None, ALU.bitwise_and)
                        dve.drain()
                        if side == other:
                            dve.tensor_copy(hi_other[key][:, :], tmp_i[:, 4, :])
                        else:
                            dve.tensor_copy(lo[key][:, :], tmp_i[:, 5, :])
                            dve.drain()
                            dve.tensor_scalar(tmp[:, 5, :], tmp[:, own, :], float(NP), 1000.0, ALU.is_ge, ALU.mult)
                            dve.drain()
                            dve.tensor_tensor(lo[key][:, :], lo[key][:, :], tmp[:, 5, :], ALU.add)
                        dve.drain()
                    for side, rows in ((own, rows_own[key]), (other, rows_other[key])):
                        sc, sc_i = dxt[0:SP_, 0:SL], dxt[0:SP_, SL:2 * SL].bitcast(i32)
                        dve.tensor_copy(sc_i, fld[:, side, :])
                        dve.tensor_scalar(sc, fld[:, side, :], float(NP), 1000.0, ALU.is_ge, ALU.mult)
                        dve.drain()
                        dve.tensor_scalar(sc_i, sc_i, P - 1, None, ALU.bitwise_and)
                        dve.drain()
                        dve.tensor_tensor(rows[:, :], sc, sc_i, ALU.add)
                        dve.drain()
                    if key == "D":
                        dve.tensor_copy(idx["Dsrc"][:, :], tmp[:, 0, :])
                        dve.tensor_copy(typ[:, :], tmp[:, 2, :])
                        dve.scalar_tensor_tensor(idx["DsrcT"][:, :], tmp[:, 2, :], float(NP), tmp[:, 0, :],
                                                 ALU.mult, ALU.add)
                    else:
                        dve.tensor_scalar(tmp[:, 1, :], tmp[:, 1, :], float(NP - 1), None, ALU.min)
                        dve.drain()
                        dve.tensor_copy(idx["Sdst"][:, :], tmp[:, 1, :])

                @block.tensor
                def _(pe):
                    pe.wait_ge(conv, 1)
                    for k in range(3):
                        for c in range(4):
                            mm = pe.transpose(ps[:, k, c * SP_:(c + 1) * SP_], fld[:, k, c * P:(c + 1) * P],
                                              ident[0:SP_, 0:SP_])
                    mm.then_inc(turned, 1)

        def gather_ahead(block, table, index):
            @block.gpsimd
            def _(pool):
                pool.tensor_copy(idx_stage[:, :], index[:, 0:RING])
                pool.drain()
                for s in range(RING):
                    pool.indirect_dma_start(ring[:, s, 0:F], None, table,
                                            bass.IndirectOffsetOnAxis(idx_stage[:, s:s + 1], 0)
                                            ).then_inc(gathered[s // GB], 16)

        def gather_issue(act, pool_idx, used, staged, tick, first=0):
            with act.Fori(first, TURNS, 1) as i:
                for j in range(NG):
                    act.wait_ge(used, i * NG + j + 1)
                    act.sem_inc(tick, 1)
                    act.activation(idx_stage[:, j * GB:(j + 1) * GB], pool_idx[:, ds(i * RING + j * GB, GB)], ACT.Copy)
                    act.drain().then_inc(staged, 1)

        def gather_rows(pool, table, width, staged, gathered, tick, first=0):
            with pool.Fori(first, TURNS, 1) as i:
                for j in range(NG):
                    pool.wait_ge(staged, i * NG + (j + 1 - first * NG))
                    pool.sem_inc(tick, 1)
                    for u in range(GB):
                        s = j * GB + u
                        pool.indirect_dma_start(ring[:, s, 0:width], None, table,
                                                bass.IndirectOffsetOnAxis(idx_stage[:, s:s + 1], 0)
                                                ).then_inc(gathered[j], 16)

        def block_tiles(pe, key, i):
            _, t = nc.values_load_multi_w_load_instructions(
                tid[key][0:1, ds(i * RING, RING)], engines=(mybir.EngineType.PE,), min_val=0, max_val=T - 1,
                skip_runtime_bounds_check_because="bases() clamps the tiles to 0..T-1")
            return t

        def parts_view(at, rows, n):
            return bigf[:, at:at + (3 * rows * n + 1) // 2].bitcast(bf16)[:, 0:3 * rows * n].rearrange(
                "p (k t n) -> p k t n", k=3, t=rows)

        def split_rows(dve, src, parts, rest):
            n = src.shape[2]
            rest = rest[:, :, 0:n]
            dve.drain()
            dve.tensor_copy(parts[:, 0], src)
            dve.drain()
            dve.tensor_tensor(rest, src, parts[:, 0], ALU.subtract)
            dve.drain()
            dve.tensor_copy(parts[:, 1], rest)
            dve.drain()
            dve.tensor_tensor(parts[:, 2], rest, parts[:, 1], ALU.subtract)
            dve.drain()

        def node_fetch(key, own, own_dest, other=None, other_dest=None, table=None, index=None, ahead=None):
            (st, block, (own_row, own_mask, own_res, other_row, other_mask, other_res, used, staged, other_taken,
                         parts_ready, t_pe, t_dve, t_act, t_pool)) = stage(
                "own_row", "own_mask", "own_result", "other_row", "other_mask", "other_result", "used", "staged",
                "other_taken", "parts_ready", "tick_pe", "tick_dve", "tick_act", "tick_pool")
            no, nx = own.shape[2], (other.shape[2] if other is not None else 0)
            om = dxt[:, 0:SL].bitcast(bf16).rearrange("p (z b f) -> p z b f", z=2, b=GB)
            xm = dxt[:, SL:2 * SL].bitcast(bf16).rearrange("p (z b f) -> p z b f", z=2, b=GB)
            own3 = parts_view(0, T, no)
            other3 = parts_view(T * no * 3 // 2 + 8, T, nx) if nx else None
            rest = bigf[:, 4096:4096 + T * max(no, nx)].rearrange("p (t k) -> p t k", t=T)
            sq = dxt[:, 4 * SL:5 * SL]
            pick = rhsf[:, 0:GB * T].rearrange("p (b h) -> p b h", b=GB)
            prod = rhsf[:, GB * T:GB * T + GB * T * HEADS]
            rows0 = before["gathered"]
            if table is not None:
                before["gathered"] += 16 * GB * TURNS

            with st:
                @block.tensor
                def _(pe):
                    def spread(q, z):
                        pick_q = identb[0:SP_, ds(q, 1)].to_broadcast([SP_, P])
                        pe.matmul(ps[:, z, :], pick_q, rows_own[key][:, :], start=True, stop=True).then_inc(own_row, 1)
                        if other is not None:
                            pe.matmul(ps[:, 2 + z, :], pick_q, rows_other[key][:, :], start=True, stop=True
                                      ).then_inc(other_row, 1)
                    spread(0, 0)
                    pe.wait_ge(parts_ready, 1)
                    with pe.Fori(0, TURNS, 1) as i:
                        t = block_tiles(pe, key, i)
                        for j in range(NG):
                            z, n = j % 2, i * NG + j
                            spread(n + 1, 1 - z)
                            if other is not None:
                                pe.wait_ge(other_mask, n + 1)
                                pe.sem_inc(t_pe, 1)
                                for u in range(GB):
                                    for k in range(3):
                                        mm = pe.matmul(ps[:, 4 + z, u * T * nx:(u + 1) * T * nx], xm[:, z, u, :],
                                                       other3[:, k], start=k == 0, stop=k == 2)
                                mm.then_inc(other_res, 1)
                            pe.wait_ge(own_mask, n + 1)
                            pe.sem_inc(t_pe, 1)
                            if table is not None:
                                pe.wait_ge(other_taken, n + 1)
                                pe.sem_inc(t_pe, 1)
                            for u in range(GB):
                                for k in range(3):
                                    mm = pe.matmul(ps[:, 6 + z, u * no:(u + 1) * no], om[:, z, u, :],
                                                   own3[:, k, ds(t[j * GB + u], 1), :], start=k == 0, stop=k == 2)
                            mm.then_inc(own_res, 1)

                @block.scalar
                def _(act):
                    def mask(z, k):
                        act.wait_ge(own_row, k)
                        act.sem_inc(t_act, 1)
                        act.activation(sq, ps[:, z, :], ACT.Square, bias=minus_part[:, 0:1])
                        act.drain()
                        act.activation(om[:, z].rearrange("p b f -> p (b f)"), sq, ACT.Relu, bias=ones[:, 0:1], scale=-1.0)
                        act.drain().then_inc(own_mask, 1)
                    mask(0, 1)
                    with act.Fori(0, TURNS, 1) as i:
                        for j in range(NG):
                            z, n = j % 2, i * NG + j
                            if table is not None:
                                act.wait_ge(used, n + 1)
                                act.sem_inc(t_act, 1)
                                act.activation(idx_stage[:, j * GB:(j + 1) * GB], index[:, ds(i * RING + j * GB, GB)],
                                               ACT.Copy)
                                act.drain().then_inc(staged, 1)
                            mask(1 - z, n + 2)
                            if table is None:
                                act.wait_ge(own_res, n + 1)
                                act.sem_inc(t_act, 1)
                                act.activation(own_dest[:, ds(i * RING + j * GB, GB), :],
                                               ps[:, 6 + z, 0:GB * no].rearrange("p (b k) -> p b k", b=GB), ACT.Copy)
                                act.drain()

                if ahead:
                    gather_ahead(block, *ahead)

                if table is not None:
                    @block.gpsimd
                    def _(pool):
                        gather_rows(pool, table, HEADS, staged, gathered, t_pool)

                @block.vector
                def _(dve):
                    def mask(z, k):
                        dve.wait_ge(other_row, k)
                        dve.sem_inc(t_dve, 1)
                        dve.tensor_scalar(xm[:, z].rearrange("p b f -> p (b f)"), ps[:, 2 + z, :], iota_part[:, 0:1],
                                          None, ALU.is_equal)
                        dve.drain().then_inc(other_mask, 1)

                    split_rows(dve, own, own3, rest)
                    if other is not None:
                        split_rows(dve, other, other3, rest)
                    dve.drain().then_inc(parts_ready, 1)
                    if other is not None:
                        mask(0, 1)
                    else:
                        dve.sem_inc(used, NG)
                        dve.sem_inc(other_taken, 2)
                    with dve.Fori(0, TURNS, 1) as i:
                        for j in range(NG):
                            z, n, b = j % 2, i * NG + j, i * RING + j * GB
                            if other is not None:
                                dve.tensor_tensor(pick, bc(iota_hi[:, :], [P, GB, T], 1),
                                                  bc(hi_other[key][:, ds(b, GB)], [P, GB, T], 2), ALU.is_equal)
                                mask(1 - z, n + 2)
                                dve.wait_ge(other_res, n + 1)
                                dve.sem_inc(t_dve, 1)
                                pr = prod[:, 0:GB * T * nx].rearrange("p (b h k) -> p b h k", b=GB, k=nx)
                                dve.tensor_tensor(pr, ps[:, 4 + z, 0:GB * T * nx].rearrange("p (b h k) -> p b h k", b=GB, k=nx),
                                                  bc(pick, [P, GB, T, nx], 3), ALU.mult)
                                dve.drain()
                                dve.tensor_reduce(other_dest[:, ds(b, GB), :], pr.rearrange("p b h k -> p b k h"), AX, ALU.add)
                            else:
                                dve.wait_ge(gathered[j], i * (16 * GB) + (rows0 + 16 * GB))
                                dve.sem_inc(t_dve, 1)
                                dve.tensor_copy(other_dest[:, ds(b, GB), :], ring[:, j * GB:(j + 1) * GB, 0:HEADS])
                                dve.drain().then_inc(used, 1)
                                rel = rhsf[:, 0:GB * NREL].rearrange("p (b r) -> p b r", b=GB)
                                dve.tensor_tensor(rel, bc(iota_hi[:, 0:NREL], [P, GB, NREL], 1),
                                                  bc(typ[:, ds(b, GB)], [P, GB, NREL], 2), ALU.is_equal)
                                dve.drain()
                                dve.wait_ge(own_res, n + 1)
                                dve.sem_inc(t_dve, 1)
                                m = no // NREL
                                pr = prod[:, 0:GB * no].rearrange("p (b k r) -> p b k r", b=GB, r=NREL)
                                dve.tensor_tensor(pr, ps[:, 6 + z, 0:GB * no].rearrange("p (b k r) -> p b k r", b=GB, r=NREL),
                                                  bc(rel, [P, GB, m, NREL], 2), ALU.mult)
                                dve.drain()
                                dve.tensor_reduce(own_dest[:, ds(b, GB), :], pr, AX, ALU.add)
                                dve.drain().then_inc(other_taken, 1)

        def weighted(dve, o, rows, w, heads):
            c = F // heads
            if heads == 1:
                dve.tensor_tensor(o, rows, w.to_broadcast([P, GB, F]), ALU.mult)
            else:
                dve.tensor_tensor(o.rearrange("p b (h c) -> p b h c", c=c), rows.rearrange("p b (h c) -> p b h c", c=c),
                                  bc(w, [P, GB, heads, c], 3), ALU.mult)

        def edge_pass(key, table=None, index=None, payload=None, heads=0, sides=(), ahead=False):
            st, block, (used, staged, ready, t_act, t_pool, t_dve, t_pe) = stage(
                "summed", "staged", "operands", "tick_act", "tick_pool", "tick_dve", "tick_pe")
            nf = F if table is not None else 0
            ns = sum(v.shape[2] for v in sides)
            n = nf + ns
            rows0 = before["gathered"]
            if table is not None:
                before["gathered"] += 16 * GB * TURNS
            acc = big_view(n)
            row_sums = psf[:, 0:T * F].rearrange("p (t f) -> p t f", f=F)
            spilled = T * ns > 512
            if ns:
                side_sums = ps[:, 7, 0:min(T, 512 // ns) * ns].rearrange("p (t f) -> p t f", f=ns)
            banks = (list(range(7)) if nf else []) + ([7] if ns else [])
            with st:
                if table is not None:
                    @block.scalar
                    def _(act):
                        gather_issue(act, index, used, staged, t_act, int(ahead))

                    @block.gpsimd
                    def _(pool):
                        gather_rows(pool, table, F, staged, gathered, t_pool, int(ahead))

                @block.vector
                def _(dve):
                    dve.sem_inc(used, NG)
                    with dve.Fori(0, TURNS, 1) as i:
                        for j in range(NG):
                            b, z = i * RING + j * GB, j % 2
                            dve.wait_ge(used, i * NG + j + NG - 1)
                            dve.sem_inc(t_dve, 1)
                            dve.tensor_tensor(onehot2[:, z], bc(iota_free[:, :], [P, GB, P], 1),
                                              bc(lo[key][:, ds(b, GB)], [P, GB, P], 2), ALU.is_equal)
                            at = nf
                            for more in sides:
                                k = more.shape[2]
                                dve.tensor_copy(rhs2[:, z, :, at:at + k], more[:, ds(b, GB), :])
                                at += k
                            if heads:
                                dve.wait_ge(gathered[j], i * (16 * GB) + (rows0 + 16 * GB))
                                dve.sem_inc(t_dve, 1)
                                weighted(dve, rhs2[:, z, :, 0:F], ring[:, j * GB:(j + 1) * GB, 0:F],
                                         payload[:, ds(b, GB), 0:heads], heads)
                            dve.drain().then_inc(ready, 1)
                    dve.wait_ge(used, NG * TURNS + NG + 1)
                    if nf:
                        dve.tensor_copy(acc[:, :, 0:F], row_sums)
                    if ns:
                        k = side_sums.shape[1]
                        dve.tensor_copy(acc[:, 0:k, nf:n], side_sums)
                        if spilled:
                            dve.tensor_copy(acc[:, k:T, nf:n],
                                            psf[:, T * F:T * F + (T - k) * ns].rearrange("p (t f) -> p t f", f=ns))

                @block.tensor
                def _(pe):
                    for k in banks:
                        pe.matmul(ps[:, k, :], zeros[:, 0:P], zeros[:, :], start=True, stop=False)
                    with pe.Fori(0, TURNS, 1) as i:
                        t = block_tiles(pe, key, i)
                        if spilled:
                            _, side = nc.values_load_multi_w_load_instructions(
                                tid_side[0:1, ds(i * RING, RING)], engines=(mybir.EngineType.PE,), min_val=T * F,
                                max_val=8 * 512 - SIDE, skip_runtime_bounds_check_because="bases() makes them from tiles 0..T-1")
                        for j in range(NG):
                            pe.wait_ge(ready, i * NG + j + 1)
                            pe.sem_inc(t_pe, 1)
                            if table is not None and not heads:
                                pe.wait_ge(gathered[j], i * (16 * GB) + (rows0 + 16 * GB))
                                pe.sem_inc(t_pe, 1)
                            for u in range(GB):
                                m, at = onehot2[:, j % 2, u, :], t[j * GB + u]
                                if nf:
                                    r = rhs2[:, j % 2, u, 0:F] if heads else ring[:, j * GB + u, 0:F]
                                    mm = pe.matmul(row_sums[:, ds(at, 1), :], m, r, start=False, stop=False,
                                                   skip_group_check=True)
                                if ns:
                                    o = psf[:, ds(side[j * GB + u], SIDE)] if spilled else side_sums[:, ds(at, 1), :]
                                    mm = pe.matmul(o, m, rhs2[:, j % 2, u, nf:n],
                                                   start=False, stop=False, skip_group_check=True)
                            mm.then_inc(used, 1)
                    for k in banks:
                        mm = pe.matmul(ps[:, k, :], zeros[:, 0:P], zeros[:, :], start=False, stop=True)
                    mm.then_inc(used, 1)

        def side_pass(key, values):
            st, block, (used, ready, t_dve, t_pe) = stage("summed", "operands", "tick_dve", "tick_pe")
            n = values.shape[2]
            acc = big_view(n)
            at, size = T * n, (3 * NB * n + 1) // 2
            parts = bigf[:, at:at + size].bitcast(bf16)[:, 0:3 * NB * n].rearrange("p (b k n) -> p b k n", k=3, n=n)
            rest = bigf[:, at + size:at + size + NB * n].rearrange("p (b n) -> p b n", n=n)
            onehots = onehot2[:, :, :, :].rearrange("p z a b -> p (z a b)").bitcast(bf16).rearrange(
                "p (z a b) -> p z a b", z=4, b=P)
            sums = ps[:, 7, 0:T * 3 * n].rearrange("p (t k n) -> p t k n", k=3, n=n)
            staged = rhsf[:, 0:(RING * 3 * n + 1) // 2].bitcast(bf16)[:, 0:RING * 3 * n].rearrange(
                "p (b k n) -> p b k n", k=3, n=n)
            with st:
                @block.vector
                def _(dve):
                    dve.sem_inc(used, NG)
                    split_rows(dve, values, parts.rearrange("p b k n -> p k b n"), rest)
                    with dve.Fori(0, TURNS, 1) as i:
                        for j in range(NG):
                            dve.wait_ge(used, i * NG + j + 1)
                            dve.sem_inc(t_dve, 1)
                            dve.tensor_tensor(onehots[:, j], bc(iota_free[:, :], [P, GB, P], 1),
                                              bc(lo[key][:, ds(i * RING + j * GB, GB)], [P, GB, P], 2), ALU.is_equal)
                            dve.tensor_copy(staged[:, j * GB:(j + 1) * GB], parts[:, ds(i * RING + j * GB, GB)])
                            dve.drain().then_inc(ready, 1)
                    dve.wait_ge(used, NG * TURNS + NG + 1)
                    dve.tensor_copy(acc, sums[:, :, 0])
                    for k in (1, 2):
                        dve.drain()
                        dve.tensor_tensor(acc, acc, sums[:, :, k], ALU.add)

                @block.tensor
                def _(pe):
                    pe.matmul(ps[:, 7, :], zeros[:, 0:P], zeros[:, :], start=True, stop=False)
                    with pe.Fori(0, TURNS, 1) as i:
                        t = block_tiles(pe, key, i)
                        for j in range(NG):
                            pe.wait_ge(ready, i * NG + j + 1)
                            pe.sem_inc(t_pe, 1)
                            for u in range(GB):
                                mm = pe.matmul(sums[:, ds(t[j * GB + u], 1)], onehots[:, j, u, :],
                                               staged[:, j * GB + u],
                                               start=False, stop=False, skip_group_check=True)
                            mm.then_inc(used, 1)
                    pe.matmul(ps[:, 7, :], zeros[:, 0:P], zeros[:, :], start=False, stop=True).then_inc(used, 1)

        def wide_pass(key, n, table, index):
            st, block, (used, staged, ready, t_act, t_pool, t_dve, t_pe) = stage(
                "summed", "staged", "operands", "tick_act", "tick_pool", "tick_dve", "tick_pe")
            rows0 = before["gathered"]
            before["gathered"] += 16 * GB * TURNS
            acc = big_view(n)
            with st:
                @block.scalar
                def _(act):
                    gather_issue(act, index, used, staged, t_act)

                @block.gpsimd
                def _(pool):
                    gather_rows(pool, table, n, staged, gathered, t_pool)

                @block.vector
                def _(dve):
                    dve.sem_inc(used, NG)
                    dve.memset(acc, 0.0)
                    with dve.Fori(0, TURNS, 1) as i:
                        _, t = nc.values_load_multi_w_load_instructions(
                            tid[key][0:1, ds(i * RING, RING)], engines=(mybir.EngineType.DVE,), min_val=0,
                            max_val=T - 1, skip_runtime_bounds_check_because="bases() clamps the tiles to 0..T-1")
                        for j in range(-2, NG):
                            if j >= 0:
                                dve.wait_ge(used, i * NG + j + NG + 1)
                                dve.sem_inc(t_dve, 1)
                                for u in range(GB):
                                    at = acc[:, ds(t[j * GB + u], 1), :]
                                    dve.tensor_tensor(at, at, ps[:, j % 2 * 4 + u:j % 2 * 4 + u + 1, 0:n], ALU.add)
                                    dve.drain()
                            if j + 2 < NG:
                                dve.tensor_tensor(onehot2[:, j % 2], bc(iota_free[:, :], [P, GB, P], 1),
                                                  bc(lo[key][:, ds(i * RING + (j + 2) * GB, GB)], [P, GB, P], 2),
                                                  ALU.is_equal)
                                dve.drain().then_inc(ready, 1)

                @block.tensor
                def _(pe):
                    with pe.Fori(0, TURNS, 1) as i:
                        for j in range(NG):
                            pe.wait_ge(ready, i * NG + j + 1)
                            pe.sem_inc(t_pe, 1)
                            pe.wait_ge(gathered[j], i * (16 * GB) + (rows0 + 16 * GB))
                            pe.sem_inc(t_pe, 1)
                            for u in range(GB):
                                mm = pe.matmul(ps[:, j % 2 * 4 + u, 0:n], onehot2[:, j % 2, u, :], ring[:, j * GB + u, 0:n],
                                               start=True, stop=True)
                            mm.then_inc(used, 1)

        def dense(sources, n, dest, bias=None, add=False, scatters=0, further=None):
            width, n = n, n + (further.shape[2] if further is not None else 0)
            chunks = sum(k for _, k, _ in sources)
            wv = w_view(chunks, n)
            din = ringf[:, 0:DT * chunks * P].rearrange("p (t f) -> p t f", t=DT)
            first = 2 if n > 256 else 5
            step = 512 if n > 256 else 256
            ov = psf[:, first * 512:min(first * 512 + DT * step, 4096)].rearrange("p (t f) -> p t f", f=step)[:, :, 0:n]
            st, block, (staged, turned, turned_kept, done, taken, t_dve, t_pe, t_act, t_pool) = stage(
                "staged", "turned", "turned_kept", "done", "taken", "tick_dve", "tick_pe", "tick_act", "tick_pool")
            with st:
                if scatters:
                    scatter_by_source(block, t_pool, scatters)

                @block.vector
                def _(dve):
                    def stage_inputs(q):
                        c = 0
                        for view, k, scaled in sources:
                            for m in range(k):
                                o = din[:, :, (c + m) * P:(c + m + 1) * P]
                                i = view[:, ds(q * DT, DT), m * P:(m + 1) * P]
                                if scaled:
                                    dve.tensor_tensor(o, i, bc(deg[:, ds(q * DT, DT)], [P, DT, P], 2), ALU.mult)
                                else:
                                    dve.tensor_copy(o, i)
                            c += k
                        dve.drain().then_inc(staged, 1)

                    def take(q):
                        d = dest[:, ds(q * DT, DT), :]
                        if bias is not None:
                            dve.tensor_tensor(d, ov, bc(bias, [P, DT, n], 1), ALU.add)
                        elif add:
                            dve.tensor_tensor(d, d, ov, ALU.add)
                        else:
                            dve.tensor_copy(d, ov[:, :, 0:width])
                        if further is not None:
                            dve.tensor_copy(further[:, ds(q * DT, DT), :], ov[:, :, width:n])
                        dve.drain().then_inc(taken, 1)

                    stage_inputs(0)
                    with dve.Fori(0, T // DT - 1, 1) as q:
                        dve.wait_ge(turned, q * chunks + chunks)
                        dve.sem_inc(t_dve, 1)
                        stage_inputs(q + 1)
                        dve.wait_ge(done, q + 1)
                        dve.sem_inc(t_dve, 1)
                        take(q)
                    dve.wait_ge(done, T // DT)
                    take(T // DT - 1)

                @block.tensor
                def _(pe):
                    pe.sem_inc(taken, 1)
                    with pe.Fori(0, T // DT, 1) as q:
                        pe.wait_ge(staged, q + 1)
                        pe.sem_inc(t_pe, 1)
                        for c in range(chunks):
                            for k in range(DT):
                                mm = pe.transpose(psf[:, (c * DT + k) * P:(c * DT + k + 1) * P],
                                                  din[:, k, c * P:(c + 1) * P], ident[:, :])
                            mm.then_inc(turned, 1)
                        pe.wait_ge(turned_kept, q + 1)
                        pe.sem_inc(t_pe, 1)
                        pe.wait_ge(taken, q + 1)
                        pe.sem_inc(t_pe, 1)
                        for k in range(DT):
                            o = psf[:, first * 512 + k * step:first * 512 + k * step + n]
                            for c in range(chunks):
                                mm = pe.matmul(o, dxt3[:, c * DT + k, :], wv[:, c, :], start=c == 0, stop=c == chunks - 1)
                        mm.then_inc(done, 1)

                @block.scalar
                def _(act):
                    with act.Fori(0, T // DT, 1) as q:
                        act.wait_ge(turned, q * chunks + chunks)
                        act.sem_inc(t_act, 1)
                        act.activation(dxt[:, 0:chunks * DT * P], psf[:, 0:chunks * DT * P], ACT.Copy)
                        act.drain().then_inc(turned_kept, 1)

        def norm(Y, n, scratch, gamma=None, beta=None, before=None, scatters=0):
            st, block, (centered, squared, var_ready, std_ready, scaled, t_pool) = stage(
                "centered", "squared", "var_ready", "std_ready", "scaled", "tick_pool")
            mean, var = sm[:, 0:T], sm[:, 32:32 + T]
            part = [P, DT, n]
            parts = [slice(t, t + DT) for t in range(0, T, DT)]
            with st:
                if scatters:
                    scatter_by_source(block, t_pool, scatters)

                @block.vector
                def _(dve):
                    if before:
                        before(dve)
                        dve.drain()
                    for q in parts:
                        dve.tensor_reduce(mean[:, q], Y[:, q, :], AX, ALU.add)
                        dve.drain()
                        dve.tensor_scalar(mean[:, q], mean[:, q], 1.0 / n, None, ALU.mult)
                        dve.drain()
                        dve.tensor_tensor(Y[:, q, :], Y[:, q, :], bc(mean[:, q], part, 2), ALU.subtract)
                        dve.drain().then_inc(centered, 1)
                    for k, q in enumerate(parts):
                        dve.wait_ge(squared, k + 1)
                        dve.tensor_reduce(var[:, q], scratch[:, q, :], AX, ALU.add)
                    dve.drain()
                    dve.tensor_scalar(var, var, 1.0 / n, EPS, ALU.mult, ALU.add)
                    dve.drain().then_inc(var_ready, 1)
                    dve.wait_ge(std_ready, 1)
                    dve.reciprocal(var, var)
                    dve.drain()
                    for q in parts:
                        dve.tensor_tensor(Y[:, q, :], Y[:, q, :], bc(var[:, q], part, 2), ALU.mult)
                        if gamma is not None:
                            dve.drain()
                            dve.tensor_tensor(Y[:, q, :], Y[:, q, :], bc(gamma, part, 1), ALU.mult)
                            dve.drain()
                            dve.tensor_tensor(Y[:, q, :], Y[:, q, :], bc(beta, part, 1), ALU.add)
                            dve.drain().then_inc(scaled, 1)

                @block.scalar
                def _(act):
                    for k, q in enumerate(parts):
                        act.wait_ge(centered, k + 1)
                        act.activation(scratch[:, q, :], Y[:, q, :], ACT.Square)
                        act.drain().then_inc(squared, 1)
                    act.wait_ge(var_ready, 1)
                    act.activation(var, var, ACT.Sqrt)
                    act.drain().then_inc(std_ready, 1)
                    if gamma is not None:
                        for k, q in enumerate(parts):
                            act.wait_ge(scaled, k + 1)
                            act.activation(Y[:, q, :], Y[:, q, :], ACT.Relu)

        def dve_stage(body, ahead=None):
            st, block, _ = stage()
            with st:
                if ahead:
                    gather_ahead(block, *ahead)

                @block.vector
                def _(dve):
                    body(dve)

        def segment_totals(op, K, rels, values, total=None, ends=None, scatters=0, ahead=None):
            st, block, (turned, tails, tails_up, carry, carry_up, done, back, taken, t_pool) = stage(
                "turned", "tails", "tails_turned", "carry", "carry_turned", "results", "back", "taken", "tick_pool")
            big3 = bigf[0:SP_, 0:5 * K * SL].rearrange("p (a k s) -> p a k s", a=5, k=K)
            V, RF, RB, TS, U = (big3[:, a] for a in range(5))
            mask = rhsf[0:SP_, 0:SL]
            maskb = rhsf[0:SP_, SL:2 * SL]
            oh = onehot2[0:SP_, :, :, :].rearrange("p z a b -> p (z a b)")
            near = [oh[:, 0:SL], oh[:, SL:2 * SL]]
            gates = dxt[0:SP_, 0:2 * SL].rearrange("p (z s) -> p z s", z=2)
            tail = sm[0:SP_, 8:8 + 4 * K].rearrange("p (z k) -> p z k", z=4)
            rows = sm[0:K, 32:32 + 4 * SP_].rearrange("p (z s) -> p z s", z=4)
            crow = dxt[0:K, 2 * SL:2 * SL + 2 * (SP_ + 1)].rearrange("p (z s) -> p z s", z=2)
            init = sm[0:SP_, 500:500 + 2 * K].rearrange("p (z k) -> p z k", z=2)
            isum = op == ALU.add
            o0, o1, start = (ALU.mult, ALU.add, 0.0) if isum else (ALU.add, ALU.max, -BIG)
            whole = [SP_, K, SL]
            with st:
                if ahead:
                    gather_ahead(block, *ahead)
                if scatters:
                    scatter_by_source(block, t_pool, scatters)

                @block.tensor
                def _(pe):
                    for h in range(K):
                        for c in range(4):
                            mm = pe.transpose(ps[0:SP_, h, c * P:(c + 1) * P],
                                              values[:, :, h].rearrange("p (q c) -> p c q", c=4)[:, c, :], ident[:, :])
                    mm.then_inc(turned, 1)

                    def give_back(src, given):
                        for k in range(given, given + K):
                            if k > 1:
                                pe.wait_ge(taken, k - 1)
                            for c in range(4):
                                mm = pe.transpose(ps[:, 6 + k % 2, c * SP_:(c + 1) * SP_],
                                                  src[:, k - given, c * P:(c + 1) * P], ident[0:SP_, 0:SP_])
                            mm.then_inc(back, 1)

                    for r in range(rels):
                        pe.wait_ge(tails, r + 1)
                        for z in range(4):
                            mm = pe.transpose(ps[0:K, 4, z * SP_:(z + 1) * SP_], tail[:, z, :], ident[0:SP_, 0:SP_])
                        mm.then_inc(tails_up, 1)
                        pe.wait_ge(carry, r + 1)
                        pe.transpose(ps[0:SP_, 5, 0:K], crow[:, 0, 0:SP_], ident[0:K, 0:K])
                        pe.transpose(ps[0:SP_, 5, K:2 * K], crow[:, 1, 1:SP_ + 1], ident[0:K, 0:K]).then_inc(carry_up, 1)
                        if ends is not None:
                            pe.wait_ge(done, r + 1)
                            give_back(U, r * K)
                    if total is not None:
                        pe.wait_ge(done, rels + 1)
                        give_back(TS, rels * K if ends is not None else 0)

                @block.vector
                def _(dve):
                    if isum:
                        dve.tensor_scalar(gates[:, 0, :], cont[:, :], 0.0, None, ALU.is_equal)
                        dve.tensor_scalar(gates[:, 1, :], isend[:, :], 0.0, None, ALU.is_equal)
                    else:
                        dve.tensor_copy(gates[:, 0, :], cont[:, :])
                        dve.tensor_scalar(gates[:, 1, :], isend[:, :], -BIG, None, ALU.mult)
                    dve.drain()
                    dve.tensor_tensor_scan(near[0], gates[:, 0, :], gates[:, 0, :], BIG, ALU.min, ALU.min)
                    dve.tensor_tensor_scan(near[1][:, ::-1], gates[:, 1, ::-1], gates[:, 1, ::-1], BIG, ALU.min, ALU.min)
                    dve.drain()
                    for z, g in ((1, near[0][:, SL - 1:SL]), (3, near[1][:, 0:1])):
                        dve.tensor_copy(tail[:, z, :], g.to_broadcast([SP_, K]) if K > 1 else g)
                    dve.wait_ge(turned, 1)
                    if rels > 1 and total is not None:
                        dve.memset(TS, 0.0)
                    for r in range(rels):
                        if rels > 1:
                            dve.drain()
                            dve.tensor_scalar(mask, typ_s[:, :], float(r), None, ALU.is_equal)
                            dve.drain()
                            dve.tensor_tensor(V, ps[0:SP_, 0:K, :], bc(mask, whole, 1), ALU.mult)
                            if not isum:
                                dve.tensor_scalar(maskb, mask, 1.0, BIG, ALU.subtract, ALU.mult)
                                dve.drain()
                                dve.tensor_tensor(V, V, bc(maskb, whole, 1), ALU.add)
                        else:
                            dve.tensor_copy(V, ps[0:SP_, 0:K, :])
                        dve.drain()
                        for k in range(K):
                            dve.tensor_tensor_scan(RF[:, k, :], gates[:, 0, :], V[:, k, :], start, o0, o1)
                            dve.tensor_tensor_scan(RB[:, k, ::-1], gates[:, 1, ::-1], V[:, k, ::-1], start, o0, o1)
                        dve.drain()
                        dve.tensor_copy(tail[:, 0, :].unsqueeze(2), RF[:, :, SL - 1:SL])
                        dve.tensor_copy(tail[:, 2, :].unsqueeze(2), RB[:, :, 0:1])
                        dve.drain().then_inc(tails, 1)
                        dve.tensor_tensor(RF, RF, RB, o1)
                        dve.drain()
                        if isum:
                            dve.tensor_tensor(RF, RF, V, ALU.subtract)
                        dve.wait_ge(tails_up, r + 1)
                        dve.tensor_copy(rows, ps[0:K, 4, 0:4 * SP_].rearrange("p (z s) -> p z s", z=4))
                        dve.memset(crow[:, 0, 0:1], start)
                        dve.memset(crow[:, 1, SP_:SP_ + 1], start)
                        dve.drain()
                        dve.tensor_tensor_scan(crow[:, 0, 1:SP_ + 1], rows[:, 1, :], rows[:, 0, :], start, o0, o1)
                        dve.tensor_tensor_scan(crow[:, 1, 0:SP_][:, ::-1], rows[:, 3, ::-1], rows[:, 2, ::-1], start, o0, o1)
                        dve.drain().then_inc(carry, 1)
                        dve.wait_ge(carry_up, r + 1)
                        dve.tensor_copy(init, ps[0:SP_, 5, 0:2 * K].rearrange("p (z k) -> p z k", z=2))
                        for z in range(2):
                            dve.drain()
                            for k in range(K):
                                dve.scalar_tensor_tensor(RF[:, k, :], near[z], init[:, z, k:k + 1], RF[:, k, :], o0, o1)
                        dve.drain()
                        if ends is not None and r:
                            dve.wait_ge(back, r * K)
                        if total is not None:
                            if rels > 1:
                                dve.tensor_tensor(U, RF, bc(mask, whole, 1), ALU.mult)
                                dve.drain()
                                dve.tensor_tensor(TS, TS, U, ALU.add)
                                dve.drain()
                            else:
                                dve.tensor_copy(TS, RF)
                        if ends is not None:
                            dve.tensor_tensor(U, RF, bc(isend[:, :], whole, 1), ALU.mult)
                            dve.drain().then_inc(done, 1)
                    if total is not None:
                        k = rels + 1 - (rels if ends is not None else 0)
                        dve.drain().then_inc(done, k)

                @block.scalar
                def _(act):
                    results = [ends[:, :, r * K:(r + 1) * K] for r in range(rels)] if ends is not None else []
                    results += [total] if total is not None else []
                    for k in range(len(results) * K):
                        act.wait_ge(back, k + 1)
                        act.activation(results[k // K][:, :, k % K].rearrange("p (q c) -> p c q", c=4),
                                       ps[:, 6 + k % 2, 0:NB].rearrange("p (c q) -> p c q", c=4), ACT.Copy)
                        act.drain().then_inc(taken, 1)

        def term_columns(w, n, vectors):
            scratch, heads = bigf[:, 0:n], n // HD

            def body(dve):
                for v, att in enumerate(vectors):
                    dve.drain()
                    dve.tensor_tensor(scratch, w[:, 0:n], att, ALU.mult)
                    dve.drain()
                    dve.tensor_reduce(w[:, n + v * heads:n + (v + 1) * heads],
                                      scratch.rearrange("p (g c) -> p g c", c=HD), AX, ALU.add)
            return body

        constants()
        store_load([],
                   [(w_view(2, HID)[:, 0, :], A["L0_gnn_W_l0"]), (w_view(2, HID)[:, 1, :], A["L0_gnn_W_r0"]),
                    (biases[:, 0:HID], rowb(A["L0_gnn_b_l0"], HID)), (biases[:, HID:2 * HID], rowb(A["L0_gnn_g0"], HID)),
                    (biases[:, 2 * HID:3 * HID], rowb(A["L0_gnn_be0"], HID)),
                    (biases[:, 3 * HID:4 * HID], rowb(A["L0_gnn_b_l1"], HID)),
                    (biases[:, 4 * HID:5 * HID], rowb(A["L0_gnn_g1"], HID)),
                    (biases[:, 5 * HID:6 * HID], rowb(A["L0_gnn_be1"], HID))])
        split_keys()
        histograms()
        bases("D")
        bases("S")
        place()
        load_list("D")

        def degrees(dve):
            dve.tensor_scalar(no_edge[:, :], deg[:, :], 0.0, None, ALU.is_equal)
            dve.drain()
            dve.tensor_scalar(deg[:, :], deg[:, :], 1.0, None, ALU.max)
            dve.drain()
            dve.reciprocal(deg[:, :], deg[:, :])
        dve_stage(degrees)

        edge_pass("D", A["x"], idx["Dsrc"][:, :])
        dense([(big_view(F), 1, True), (X[:, :, :], 1, False)], HID, hid, bias=biases[:, 0:HID], scatters=3)
        norm(hid, HID, big_view(HID), biases[:, HID:2 * HID], biases[:, 2 * HID:3 * HID], scatters=2)
        kn = "(k p) n -> p k n"
        store_load([(tiles(hidden1_table), hid)],
                   [(w_view(4, HID)[:, 0:2, :], A["L0_gnn_W_l1"].rearrange(kn, p=P)),
                    (w_view(4, HID)[:, 2:4, :], A["L0_gnn_W_r1"].rearrange(kn, p=P))])
        wide_pass("D", HID, hidden1_table, idx["Dsrc"][:, :])
        dense([(big_view(HID), 2, True), (hid, 2, False)], HID, hid, bias=biases[:, 3 * HID:4 * HID], scatters=4)
        norm(hid, HID, big_view(HID), biases[:, 4 * HID:5 * HID], biases[:, 5 * HID:6 * HID], scatters=2)
        store_load([], [(w_view(2, F), A["L0_gnn_W_l2"].rearrange(kn, p=P))])
        dense([(hid, 2, False)], F, big_view(F), scatters=1)
        store_load([(tiles(proj2_table), big_view(F))],
                   [(w_view(2, F), A["L0_gnn_W_r2"].rearrange(kn, p=P)),
                    (biases[:, 0:F], rowb(A["L0_gnn_b_l2"], F))])
        edge_pass("D", proj2_table, idx["Dsrc"][:, :])
        full = [P, T, F]

        def sage2(dve):
            acc = big_view(F)
            dve.tensor_tensor(acc, acc, bc(deg[:, :], full, 2), ALU.mult)
            dve.drain()
            dve.tensor_tensor(acc, acc, bc(biases[:, 0:F], full, 1), ALU.add)
            dve.drain()
            dve.tensor_tensor(X[:, :, :], X[:, :, :], acc, ALU.add)
        dve_stage(sage2)
        dense([(hid, 2, False)], F, X[:, :, :], add=True, scatters=1)
        norm(X[:, :, :], F, big_view(F), scatters=1)

        att_src, att_dst = biases[:, 0:384], biases[:, 384:768]
        rel_bias, rel_w = biases[:, 768:1152], biases[:, 1152:1155]
        rhc = "(o r) h c -> o (r h c)"
        rel_weights = w_view(1, 384 + SIDE)[:, 0, :]
        store_load([], [(rel_weights[:, 0:384].rearrange("p (r n) -> p r n", r=NREL), A["L1_gnn_W"].rearrange("r p n -> p r n")),
                        (att_src, A["L1_gnn_att_src"].rearrange(rhc, o=1).to_broadcast([P, 384])),
                        (att_dst, A["L1_gnn_att_dst"].rearrange(rhc, o=1).to_broadcast([P, 384])),
                        (rel_bias, A["L1_gnn_bias"].rearrange("(o r) c -> o (r c)", o=1).to_broadcast([P, 384])),
                        (rel_w, rowb(A["L1_gnn_rel_w"], NREL))])
        relh = big_view(384)
        dve_stage(term_columns(rel_weights, 384, [att_src, att_dst]))
        dense([(X[:, :, :], 1, False)], 384, relh, scatters=2, further=node_a[:, :, 0:SIDE])
        own24 = weights[:, 384 + SIDE:384 + SIDE + T * SIDE].rearrange("p (t k) -> p t k", t=T)

        def rel_terms(dve):
            dve.tensor_copy(late_pos, pos_src[:, IB - 2 * SB * LATE:IB])
            dve.tensor_copy(late_rec, rec_all[:, IB - 2 * SB * LATE:IB, :])
            for r in range(NREL):
                dve.tensor_copy(own24[:, :, r:12:NREL], node_a[:, :, 12 + 4 * r:16 + 4 * r])
                dve.tensor_copy(own24[:, :, 12 + r:24:NREL], node_a[:, :, 4 * r:4 * r + 4])
            dve.tensor_reduce(sm[:, 0:1], rel_w, AX, ALU.max)
            dve.drain()
            dve.tensor_scalar(rel_w, rel_w, sm[:, 0:1], None, ALU.subtract)

        def exp_stage(before, pairs):
            st, block, (arg,) = stage("argument")
            with st:
                @block.vector
                def _(dve):
                    before(dve)
                    dve.drain().then_inc(arg, 1)

                @block.scalar
                def _(act):
                    act.wait_ge(arg, 1)
                    for o, i, f in pairs:
                        act.activation(o, i, f)
        exp_stage(rel_terms, [(rel_w, rel_w, ACT.Exp)])
        rows = [slice(r * NP, (r + 1) * NP) for r in range(NREL)]
        store_load([(tiles(rel_h_table[rows[r], :]), relh[:, :, r * F:(r + 1) * F]) for r in range(NREL)]
                   + [(tiles(rel_src_table[rows[r], :]), node_a[:, :, 4 * r:4 * r + 4]) for r in range(NREL)], [])
        ends_sum = hidf[:, 0:NB * 12].rearrange("p (b k) -> p b k", k=12)
        e_src, e_dst, e_own, e_max = ebuf[:, :, 0:4], ebuf[:, :, 4:8], ebuf[:, :, 8:12], ends_sum[:, :, 0:4]
        node_fetch("D", own24, ebuf[:, :, 4:12], other_dest=e_src, table=rel_src_table, index=idx["DsrcT"][:, :])
        segment_totals(ALU.max, HEADS, NREL, e_src, total=e_max, ends=em, scatters=6)

        def leaky(dve, a, slope):
            dve.scalar_tensor_tensor(a, a, slope, a, ALU.mult, ALU.max)

        def rel_args(dve):
            dve.tensor_tensor(e_max, e_max, e_own, ALU.max)
            dve.tensor_tensor(e_src, e_src, e_dst, ALU.add)
            dve.drain()
            dve.tensor_tensor(e_max, e_max, e_dst, ALU.add)
            dve.tensor_tensor(e_own, e_own, e_dst, ALU.add)
            dve.drain()
            for a in (e_src, e_own, e_max):
                leaky(dve, a, 0.2)
            dve.drain()
            dve.tensor_tensor(e_src, e_src, e_max, ALU.subtract)
            dve.tensor_tensor(e_own, e_own, e_max, ALU.subtract)
            dve.tensor_reduce(sm[:, 0:1], rel_w, AX, ALU.add)
            dve.drain()
            dve.reciprocal(sm[:, 0:1], sm[:, 0:1])
            dve.drain()
            dve.tensor_scalar(rel_w, rel_w, sm[:, 0:1], None, ALU.mult)
        exp_stage(rel_args, [(e_src, e_src, ACT.Exp), (e_own, e_own, ACT.Exp)])
        segment_totals(ALU.add, HEADS, NREL, e_src, total=e_dst, ends=ends_sum, scatters=4)

        def rel_alphas(dve):
            share, one = bigf[:, 0:NB], bigf[:, NB:2 * NB]
            dve.tensor_tensor(e_dst, e_dst, e_own, ALU.add)
            dve.memset(share, 0.0)
            dve.drain()
            dve.reciprocal(e_dst, e_dst)
            for r in range(NREL):
                dve.drain()
                dve.tensor_scalar(one, typ[:, :], float(r), None, ALU.is_equal)
                dve.drain()
                dve.scalar_tensor_tensor(share, one, rel_w[:, r:r + 1], share, ALU.mult, ALU.add)
            dve.tensor_tensor(e_src, e_src, e_dst, ALU.mult)
            dve.drain()
            dve.tensor_tensor(e_src, e_src, bc(share, [P, NB, HEADS], 2), ALU.mult)
        dve_stage(rel_alphas, ahead=(rel_h_table, idx["DsrcT"][:, :]))
        edge_pass("D", rel_h_table, idx["DsrcT"][:, :], ahead=True, payload=e_src, heads=HEADS, sides=(em, ends_sum))

        acc = big_view(F + SIDE)
        own_w, own_m = node_a[:, :, 0:12], node_a[:, :, 24:36]
        node_max, node_sum = acc[:, :, F:F + 12], acc[:, :, F + 12:F + 24]

        def own_args(dve):
            lone = sm[:, 64:64 + T]
            dve.tensor_scalar(lone, no_edge[:, :], -BIG, None, ALU.mult)
            dve.drain()
            dve.tensor_tensor(own_m, node_max, bc(lone, [P, T, 12], 2), ALU.add)
            dve.drain()
            dve.tensor_tensor(own_m, own_m, own_w, ALU.max)
            dve.drain()
            dve.tensor_tensor(own_m, own_m, node_a[:, :, 12:24], ALU.add)
            dve.tensor_tensor(own_w, own_w, node_a[:, :, 12:24], ALU.add)
            dve.drain()
            leaky(dve, own_m, 0.2)
            leaky(dve, own_w, 0.2)
            dve.drain()
            dve.tensor_tensor(own_w, own_w, own_m, ALU.subtract)
        exp_stage(own_args, [(own_w, own_w, ACT.Exp)])

        def own_alphas(dve):
            dve.tensor_tensor(node_sum, node_sum, own_w, ALU.add)
            dve.drain()
            dve.reciprocal(node_sum, node_sum)
            dve.tensor_tensor(X[:, :, :], X[:, :, :], acc[:, :, 0:F], ALU.add)
            dve.drain()
            dve.tensor_tensor(own_w, own_w, node_sum, ALU.mult)
            for r in range(NREL):
                dve.drain()
                dve.tensor_scalar(own_w[:, :, 4 * r:4 * r + 4], own_w[:, :, 4 * r:4 * r + 4], rel_w[:, r:r + 1], None, ALU.mult)
                dve.tensor_scalar(rel_bias[:, r * F:(r + 1) * F], rel_bias[:, r * F:(r + 1) * F], rel_w[:, r:r + 1], None,
                                  ALU.mult)
        dve_stage(own_alphas)
        full = [P, T, F]
        own_rows = [hidf[:, 0:T * F].rearrange("p (t f) -> p t f", t=T), hidf[:, T * F:2 * T * F].rearrange("p (t f) -> p t f", t=T),
                    bigf[:, 0:T * F].rearrange("p (t f) -> p t f", t=T)]
        store_load([], [(own_rows[r], tiles(rel_h_table[rows[r], :])) for r in range(NREL)])

        def own_sums(dve):
            for r in range(NREL):
                for t in range(0, T, DT):
                    h = own_rows[r][:, t:t + DT, :].rearrange("p t (h c) -> p t h c", c=HD)
                    dve.tensor_tensor(h, h, bc(own_w[:, t:t + DT, 4 * r:4 * r + 4], [P, DT, HEADS, HD], 3), ALU.mult)
            dve.tensor_tensor(rel_bias[:, 0:F], rel_bias[:, 0:F], rel_bias[:, F:2 * F], ALU.add)
            dve.drain()
            dve.tensor_tensor(rel_bias[:, 0:F], rel_bias[:, 0:F], rel_bias[:, 2 * F:3 * F], ALU.add)
            dve.drain()
            dve.tensor_tensor(X[:, :, :], X[:, :, :], bc(rel_bias[:, 0:F], full, 1), ALU.add)
            for r in range(NREL):
                dve.drain()
                dve.tensor_tensor(X[:, :, :], X[:, :, :], own_rows[r], ALU.add)
        dve_stage(own_sums)
        norm(X[:, :, :], F, big_view(F))

        load_list("S")
        w2 = w_view(1, F + 2)[:, 0, :]
        store_load([], [(w2[:, 0:F], A["L2_gnn_W"]),
                        (w2[:, F:F + 1], A["L2_gnn_a_j"].rearrange("(p o) -> p o", o=1)),
                        (w2[:, F + 1:F + 2], A["L2_gnn_a_i"].rearrange("(p o) -> p o", o=1))])
        dense([(X[:, :, :], 1, False)], F, H1, further=node_a[:, :, 0:2])
        sj, si, sm_ = node_a[:, :, 0:1], node_a[:, :, 1:2], node_a[:, :, 2:3]

        def l2_rows(dve):
            dve.tensor_tensor(H1, H1, X[:, :, :], ALU.add)
        dve_stage(l2_rows)
        c0, c4, c8 = ebuf[:, :, 0:1], ebuf[:, :, 4:5], ebuf[:, :, 8:9]
        node_fetch("D", si, c4, other=sj, other_dest=c0)
        segment_totals(ALU.max, 1, 1, c0, total=c8, ends=em[:, :, 0:1])

        def weight_args(a, d, m, slope):
            def body(dve):
                dve.tensor_tensor(a, a, d, ALU.add)
                dve.tensor_tensor(m, m, d, ALU.add)
                dve.drain()
                leaky(dve, a, slope)
                leaky(dve, m, slope)
                dve.drain()
                dve.tensor_tensor(a, a, m, ALU.subtract)
            return body
        exp_stage(weight_args(c0, c4, c8, 0.01), [(c0, c0, ACT.Exp)])
        segment_totals(ALU.add, 1, 1, c0, ends=em[:, :, 1:2])
        side_pass("D", em[:, :, 0:2])

        def l2_messages(dve):
            sums, den = big_view(2), sm[:, 0:T]
            dve.tensor_tensor(sm_, sums[:, :, 0:1], si, ALU.add)
            dve.tensor_tensor(den, sums[:, :, 1], no_edge[:, :], ALU.add)
            dve.drain()
            leaky(dve, sm_, 0.01)
            dve.reciprocal(den, den)
            dve.drain()
            dve.tensor_tensor(H1, H1, bc(den, full, 2), ALU.mult)
        dve_stage(l2_messages)
        store_load([(tiles(row_table[0]), H1)], [])
        node_fetch("S", sj, c0, other=node_a[:, :, 1:3], other_dest=ebuf[:, :, 4:6],
                   ahead=(row_table[0], idx["Sdst"][:, :]))

        def l2_args(dve):
            dve.tensor_tensor(c0, c0, c4, ALU.add)
            dve.drain()
            leaky(dve, c0, 0.01)
            dve.drain()
            dve.tensor_tensor(c0, c0, ebuf[:, :, 5:6], ALU.subtract)
        exp_stage(l2_args, [(c0, c0, ACT.Exp)])
        edge_pass("S", row_table[0], idx["Sdst"][:, :], ahead=True, payload=c0, heads=1)
        exp_stage(lambda dve: None, [(big_view(F), big_view(F), ACT.Gelu)])

        def add_acc(dve):
            dve.tensor_tensor(X[:, :, :], X[:, :, :], big_view(F), ALU.add)
        norm(X[:, :, :], F, big_view(F), before=add_acc)

        def keep_x(dve):
            dve.tensor_copy(XR, X[:, :, :])
        dve_stage(keep_x)
        for l in range(2):
            w3 = w_view(1, F + 2 * HEADS)[:, 0, :]
            store_load([], [(w3[:, 0:F], A["L3_gnn_W"][l]),
                            (biases[:, 0:F], A["L3_gnn_a_src"][l:l + 1].rearrange("o h c -> o (h c)").to_broadcast([P, F])),
                            (biases[:, F:2 * F], A["L3_gnn_a_dst"][l:l + 1].rearrange("o h c -> o (h c)").to_broadcast([P, F])),
                            (biases[:, 2 * F:3 * F], A["L3_gnn_b"][l:l + 1, :].to_broadcast([P, F]))])
            dve_stage(term_columns(w3, F, [biases[:, 0:F], biases[:, F:2 * F]]))
            dense([(X[:, :, :], 1, False)], F, H1, further=node_a[:, :, 0:2 * HEADS])
            store_load([(tiles(row_table[1 + l]), H1)], [])
            node_fetch("D", node_a[:, :, 4:8], ebuf[:, :, 4:8], other=node_a[:, :, 0:4], other_dest=ebuf[:, :, 0:4])
            segment_totals(ALU.max, HEADS, 1, ebuf[:, :, 0:4], total=ebuf[:, :, 8:12],
                           ahead=(row_table[1 + l], idx["Dsrc"][:, :]))
            exp_stage(weight_args(ebuf[:, :, 0:4], ebuf[:, :, 4:8], ebuf[:, :, 8:12], 0.2),
                      [(ebuf[:, :, 0:4], ebuf[:, :, 0:4], ACT.Exp)])
            edge_pass("D", row_table[1 + l], idx["Dsrc"][:, :], ahead=True, payload=ebuf[:, :, 0:4], heads=HEADS,
                      sides=(ebuf[:, :, 0:4],))
            acc = big_view(F + 4)

            def gat_node(dve):
                dve.tensor_scalar(acc[:, :, F:F + 4], acc[:, :, F:F + 4], 1e-16, None, ALU.add)
                dve.tensor_tensor(X[:, :, :], X[:, :, :], bc(biases[:, 2 * F:3 * F], full, 1), ALU.add)
                dve.drain()
                dve.reciprocal(acc[:, :, F:F + 4], acc[:, :, F:F + 4])
                dve.drain()
                for t in range(0, T, DT):
                    a = acc[:, t:t + DT, 0:F].rearrange("p t (h c) -> p t h c", c=HD)
                    dve.tensor_tensor(a, a, bc(acc[:, t:t + DT, F:F + 4], [P, DT, HEADS, HD], 3), ALU.mult)
                dve.drain()
                dve.tensor_tensor(X[:, :, :], X[:, :, :], acc[:, :, 0:F], ALU.add)
                if l == 0:
                    dve.drain()
                    dve.tensor_scalar(H1, X[:, :, :], 0.0, None, ALU.min)

            def elu_sum(dve):
                dve.tensor_scalar(X[:, :, :], X[:, :, :], 0.0, -1.0, ALU.max, ALU.add)
                dve.drain()
                dve.tensor_tensor(X[:, :, :], X[:, :, :], H1, ALU.add)
            if l == 0:
                exp_stage(gat_node, [(H1, H1, ACT.Exp)])
                dve_stage(elu_sum)
            else:
                dve_stage(gat_node)

        def add_back(dve):
            dve.tensor_tensor(X[:, :, :], X[:, :, :], XR, ALU.add)
        norm(X[:, :, :], F, big_view(F), before=add_back)
        store_load([(out[0:(T - 1) * P, :].rearrange("(t p) f -> p t f", p=P), X[:, 0:T - 1, :]),
                    (out[(T - 1) * P:N, :], X[0:TAIL, T - 1, :])], [])


_IN = ["x", "src", "dst", "edge_type_3", "L0_gnn_W_l0", "L0_gnn_b_l0", "L0_gnn_W_r0", "L0_gnn_g0", "L0_gnn_be0",
       "L0_gnn_W_l1", "L0_gnn_b_l1", "L0_gnn_W_r1", "L0_gnn_g1", "L0_gnn_be1", "L0_gnn_W_l2", "L0_gnn_b_l2",
       "L0_gnn_W_r2", "L1_gnn_W", "L1_gnn_att_src", "L1_gnn_att_dst", "L1_gnn_bias", "L1_gnn_rel_w", "L2_gnn_a_i",
       "L2_gnn_a_j", "L2_gnn_W", "L3_gnn_W", "L3_gnn_a_src", "L3_gnn_a_dst", "L3_gnn_b"]


def kernel(**inputs):
    import numpy as np
    import concourse.bacc as bacc
    from concourse.bass_utils import run_bass_kernel_spmd as run
    nc = bacc.Bacc("TRN2", target_bir_lowering=False, num_devices=1)
    arrays, aps = {}, {}
    for name in _IN:
        a = np.ascontiguousarray(inputs[name])
        arrays["in_" + name] = a
        aps[name] = nc.dram_tensor("in_" + name, a.shape, mybir.dt.from_np(a.dtype), kind="ExternalInput").ap()
    o = nc.dram_tensor("out", (N, F), mybir.dt.float32, kind="ExternalOutput").ap()
    build(nc, aps, o)
    r = run(nc, [arrays], core_ids=[0])
    return r.results[0]["out"]
```
